# Optimizing a Trainium2 kernel written in Bass

```python
import numpy as np
import jax
import jax.numpy as jnp

def _softmax(x, axis=-1):
    return jax.nn.softmax(x, axis=axis)

def _gelu(x):
    return jax.nn.gelu(x, approximate=True)

def _silu(x):
    return jax.nn.silu(x)

def _sigmoid(x):
    return jax.nn.sigmoid(x)

def _layernorm(x, axis=-1, eps=1e-05):
    m = jnp.mean(x, axis=axis, keepdims=True)
    v = jnp.var(x, axis=axis, keepdims=True)
    return (x - m) / jnp.sqrt(v + eps)

def _scatter_add(tgt, idx, src, axis=0):
    return tgt.at[idx].add(src)

def _segment_sum(src, seg, n):
    return jax.ops.segment_sum(src, seg, n)
kernel_name = 'mk_recurrent_d4_jaxref_r4_d63aa6'

def setup_inputs(seed: int=0):
    np.random.seed(seed)
    _w = jnp.asarray

    def _L0_attn_setup():
        import jax, jax.numpy as jnp
        import numpy as np
        DIM = 256
        key = jax.random.key(seed)
        kx, kw = jax.random.split(key)
        x = jax.random.normal(kx, (4, 512, DIM), dtype=jnp.float32)
        W_qkv = jax.random.normal(kw, (3 * DIM, DIM), dtype=jnp.float32) * DIM ** (-0.5)
        return {'x': x, 'W_qkv': W_qkv}
    _L0_attn_in = _L0_attn_setup()

    def _L0_ffn_setup():
        import jax, jax.numpy as jnp
        import numpy as np
        DIM = 256
        HIDDEN = 768
        SCALE = 1.0 / 127.0

        def _dequant(w_int, dtype):
            return w_int.astype(dtype) * jnp.asarray(SCALE, dtype)
        key = jax.random.key(seed)
        k_x, k_g, k_u, k_d = jax.random.split(key, 4)
        x = jax.random.normal(k_x, (4, 512, DIM), dtype=jnp.float32)
        w_gate = jax.random.randint(k_g, (HIDDEN, DIM), -127, 128, dtype=jnp.int32)
        w_up = jax.random.randint(k_u, (HIDDEN, DIM), -127, 128, dtype=jnp.int32)
        w_down = jax.random.randint(k_d, (DIM, HIDDEN), -127, 128, dtype=jnp.int32)
        return {'x': x, 'w_gate': w_gate, 'w_up': w_up, 'w_down': w_down}
    _L0_ffn_in = _L0_ffn_setup()

    def _L1_attn_setup():
        import jax, jax.numpy as jnp
        import numpy as np
        N_HEADS = 16
        ROPE_BASE = 10000.0

        def _rope_tables(seq_len, d_head, dtype):
            inv_freq = 1.0 / ROPE_BASE ** (jnp.arange(0, d_head, 2, dtype=jnp.float32) / d_head)
            t = jnp.arange(seq_len, dtype=jnp.float32)
            freqs = t[:, None] * inv_freq[None, :]
            return (jnp.cos(freqs).astype(dtype), jnp.sin(freqs).astype(dtype))

        def _apply_rope(x, cos, sin):
            half = x.shape[-1] // 2
            x1, x2 = (x[..., :half], x[..., half:])
            return jnp.concatenate([x1 * cos - x2 * sin, x2 * cos + x1 * sin], axis=-1)
        key = jax.random.key(seed)
        k1, k2, k3 = jax.random.split(key, 3)
        d_model = 256
        x = jax.random.normal(k1, (2, 512, d_model), dtype=jnp.float32)
        w_qkv = jax.random.normal(k2, (d_model, 3 * d_model), dtype=jnp.float32) * d_model ** (-0.5)
        w_out = jax.random.normal(k3, (d_model, d_model), dtype=jnp.float32) * d_model ** (-0.5)
        return {'x': x, 'w_qkv': w_qkv, 'w_out': w_out}
    _L1_attn_in = _L1_attn_setup()

    def _L1_ffn_setup():
        import jax, jax.numpy as jnp
        import numpy as np
        LN_EPS = 1e-05
        NORM_EPS = 1e-12

        def _layernorm(x, gamma, beta):
            mu = x.mean(axis=-1, keepdims=True)
            var = ((x - mu) ** 2).mean(axis=-1, keepdims=True)
            return (x - mu) * jax.lax.rsqrt(var + LN_EPS) * gamma + beta

        def _l2norm(x, axis):
            n = jnp.sqrt((x ** 2).sum(axis=axis, keepdims=True))
            return x / jnp.maximum(n, NORM_EPS)
        key = jax.random.key(seed)
        ks = jax.random.split(key, 4)
        B, N, D, E, S, H = (64, 64, 256, 16, 16, 64)
        x = jax.random.normal(ks[0], (B, N, D), dtype=jnp.float32)
        mu = jax.random.normal(ks[1], (D, E, S), dtype=jnp.float32) / np.sqrt(D)
        w1 = jax.random.normal(ks[2], (E, D, H), dtype=jnp.float32) * np.sqrt(2.0 / D)
        w2 = jax.random.normal(ks[3], (E, H, D), dtype=jnp.float32) * np.sqrt(2.0 / (H + D))
        return {'x': x, 'ln_gamma': jnp.ones((D,), jnp.float32), 'ln_beta': jnp.zeros((D,), jnp.float32), 'mu': mu, 'scale': jnp.ones((1,), jnp.float32), 'w1': w1, 'b1': jnp.zeros((E, H), jnp.float32), 'w2': w2, 'b2': jnp.zeros((E, D), jnp.float32)}
    _L1_ffn_in = _L1_ffn_setup()

    def _L2_attn_setup():
        import jax, jax.numpy as jnp
        import numpy as np
        B, L, D, H = (2, 512, 256, 16)
        Dh = D // H
        key = jax.random.key(seed)
        kx, kq, kk, kv, ko = jax.random.split(key, 5)
        scale = 1.0 / np.sqrt(D)
        return {'x': jax.random.normal(kx, (B, L, D), dtype=jnp.float32), 'Wq': jax.random.normal(kq, (D, H, Dh), dtype=jnp.float32) * scale, 'Wk': jax.random.normal(kk, (D, H, Dh), dtype=jnp.float32) * scale, 'Wv': jax.random.normal(kv, (D, H, Dh), dtype=jnp.float32) * scale, 'Wout': jax.random.normal(ko, (H, Dh, D), dtype=jnp.float32) * (1.0 / np.sqrt(D))}
    _L2_attn_in = _L2_attn_setup()

    def _L2_ffn_setup():
        import jax, jax.numpy as jnp
        import numpy as np
        HIDDEN = 256
        FF = 1024
        N_EXPERTS = 8
        CAP_FACTOR = 1.0
        B, S = (4, 512)
        STD = 0.02

        def _gelu(x):
            return x * 0.5 * (1.0 + jax.lax.erf(x / 1.41421))
        key = jax.random.key(seed)
        ks = jax.random.split(key, 6)
        x = jax.random.normal(ks[0], (B, S, HIDDEN), dtype=jnp.float32)
        W_sw = jax.random.normal(ks[1], (HIDDEN, N_EXPERTS), dtype=jnp.float32) * STD
        b_sw = jnp.zeros((N_EXPERTS,), dtype=jnp.float32)
        W1 = jax.random.normal(ks[2], (N_EXPERTS, HIDDEN, FF), dtype=jnp.float32) * STD
        b1 = jnp.zeros((N_EXPERTS, FF), dtype=jnp.float32)
        W2 = jax.random.normal(ks[3], (N_EXPERTS, FF, HIDDEN), dtype=jnp.float32) * STD
        b2 = jnp.zeros((N_EXPERTS, HIDDEN), dtype=jnp.float32)
        return {'x': x, 'W_sw': W_sw, 'b_sw': b_sw, 'W1': W1, 'b1': b1, 'W2': W2, 'b2': b2}
    _L2_ffn_in = _L2_ffn_setup()

    def _L3_attn_setup():
        import jax, jax.numpy as jnp
        import numpy as np
        B, T, HID = (16, 128, 256)
        NH, NKV, D = (8, 4, 128)
        THETA = 10000.0

        def _rotate_half(x):
            x1, x2 = (x[..., :x.shape[-1] // 2], x[..., x.shape[-1] // 2:])
            return jnp.concatenate((-x2, x1), axis=-1)
        key = jax.random.key(seed)
        k0, k1, k2, k3, k4 = jax.random.split(key, 5)
        s = 0.02
        return {'hidden_states': jax.random.normal(k0, (B, T, HID), dtype=jnp.float32), 'Wq': s * jax.random.normal(k1, (HID, NH * D), dtype=jnp.float32), 'Wk': s * jax.random.normal(k2, (HID, NKV * D), dtype=jnp.float32), 'Wv': s * jax.random.normal(k3, (HID, NKV * D), dtype=jnp.float32), 'Wo': s * jax.random.normal(k4, (NH * D, HID), dtype=jnp.float32)}
    _L3_attn_in = _L3_attn_setup()

    def _L3_ffn_setup():
        import jax, jax.numpy as jnp
        import numpy as np
        DIM = 256
        HIDDEN = 768
        SCALE = 1.0 / 127.0

        def _dequant(w_int, dtype):
            return w_int.astype(dtype) * jnp.asarray(SCALE, dtype)
        key = jax.random.key(seed)
        k_x, k_g, k_u, k_d = jax.random.split(key, 4)
        x = jax.random.normal(k_x, (4, 512, DIM), dtype=jnp.float32)
        w_gate = jax.random.randint(k_g, (HIDDEN, DIM), -127, 128, dtype=jnp.int32)
        w_up = jax.random.randint(k_u, (HIDDEN, DIM), -127, 128, dtype=jnp.int32)
        w_down = jax.random.randint(k_d, (DIM, HIDDEN), -127, 128, dtype=jnp.int32)
        return {'x': x, 'w_gate': w_gate, 'w_up': w_up, 'w_down': w_down}
    _L3_ffn_in = _L3_ffn_setup()
    _d = {'L0_attn_x': _L0_attn_in['x'], 'L0_attn_W_qkv': _L0_attn_in['W_qkv'], 'L0_ffn_w_gate': _L0_ffn_in['w_gate'], 'L0_ffn_w_up': _L0_ffn_in['w_up'], 'L0_ffn_w_down': _L0_ffn_in['w_down'], 'L1_attn_w_qkv': _L1_attn_in['w_qkv'], 'L1_attn_w_out': _L1_attn_in['w_out'], 'L1_ffn_ln_gamma': _L1_ffn_in['ln_gamma'], 'L1_ffn_ln_beta': _L1_ffn_in['ln_beta'], 'L1_ffn_mu': _L1_ffn_in['mu'], 'L1_ffn_scale': _L1_ffn_in['scale'], 'L1_ffn_w1': _L1_ffn_in['w1'], 'L1_ffn_b1': _L1_ffn_in['b1'], 'L1_ffn_w2': _L1_ffn_in['w2'], 'L1_ffn_b2': _L1_ffn_in['b2'], 'L2_attn_Wq': _L2_attn_in['Wq'], 'L2_attn_Wk': _L2_attn_in['Wk'], 'L2_attn_Wv': _L2_attn_in['Wv'], 'L2_attn_Wout': _L2_attn_in['Wout'], 'L2_ffn_W_sw': _L2_ffn_in['W_sw'], 'L2_ffn_b_sw': _L2_ffn_in['b_sw'], 'L2_ffn_W1': _L2_ffn_in['W1'], 'L2_ffn_b1': _L2_ffn_in['b1'], 'L2_ffn_W2': _L2_ffn_in['W2'], 'L2_ffn_b2': _L2_ffn_in['b2'], 'L3_attn_Wq': _L3_attn_in['Wq'], 'L3_attn_Wk': _L3_attn_in['Wk'], 'L3_attn_Wv': _L3_attn_in['Wv'], 'L3_attn_Wo': _L3_attn_in['Wo'], 'L3_ffn_w_gate': _L3_ffn_in['w_gate'], 'L3_ffn_w_up': _L3_ffn_in['w_up'], 'L3_ffn_w_down': _L3_ffn_in['w_down']}
    _x0 = _d['L0_attn_x']
    _d['L0_attn_x'] = jax.random.normal(jax.random.fold_in(jax.random.key(seed), 1), (4, 1024, 256), dtype=_x0.dtype)
    del _x0
    return _d

def reference(L0_attn_x, L0_attn_W_qkv, L0_ffn_w_gate, L0_ffn_w_up, L0_ffn_w_down, L1_attn_w_qkv, L1_attn_w_out, L1_ffn_ln_gamma, L1_ffn_ln_beta, L1_ffn_mu, L1_ffn_scale, L1_ffn_w1, L1_ffn_b1, L1_ffn_w2, L1_ffn_b2, L2_attn_Wq, L2_attn_Wk, L2_attn_Wv, L2_attn_Wout, L2_ffn_W_sw, L2_ffn_b_sw, L2_ffn_W1, L2_ffn_b1, L2_ffn_W2, L2_ffn_b2, L3_attn_Wq, L3_attn_Wk, L3_attn_Wv, L3_attn_Wo, L3_ffn_w_gate, L3_ffn_w_up, L3_ffn_w_down):

    def _L0_attn_ref(x, W_qkv):
        import jax, jax.numpy as jnp
        import numpy as np
        DIM = 256
        qkv = jnp.einsum('bnd,ed->bne', x, W_qkv)
        B, N, _ = qkv.shape
        qkv = qkv.reshape(B, N, 3, DIM).transpose(2, 0, 1, 3)
        q, k, v = (qkv[0], qkv[1], qkv[2])
        scale = DIM ** (-0.5)
        attn = jnp.einsum('bnd,bmd->bnm', q * scale, k)
        attn = jax.nn.softmax(attn, axis=-1)
        out = jnp.einsum('bnm,bmd->bnd', attn, v)
        return out

    def _L0_ffn_ref(x, w_gate, w_up, w_down):
        import jax, jax.numpy as jnp
        import numpy as np
        DIM = 256
        HIDDEN = 768
        SCALE = 1.0 / 127.0

        def _dequant(w_int, dtype):
            return w_int.astype(dtype) * jnp.asarray(SCALE, dtype)
        wg = _dequant(w_gate, x.dtype)
        wu = _dequant(w_up, x.dtype)
        wd = _dequant(w_down, x.dtype)
        gate = jnp.einsum('bsd,hd->bsh', x, wg)
        up = jnp.einsum('bsd,hd->bsh', x, wu)
        h = jax.nn.silu(gate) * up
        return jnp.einsum('bsh,dh->bsd', h, wd)

    def _L1_attn_ref(x, w_qkv, w_out):
        import jax, jax.numpy as jnp
        import numpy as np
        N_HEADS = 16
        ROPE_BASE = 10000.0

        def _rope_tables(seq_len, d_head, dtype):
            inv_freq = 1.0 / ROPE_BASE ** (jnp.arange(0, d_head, 2, dtype=jnp.float32) / d_head)
            t = jnp.arange(seq_len, dtype=jnp.float32)
            freqs = t[:, None] * inv_freq[None, :]
            return (jnp.cos(freqs).astype(dtype), jnp.sin(freqs).astype(dtype))

        def _apply_rope(x, cos, sin):
            half = x.shape[-1] // 2
            x1, x2 = (x[..., :half], x[..., half:])
            return jnp.concatenate([x1 * cos - x2 * sin, x2 * cos + x1 * sin], axis=-1)
        B, S, D = x.shape
        H = N_HEADS
        dh = D // H
        scale = dh ** (-0.5)
        qkv = x @ w_qkv
        q, k, v = jnp.split(qkv, 3, axis=-1)

        def to_heads(t):
            return t.reshape(B, S, H, dh).transpose(0, 2, 1, 3)
        q, k, v = (to_heads(q), to_heads(k), to_heads(v))
        cos, sin = _rope_tables(S, dh, x.dtype)
        q = _apply_rope(q, cos, sin)
        k = _apply_rope(k, cos, sin)
        scores = jnp.einsum('bhqd,bhkd->bhqk', q, k) * scale
        causal = jnp.tril(jnp.ones((S, S), dtype=bool))
        scores = jnp.where(causal, scores, jnp.finfo(scores.dtype).min)
        attn = jax.nn.softmax(scores, axis=-1)
        out = jnp.einsum('bhqk,bhkd->bhqd', attn, v)
        out = out.transpose(0, 2, 1, 3).reshape(B, S, D)
        return out @ w_out

    def _L1_ffn_ref(x, ln_gamma, ln_beta, mu, scale, w1, b1, w2, b2):
        import jax, jax.numpy as jnp
        import numpy as np
        LN_EPS = 1e-05
        NORM_EPS = 1e-12

        def _layernorm(x, gamma, beta):
            mu = x.mean(axis=-1, keepdims=True)
            var = ((x - mu) ** 2).mean(axis=-1, keepdims=True)
            return (x - mu) * jax.lax.rsqrt(var + LN_EPS) * gamma + beta

        def _l2norm(x, axis):
            n = jnp.sqrt((x ** 2).sum(axis=axis, keepdims=True))
            return x / jnp.maximum(n, NORM_EPS)
        B, N, D = x.shape
        _, E, S = mu.shape
        xn = _layernorm(x, ln_gamma, ln_beta)
        x_unit = _l2norm(xn, axis=-1)
        mu_unit = _l2norm(mu, axis=0)
        logits = jnp.einsum('bnd,des->bnes', x_unit * scale, mu_unit)
        dispatch = jax.nn.softmax(logits, axis=1)
        combine = jax.nn.softmax(logits.reshape(B, N, E * S), axis=-1).reshape(B, N, E, S)
        slot_in = jnp.einsum('bnd,bnes->besd', xn, dispatch)
        h = jax.nn.gelu(jnp.einsum('besd,edh->besh', slot_in, w1) + b1[None, :, None, :], approximate=False)
        slot_out = jnp.einsum('besh,ehd->besd', h, w2) + b2[None, :, None, :]
        out = jnp.einsum('besd,bnes->bnd', slot_out, combine)
        return out

    def _L2_attn_ref(x, Wq, Wk, Wv, Wout):
        import jax, jax.numpy as jnp
        import numpy as np
        B, L, D, H = (2, 512, 256, 16)
        Dh = D // H
        q = jnp.einsum('bld,dhe->blhe', x, Wq)
        k = jnp.einsum('bld,dhe->blhe', x, Wk)
        v = jnp.einsum('bld,dhe->blhe', x, Wv)
        a = jnp.einsum('bqhd,bkhd->bhqk', q, k) / Dh ** 0.5
        Lq = x.shape[1]
        mask = jnp.tril(jnp.ones((1, 1, Lq, Lq), dtype=jnp.bool_))
        NEG_INF = jnp.finfo(jnp.float32).min
        a = jnp.where(mask, a, NEG_INF)
        a = jax.nn.softmax(a, axis=-1)
        o = jnp.einsum('bhqk,bkhd->bqhd', a, v)
        return jnp.einsum('blhe,hed->bld', o, Wout)

    def _L2_ffn_ref(x, W_sw, b_sw, W1, b1, W2, b2):
        import jax, jax.numpy as jnp
        import numpy as np
        HIDDEN = 256
        FF = 1024
        N_EXPERTS = 8
        CAP_FACTOR = 1.0
        B, S = (4, 512)
        STD = 0.02

        def _gelu(x):
            return x * 0.5 * (1.0 + jax.lax.erf(x / 1.41421))
        Bb, Ss, D = x.shape
        T = Bb * Ss
        E = W1.shape[0]
        capacity = int(CAP_FACTOR * T / E)
        xf = x.reshape(T, D)
        logits = xf @ W_sw + b_sw
        probs = jax.nn.softmax(logits, axis=-1)
        pmax = jnp.max(probs, axis=-1)
        routes = jnp.argmax(probs, axis=-1)
        factor = pmax / jax.lax.stop_gradient(pmax)
        xs = xf * factor[:, None]
        onehot = jax.nn.one_hot(routes, E, dtype=jnp.int32)
        pos = jnp.cumsum(onehot, axis=0) - 1
        pos_tok = jnp.take_along_axis(pos, routes[:, None], axis=1)[:, 0]
        keep = pos_tok < capacity
        pos_safe = jnp.where(keep, pos_tok, capacity)
        buf = jnp.zeros((E, capacity + 1, D), dtype=xs.dtype)
        buf = buf.at[routes, pos_safe].set(xs)
        buf = buf[:, :capacity]
        h = _gelu(jnp.einsum('ecd,edf->ecf', buf, W1) + b1[:, None, :])
        expert_out = jnp.einsum('ecf,efd->ecd', h, W2) + b2[:, None, :]
        gathered = expert_out[routes, jnp.minimum(pos_tok, capacity - 1)]
        final = jnp.where(keep[:, None], gathered, xs)
        return final.reshape(Bb, Ss, D)

    def _L3_attn_ref(hidden_states, Wq, Wk, Wv, Wo):
        import jax, jax.numpy as jnp
        import numpy as np
        B, T, HID = (16, 128, 256)
        NH, NKV, D = (8, 4, 128)
        THETA = 10000.0

        def _rotate_half(x):
            x1, x2 = (x[..., :x.shape[-1] // 2], x[..., x.shape[-1] // 2:])
            return jnp.concatenate((-x2, x1), axis=-1)
        b, t, _ = hidden_states.shape
        q = (hidden_states @ Wq).reshape(b, t, NH, D).transpose(0, 2, 1, 3)
        k = (hidden_states @ Wk).reshape(b, t, NKV, D).transpose(0, 2, 1, 3)
        v = (hidden_states @ Wv).reshape(b, t, NKV, D).transpose(0, 2, 1, 3)
        inv_freq = 1.0 / THETA ** (jnp.arange(0, D, 2, dtype=jnp.float32) / D)
        freqs = jnp.outer(jnp.arange(t, dtype=jnp.float32), inv_freq)
        emb = jnp.concatenate((freqs, freqs), axis=-1)
        cos, sin = (jnp.cos(emb), jnp.sin(emb))
        q = q * cos + _rotate_half(q) * sin
        k = k * cos + _rotate_half(k) * sin
        groups = NH // NKV
        k = jnp.repeat(k, groups, axis=1)
        v = jnp.repeat(v, groups, axis=1)
        scale = 1.0 / jnp.sqrt(jnp.float32(D))
        attn = jnp.einsum('bhtd,bhsd->bhts', q, k) * scale
        causal = jnp.triu(jnp.ones((t, t), dtype=bool), k=1)
        attn = jnp.where(causal, -jnp.inf, attn)
        attn = jax.nn.softmax(attn, axis=-1)
        out = jnp.einsum('bhts,bhsd->bhtd', attn, v)
        out = out.transpose(0, 2, 1, 3).reshape(b, t, NH * D)
        return out @ Wo

    def _L3_ffn_ref(x, w_gate, w_up, w_down):
        import jax, jax.numpy as jnp
        import numpy as np
        DIM = 256
        HIDDEN = 768
        SCALE = 1.0 / 127.0

        def _dequant(w_int, dtype):
            return w_int.astype(dtype) * jnp.asarray(SCALE, dtype)
        wg = _dequant(w_gate, x.dtype)
        wu = _dequant(w_up, x.dtype)
        wd = _dequant(w_down, x.dtype)
        gate = jnp.einsum('bsd,hd->bsh', x, wg)
        up = jnp.einsum('bsd,hd->bsh', x, wu)
        h = jax.nn.silu(gate) * up
        return jnp.einsum('bsh,dh->bsd', h, wd)
    x = L0_attn_x
    xn = _layernorm(x, axis=-1)
    s = _L0_attn_ref(xn, L0_attn_W_qkv)
    g = _silu(_L0_ffn_ref(xn, L0_ffn_w_gate, L0_ffn_w_up, L0_ffn_w_down))
    x = x + s * g
    xn = _layernorm(x, axis=-1)
    s = _L1_attn_ref(xn, L1_attn_w_qkv, L1_attn_w_out)
    g = _silu(_L1_ffn_ref(xn, L1_ffn_ln_gamma, L1_ffn_ln_beta, L1_ffn_mu, L1_ffn_scale, L1_ffn_w1, L1_ffn_b1, L1_ffn_w2, L1_ffn_b2))
    x = x + s * g
    xn = _layernorm(x, axis=-1)
    s = _L2_attn_ref(xn, L2_attn_Wq, L2_attn_Wk, L2_attn_Wv, L2_attn_Wout)
    g = _silu(_L2_ffn_ref(xn, L2_ffn_W_sw, L2_ffn_b_sw, L2_ffn_W1, L2_ffn_b1, L2_ffn_W2, L2_ffn_b2))
    x = x + s * g
    xn = _layernorm(x, axis=-1)
    s = _L3_attn_ref(xn, L3_attn_Wq, L3_attn_Wk, L3_attn_Wv, L3_attn_Wo)
    g = _silu(_L3_ffn_ref(xn, L3_ffn_w_gate, L3_ffn_w_up, L3_ffn_w_down))
    x = x + s * g
    return x

_drawn_inputs = setup_inputs


def setup_inputs(seed=0):
    import zlib

    import numpy as np

    out = dict(_drawn_inputs(seed))
    spreads = {'L1_ffn_ln_gamma': (1.0, 0.6),
     'L1_ffn_ln_beta': (0.0, 0.8),
     'L1_ffn_b1': (0.0, 0.8),
     'L1_ffn_b2': (0.0, 0.8),
     'L2_ffn_b_sw': (0.0, 0.8),
     'L2_ffn_b1': (0.0, 0.8),
     'L2_ffn_b2': (0.0, 0.8)}
    factors = {'L1_attn_w_qkv': 8.0,
     'L1_attn_w_out': 8.0,
     'L1_ffn_mu': 8.0,
     'L1_ffn_w1': 8.0,
     'L1_ffn_w2': 8.0,
     'L2_attn_Wq': 8.0,
     'L2_attn_Wk': 8.0,
     'L2_attn_Wv': 8.0,
     'L2_attn_Wout': 8.0,
     'L2_ffn_W_sw': 8.0,
     'L2_ffn_W1': 8.0,
     'L2_ffn_W2': 8.0,
     'L3_attn_Wq': 8.0,
     'L3_attn_Wk': 8.0}
    for name, (base, spread) in spreads.items():
        noise = np.random.default_rng([zlib.crc32(name.encode()), seed]).standard_normal(out[name].shape)
        drawn = base * np.exp(spread * noise) if base else spread * noise
        out[name] = jnp.asarray(drawn.astype(out[name].dtype))
    for name, factor in factors.items():
        out[name] = (out[name] * factor).astype(out[name].dtype)
    return out
```

```python
import numpy as np
import concourse.bass as bass
from concourse import mybir
from contextlib import ExitStack

F32 = mybir.dt.float32
BF16 = mybir.dt.bfloat16
I32 = mybir.dt.int32
U32 = mybir.dt.uint32
ALU = mybir.AluOpType
ACT = mybir.ActivationFunctionType
AX = mybir.AxisListType.X

P = 128
B, S, D = 4, 1024, 256
TOK = B * S
CH = 512
KC = D // P
TT = CH // P
QB = S // P
NEG = -1.0e30


class Chain:

    def __init__(self, eng, sem, base=0):
        self.eng, self.sem, self.base, self.n = eng, sem, base, 0

    def __call__(self, ins):
        self.n += 1
        ins.then_inc(self.sem, 1)
        self.eng.wait_ge(self.sem, self.base + self.n)


class SeqNumber:

    def __init__(self, value, rest, banks):
        self.value, self.rest, self.banks = value, rest % banks, banks

    def __add__(self, k):
        return SeqNumber(self.value + k, self.rest + k, self.banks)


def count(q):
    return q.value if isinstance(q, SeqNumber) else q


class Stage:

    def __init__(self, nc, name):
        self.nc, self.name, self.ctx, self.sems = nc, name, ExitStack(), []
        self.ctx.callback(self.clear)

    def clear(self):
        self.nc.clear_and_free_semaphores(self.sems)
        self.nc.all_engine_barrier()

    def sb(self, name, shape, dt=F32):
        return self.ctx.enter_context(self.nc.sbuf_tensor(f"{self.name}_{name}", shape, dt))

    def ps(self, name, shape=(P, 512), dt=F32):
        return self.ctx.enter_context(self.nc.psum_tensor(f"{self.name}_{name}", list(shape), dt))

    def sem(self, name):
        self.sems.append(self.nc.alloc_semaphore(name=f"{self.name}_{name}"))
        return self.sems[-1]


def one(ap, i):
    return ap[bass.ds(i, 1)]


def update_stage(nc, name, consts, x_in, x_out=None, xnT=None, xn=None, s_in=None, o_in=None, w_o=None,
                 o_chunks=0, g_in=None):
    st = Stage(nc, name)
    with st.ctx:
        upd, norm, proj = g_in is not None, xnT is not None, o_in is not None
        ident = st.sb("ident", [P, P])
        xt = st.sb("x", [P, 2, TT, D])
        if upd:
            gt = st.sb("g", [P, 2, TT, D])
            tmp = st.sb("tmp", [P, TT, D])
            if not proj:
                sin = st.sb("s", [P, 2, TT, D])
        if proj:
            NG = TT * o_chunks // 4
            ot = st.sb("o", [P, 2, TT, o_chunks * P])
            oT = st.sb("oT", [P, TT * o_chunks, P])
            wo = st.sb("wo", [P, o_chunks, D])
            T = [st.ps(f"T{k}") for k in range(2)]
            SP_ = [st.ps(f"S{k}", (P, 2, D)) for k in range(2)]
        if norm:
            stats = st.sb("stats", [P, TT, 6])
            mv = st.sb("mv", [P, TT, 2])
            vep = st.sb("vep", [P, TT])
            std = st.sb("std", [P, TT])
            rstd = st.sb("rstd", [P, TT])
            xnt = st.sb("xn", [P, 2, TT, D])
            xnTt = st.sb("xnT", [P, 2, KC, CH])
            X = [st.ps(f"X{k}") for k in range(2)]
        loaded = [st.sem(f"loaded{u}") for u in range(2)]
        consts_in = st.sem("consts_in")
        x_stored = [st.sem(f"x_stored{u}") for u in range(2)]
        stored = [st.sem(f"stored{u}") for u in range(2)]
        stats_seen = st.sem("stats_seen")
        inputs_free = st.sem("inputs_free")
        oT_ready = st.sem("oT_ready")
        oT_copied = st.sem("oT_copied")
        s_ready = st.sem("s_ready")
        s_used = st.sem("s_used")
        x_ready = st.sem("x_ready")
        var_ready = st.sem("var_ready")
        std_ready = st.sem("std_ready")
        xn_ready = st.sem("xn_ready")
        xT_ready = st.sem("xT_ready")
        xT_copied = st.sem("xT_copied")
        dve_self = st.sem("dve_self")
        loads = 1 + (1 if upd else 0) + (1 if upd and not proj else 0) + (len(o_in(0, 0)) if proj else 0)
        stores = (1 if norm else 0) + (1 if xn is not None else 0)
        block = st.ctx.enter_context(nc.Block())

        @block.sync
        def _(sp):
            sp.dma_start(ident[:], consts["ident"]).then_inc(consts_in, 16)
            if proj:
                sp.dma_start(wo[:], w_o.rearrange("(c p) n -> p c n", p=P)).then_inc(consts_in, 16)

            def load(i, u):
                n = i * 2 + u
                sp.dma_start(xt[:, u], one(x_in, n).rearrange("c p t d -> p (c t) d")).then_inc(loaded[u], 16)
                if upd:
                    sp.dma_start(gt[:, u], one(g_in, n).rearrange("c p t d -> p (c t) d")).then_inc(loaded[u], 16)
                    if not proj:
                        sp.dma_start(sin[:, u], one(s_in, n).rearrange("c p t d -> p (c t) d")).then_inc(loaded[u], 16)
                if proj:
                    for lo, hi, src in o_in(i, u):
                        sp.dma_start(ot[:, u, lo:hi, :].rearrange("p t (c n) -> p t c n", n=P), src).then_inc(loaded[u], 16)

            def body(i, more):
                for u in range(2):
                    n = i * 2 + u
                    if x_out is not None:
                        sp.wait_ge(x_ready, n + 1)
                        sp.dma_start(one(x_out, n).rearrange("c p t d -> p (c t) d"), xt[:, u]).then_inc(x_stored[u], 16)
                    if xn is not None:
                        sp.wait_ge(xn_ready, n + 1)
                        sp.dma_start(one(xn, n).rearrange("c p t d -> p (c t) d"), xnt[:, u]).then_inc(stored[u], 16)
                    if more:
                        if x_out is not None:
                            sp.wait_ge(x_stored[u], (i + 1) * 16)
                        sp.wait_ge(inputs_free, n + 1)
                        load(i + 1, u)
                    if norm:
                        sp.wait_ge(xT_copied, n * KC + 2 * KC)
                        sp.dma_start(xnT[:, :, bass.ds(n * CH, CH)], xnTt[:, u]).then_inc(stored[u], 16)
            load(0, 0)
            load(0, 1)
            with sp.Fori(0, B - 1) as i:
                body(i, True)
            body(B - 1, False)
            for u in range(2):
                if x_out is not None:
                    sp.wait_ge(x_stored[u], 16 * B)
                if stores:
                    sp.wait_ge(stored[u], 16 * stores * B)

        @block.tensor
        def _(pe):
            pe.wait_ge(consts_in, 32 if proj else 16)
            with pe.Fori(0, B) as i:
                if proj:
                    for u in range(2):
                        n = i * 2 + u
                        pe.wait_ge(loaded[u], (i + 1) * (16 * loads))
                        for g in range(NG):
                            pe.wait_ge(oT_copied, n * NG + g + 1)
                            for k in range(4):
                                t, c = divmod(g * 4 + k, o_chunks)
                                last = pe.transpose(T[g % 2][:, k * P:(k + 1) * P], ot[:, u, t, c * P:(c + 1) * P], ident[:])
                            last.then_inc(oT_ready, 1)
                        pe.wait_ge(oT_copied, n * NG + NG + 2)
                        for t in range(TT):
                            if t % 2 == 0:
                                pe.wait_ge(s_used, n * 2 + t // 2 + 1)
                            for c in range(o_chunks):
                                last = pe.matmul(SP_[t // 2][:, t % 2, :], oT[:, t * o_chunks + c, :], wo[:, c, :],
                                                 start=(c == 0), stop=(c == o_chunks - 1))
                            if t % 2 == 1:
                                last.then_inc(s_ready, 1)
                if norm:
                    for u in range(2):
                        n = i * 2 + u
                        pe.wait_ge(xn_ready, n + 1)
                        for c in range(KC):
                            pe.wait_ge(xT_copied, n * KC + c + 1)
                            for t in range(TT):
                                last = pe.transpose(X[c][:, t * P:(t + 1) * P], xnt[:, u, t, c * P:(c + 1) * P], ident[:])
                            last.then_inc(xT_ready, 1)

        @block.scalar
        def _(act):
            act.sem_inc(oT_copied, 2)
            act.sem_inc(xT_copied, KC)
            with act.Fori(0, B) as i:
                if proj:
                    for u in range(2):
                        n = i * 2 + u
                        for g in range(NG):
                            if g == 0:
                                act.wait_ge(s_ready, n * 2)
                            act.wait_ge(oT_ready, n * NG + g + 1)
                            act.copy(oT[:, g * 4:g * 4 + 4, :].rearrange("p a b -> p (a b)"), T[g % 2][:]).then_inc(oT_copied, 1)
                if norm:
                    for u in range(2):
                        n = i * 2 + u
                        act.wait_ge(var_ready, n + 1)
                        act.activation(std[:], vep[:], ACT.Sqrt).then_inc(std_ready, 1)
                        act.wait_ge(stored[u], i * (16 * stores))
                        for c in range(KC):
                            act.wait_ge(xT_ready, n * KC + c + 1)
                            act.copy(xnTt[:, u, c, :], X[c][:]).then_inc(xT_copied, 1)

        @block.vector
        def _(dve):
            dve.sem_inc(s_used, 2)
            PER = 2 * ((1 if proj else 2 if upd else 0) + (3 if norm else 0))
            with dve.Fori(0, B) as i:
                link = Chain(dve, dve_self, i * PER)
                for u in range(2):
                    n = i * 2 + u
                    dve.wait_ge(loaded[u], (i + 1) * (16 * loads))
                    if upd and proj:
                        for h in range(2):
                            dve.wait_ge(s_ready, n * 2 + h + 1)
                            dve.tensor_tensor(tmp[:, 2 * h:2 * h + 2, :], SP_[h][:], gt[:, u, 2 * h:2 * h + 2, :],
                                              ALU.mult).then_inc(s_used, 1)
                        dve.wait_ge(s_used, n * 2 + 4)
                        link(dve.tensor_tensor(xt[:, u], xt[:, u], tmp[:], ALU.add))
                    elif upd:
                        link(dve.tensor_tensor(tmp[:], sin[:, u], gt[:, u], ALU.mult))
                        link(dve.tensor_tensor(xt[:, u], xt[:, u], tmp[:], ALU.add))
                    if x_out is not None:
                        dve.sem_inc(x_ready, 1)
                    if not norm:
                        dve.sem_inc(inputs_free, 1)
                        continue
                    for t in range(TT):
                        last = dve.bn_stats(stats[:, t, :], xt[:, u, t, :])
                    link(last)
                    dve.sem_inc(stats_seen, 1)
                    for t in range(TT):
                        last = dve.bn_aggr(mv[:, t, :], stats[:, t, :])
                    link(last)
                    dve.tensor_scalar(vep[:], mv[:, :, 1], 1e-5, None, ALU.add).then_inc(var_ready, 1)
                    dve.wait_ge(std_ready, n + 1)
                    link(dve.reciprocal(rstd[:], std[:]))
                    dve.wait_ge(stored[u], i * (16 * stores))
                    for t in range(TT):
                        last = dve.tensor_scalar(xnt[:, u, t, :], xt[:, u, t, :], mv[:, t, 0:1], rstd[:, t:t + 1],
                                                 ALU.subtract, ALU.mult)
                    last.then_inc(xn_ready, 1)
                    dve.wait_ge(xn_ready, n + 1)
                    dve.sem_inc(inputs_free, 1)


def project_stage(nc, name, consts, xnT, w, q_tiles, k_tiles, v_cols, q_scale, qk_out, v_out, rope=None, parts=False):
    st = Stage(nc, name)
    with st.ctx:
        J = q_tiles + k_tiles
        NW = J * P + v_cols
        VB = v_cols // 256
        VS = TT * VB // 2
        VD = len(v_out(0, 0))
        xT = st.sb("xT", [P, 2, KC, CH])
        wt = st.sb("w", [P, KC, NW])
        qs = st.sb("qs", [P, 2, CH])
        if rope:
            perm = st.sb("perm", [P, P])
            cos = st.sb("cos", [P, S])
            sin = st.sb("sin", [P, S])
            tc = st.sb("tc", [P, 2, CH])
            ts = st.sb("ts", [P, 2, CH])
            RP = [st.ps(f"R{k}") for k in range(2)]
        if parts:
            part = st.sb("part", [P, 2, 3, CH], BF16)
            rest = st.sb("rest", [P, 2, CH])
        if rope or not parts:
            fin = st.sb("fin", [P, 2, CH])
        else:
            fin = qs
        vs = st.sb("v", [P, 2, TT, v_cols])
        QP = [st.ps(f"Q{k}") for k in range(2)]
        VP = [st.ps(f"V{k}") for k in range(2)]
        consts_in = st.sem("consts_in")
        x_in = [st.sem(f"x_in{u}") for u in range(2)]
        x_free = st.sem("x_free")
        q_ready = st.sem("q_ready")
        q_copied = st.sem("q_copied")
        r_ready = st.sem("r_ready")
        cos_ready = st.sem("cos_ready")
        f_ready = st.sem("f_ready")
        hi_ready = st.sem("hi_ready")
        r1_ready = st.sem("r1_ready")
        mid_ready = st.sem("mid_ready")
        tile_ready = st.sem("tile_ready")
        tile_stored = [st.sem(f"tile_stored{k}") for k in range(2)]
        v_ready = st.sem("v_ready")
        v_copied = st.sem("v_copied")
        v_stored = [st.sem(f"v_stored{u}") for u in range(2)]
        dve_self = st.sem("dve_self")
        assert J % 2 == 0
        block = st.ctx.enter_context(nc.Block())

        @block.sync
        def _(sp):
            sp.dma_start(wt[:], w.rearrange("(c p) n -> p c n", p=P)).then_inc(consts_in, 16)
            if rope:
                for t, src in zip((perm, cos, sin), rope):
                    sp.dma_start(t[:], src).then_inc(consts_in, 16)

            def load(i, u):
                sp.dma_start(xT[:, u], xnT[:, :, bass.ds((i * 2 + u) * CH, CH)]).then_inc(x_in[u], 16)
            ready, credits = (tile_ready, 2) if parts else (f_ready, 2) if rope else (q_copied, 2)

            def body(i, more):
                for u in range(2):
                    n = i * 2 + u
                    for j in range(J):
                        sp.wait_ge(ready, n * J + (j + 1 + credits))
                        sp.dma_start(qk_out(i, u, j), part[:, j % 2] if parts else fin[:, j % 2]).then_inc(tile_stored[j % 2], 16)
                    sp.wait_ge(v_copied, (n + 1) * VS + 2)
                    for lo, hi, dst in v_out(i, u):
                        sp.dma_start(dst, vs[:, u, lo:hi, :].rearrange("p t (c n) -> p t c n", n=P)).then_inc(v_stored[u], 16)
                    if more:
                        sp.wait_ge(x_free, n + 1)
                        load(i + 1, u)
            load(0, 0)
            load(0, 1)
            with sp.Fori(0, B - 1) as i:
                body(i, True)
            body(B - 1, False)
            for k in range(2):
                sp.wait_ge(tile_stored[k], 16 * B * J)
                sp.wait_ge(v_stored[k], 16 * VD * B)

        @block.tensor
        def _(pe):
            pe.wait_ge(consts_in, 64 if rope else 16)

            def rotate(n, j):
                m = n * J + j
                pe.wait_ge(q_copied, m + 3)
                pe.wait_ge(f_ready, m + 1)
                pe.matmul(RP[j % 2][:], perm[:], qs[:, j % 2], start=True, stop=True).then_inc(r_ready, 1)

            with pe.Fori(0, B) as i:
                for u in range(2):
                    n = i * 2 + u
                    pe.wait_ge(x_in[u], (i + 1) * 16)
                    for j in range(J):
                        pe.wait_ge(q_copied, n * J + j + 1)
                        for c in range(KC):
                            last = pe.matmul(QP[j % 2][:], wt[:, c, j * P:(j + 1) * P], xT[:, u, c, :],
                                             start=(c == 0), stop=(c == KC - 1))
                        last.then_inc(q_ready, 1)
                        if rope and j:
                            rotate(n, j - 1)
                    for k in range(VS):
                        pe.wait_ge(v_copied, n * VS + k + 1)
                        for h in range(2):
                            t, b = divmod(k * 2 + h, VB)
                            for c in range(KC):
                                last = pe.matmul(VP[k % 2][:, h * 256:(h + 1) * 256], xT[:, u, c, t * P:(t + 1) * P],
                                                 wt[:, c, J * P + b * 256:J * P + (b + 1) * 256],
                                                 start=(c == 0), stop=(c == KC - 1))
                        last.then_inc(v_ready, 1)
                        if rope and k == 0:
                            rotate(n, J - 1)
                    pe.wait_ge(v_ready, (n + 1) * VS)
                    pe.sem_inc(x_free, 1)

        @block.scalar
        def _(act):
            act.sem_inc(q_copied, 2)
            with act.Fori(0, B) as i:
                for u in range(2):
                    n = i * 2 + u

                    def high(j):
                        m = n * J + j
                        if rope:
                            act.wait_ge(f_ready, m + 3)
                        act.wait_ge(tile_stored[j % 2], (n * (J // 2) + j // 2) * 16)
                        act.copy(part[:, j % 2, 0, :], fin[:, j % 2]).then_inc(hi_ready, 1)

                    def mid(j):
                        m = n * J + j
                        act.wait_ge(r1_ready, m + 1)
                        act.copy(part[:, j % 2, 1, :], rest[:, j % 2]).then_inc(mid_ready, 1)

                    for j in range(J):
                        m = n * J + j
                        act.wait_ge(q_ready, m + 1)
                        if rope:
                            act.wait_ge(f_ready, m + 1)
                            act.wait_ge(cos_ready, m + 1)
                        elif parts:
                            act.wait_ge(tile_ready, m + 1)
                        else:
                            act.wait_ge(tile_stored[j % 2], (n * (J // 2) + j // 2) * 16)
                        dst = qs if (rope or parts) else fin
                        ins = act.activation(dst[:, j % 2], QP[j % 2][:], ACT.Copy, scale=q_scale if j < q_tiles else 1.0)
                        ins.then_inc(q_copied, 1)
                        if parts and not rope:
                            act.wait_ge(q_copied, m + 3)
                            high(j)
                            mid(j)
                        if parts and rope and j:
                            high(j - 1)
                            mid(j - 1)
                    if parts and rope:
                        high(J - 1)
                        mid(J - 1)
                    act.wait_ge(v_stored[u], i * (16 * VD))
                    for k in range(VS):
                        act.wait_ge(v_ready, n * VS + k + 1)
                        act.copy(vs[:, u].rearrange("p t n -> p (t n)")[:, k * 512:(k + 1) * 512], VP[k % 2][:]).then_inc(v_copied, 1)

        @block.vector
        def _(dve):
            dve.sem_inc(f_ready, 2)
            dve.sem_inc(tile_ready, 2)
            if not (rope or parts):
                return
            per = 1 if rope else 0
            with dve.Fori(0, B) as i:
                link = Chain(dve, dve_self, i * (2 * J * per))
                for u in range(2):
                    n = i * 2 + u
                    for j in range(J):
                        m, k = n * J + j, j % 2
                        if rope:
                            dve.wait_ge(r_ready, m + 1)
                            half = sin[:, u * CH:(u + 1) * CH]
                            link(dve.tensor_tensor(ts[:, k], RP[k][:], half, ALU.mult))
                            dve.wait_ge(cos_ready, m + 3)
                            if not parts:
                                dve.wait_ge(tile_stored[k], (n * (J // 2) + j // 2) * 16)
                            dve.tensor_tensor(fin[:, k], tc[:, k], ts[:, k], ALU.add).then_inc(f_ready, 1)
                        if parts:
                            dve.wait_ge(hi_ready, m + 1)
                            dve.tensor_tensor(rest[:, k], fin[:, k], part[:, k, 0, :], ALU.subtract).then_inc(r1_ready, 1)
                            dve.wait_ge(mid_ready, m + 1)
                            dve.tensor_tensor(part[:, k, 2, :], rest[:, k], part[:, k, 1, :], ALU.subtract).then_inc(tile_ready, 1)

        @block.gpsimd
        def _(pool):
            pool.sem_inc(cos_ready, 2)
            pool.sem_inc(v_copied, 2)
            if not rope:
                return
            with pool.Fori(0, B) as i:
                for u in range(2):
                    for j in range(J):
                        m, k = (i * 2 + u) * J + j, j % 2
                        pool.wait_ge(q_copied, m + 3)
                        pool.wait_ge(f_ready, m + 1)
                        pool.tensor_tensor(tc[:, k], qs[:, k], cos[:, u * CH:(u + 1) * CH], ALU.mult).then_inc(cos_ready, 1)


def attention_stage(nc, name, consts, qT, kT, v, out, units, heads, kc, dv, causal):
    st = Stage(nc, name)
    with st.ctx:
        qt = st.sb("q", [P, 2, heads, kc, S])
        kt = st.sb("k", [P, 2, kc, S])
        vt = st.sb("v", [P, 2, QB, dv])
        ident = st.sb("ident", [P, P])
        if causal:
            identb = st.sb("identb", [P, P], BF16)
            mask = st.sb("mask", [P, P], BF16)
        prob = st.sb("prob", [P, 2, S])
        pT = st.sb("pT", [P, 2, QB, P])
        nmax = st.sb("nmax", [P, 2])
        rsum = st.sb("rsum", [P, 4])
        rinv = st.sb("rinv", [P, 2])
        ot = st.sb("o", [P, 2, dv])
        SC = [st.ps(f"SC{k}", (P, S)) for k in range(2)]
        T = [st.ps(f"T{k}") for k in range(2)]
        O = [st.ps(f"O{k}", (P, dv)) for k in range(2)]
        consts_in = st.sem("consts_in")
        loaded = [st.sem(f"loaded{u}") for u in range(2)]
        unit_free = st.sem("unit_free")
        s_ready = st.sem("s_ready")
        m_ready = st.sem("m_ready")
        p_ready = st.sem("p_ready")
        t_ready = st.sem("t_ready")
        a_copied = st.sem("a_copied")
        d_copied = st.sem("d_copied")
        o_ready = st.sem("o_ready")
        o_used = st.sem("o_used")
        stored = [st.sem(f"stored{k}") for k in range(2)]
        dve_self = st.sem("dve_self")
        blocks = [(qb + 1 if causal else QB) for qb in range(QB)]
        NS = 2 * heads * QB
        nb = [blocks[s % QB] for s in range(NS)]
        ng = [(b + 3) // 4 for b in nb]
        gbase = [sum(ng[:s]) for s in range(NS + 1)]
        acount = [sum(1 for g in range(gbase[s]) if g % 2 == 0) for s in range(NS + 1)]
        dcount = [sum(1 for g in range(gbase[s]) if g % 2 == 1) for s in range(NS + 1)]
        assert gbase[NS] % 2 == 0
        A, DC = acount[NS], dcount[NS]
        TC = ng[NS - 1]
        block = st.ctx.enter_context(nc.Block())

        @block.sync
        def _(sp):
            sp.dma_start(ident[:], consts["ident"]).then_inc(consts_in, 16)
            if causal:
                sp.dma_start(identb[:], consts["identb"]).then_inc(consts_in, 16)
                sp.dma_start(mask[:], consts["mask"]).then_inc(consts_in, 16)
            def load(i, u):
                n = i * 2 + u
                sp.wait_ge(unit_free, n + 1)
                for h in range(heads):
                    sp.dma_start(qt[:, u, h], one(qT, n)[:, h].rearrange("a (c p) t -> p (a c) t", p=P)).then_inc(loaded[u], 16)
                sp.dma_start(kt[:, u], one(kT, n).rearrange("a (c p) t -> p (a c) t", p=P)).then_inc(loaded[u], 16)
                sp.dma_start(vt[:, u], one(v, n).rearrange("a (b p) n -> p (a b) n", p=P)).then_inc(loaded[u], 16)
            for u in range(2):
                load(0, u)

            def body(i, more):
                for s in range(NS):
                    u, h, qb = s // (heads * QB), s // QB % heads, s % QB
                    k = s % 2
                    sp.wait_ge(o_used, i * NS + s + 1 + 2)
                    sp.dma_start(one(out, i * 2 + u)[:, h, qb * P:(qb + 1) * P, :].rearrange("a p n -> (a p) n"),
                                 ot[:, k]).then_inc(stored[k], 16)
                    if more and (s + 1) % (heads * QB) == 0:
                        load(i + 1, u)
            with sp.Fori(0, units // 2 - 1) as i:
                body(i, True)
            body(units // 2 - 1, False)
            for k in range(2):
                sp.wait_ge(stored[k], 16 * (units // 2) * (NS // 2))

        @block.tensor
        def _(pe):
            pe.sem_inc(unit_free, 2)
            pe.wait_ge(consts_in, 48 if causal else 16)

            def scores(i, s):
                n, k = i * NS + s, s % 2
                u, h, qb = s // (heads * QB), s // QB % heads, s % QB
                if s % (heads * QB) == 0:
                    pe.wait_ge(loaded[u], (i + 1) * (16 * (heads + 2)))
                pe.wait_ge(p_ready, n + 1)
                w = nb[s] * P
                for lo in range(0, w, 512):
                    hi = min(w, lo + 512)
                    last_part = causal and hi == w
                    for c in range(kc):
                        last = pe.matmul(SC[k][:, lo:hi], qt[:, u, h, c, qb * P:(qb + 1) * P], kt[:, u, c, lo:hi],
                                         start=(c == 0), stop=(c == kc - 1 and not last_part))
                    if last_part:
                        last = pe.matmul(SC[k][:, w - P:w], identb[:], mask[:], start=False, stop=True)
                last.then_inc(s_ready, 1)

            def transposes(i, s):
                n, k = i * NS + s, s % 2
                pe.wait_ge(p_ready, n + 1 + 2)
                for g in range(ng[s]):
                    m = gbase[s] + g
                    if m % 2 == 0:
                        pe.wait_ge(a_copied, i * A + m // 2 + 1)
                    else:
                        pe.wait_ge(d_copied, i * DC + m // 2 + 1)
                    for b in range(g * 4, min(nb[s], g * 4 + 4)):
                        last = pe.transpose(T[m % 2][:, b % 4 * P:(b % 4 + 1) * P], prob[:, k, b * P:(b + 1) * P], ident[:])
                    last.then_inc(t_ready, 1)

            def values(i, s):
                n, k = i * NS + s, s % 2
                u = s // (heads * QB)
                pe.wait_ge(a_copied, i * A + acount[s + 1] + 1)
                pe.wait_ge(d_copied, i * DC + dcount[s + 1] + 1)
                pe.wait_ge(o_used, n + 1)
                for b in range(nb[s]):
                    last = pe.matmul(O[k][:], pT[:, k, b, :], vt[:, u, b, :], start=(b == 0), stop=(b == nb[s] - 1))
                last.then_inc(o_ready, 1)
                if (s + 1) % (heads * QB) == 0:
                    pe.wait_ge(o_ready, n + 1 + 2)
                    pe.sem_inc(unit_free, 1)

            def ahead(part, i, s, more):
                if s < NS:
                    part(i, s)
                elif more:
                    part(i + 1, s - NS)

            def body(i, more):
                for s in range(NS):
                    ahead(scores, i, s + 2, more)
                    ahead(transposes, i, s + 1, more)
                    values(i, s)
            pe.sem_inc(o_ready, 2)
            pe.sem_inc(t_ready, TC)
            scores(0, 0)
            scores(0, 1)
            transposes(0, 0)
            with pe.Fori(0, units // 2 - 1) as i:
                body(i, True)
            body(units // 2 - 1, False)

        @block.scalar
        def _(act):
            act.sem_inc(p_ready, 2)
            act.sem_inc(a_copied, 1)

            def exps(i, s):
                n, k = i * NS + s, s % 2
                act.wait_ge(m_ready, n + 1)
                act.wait_ge(t_ready, i * (A + DC) + (gbase[s - 1] + TC if s else 0))
                act.activation(prob[:, k, 0:nb[s] * P], SC[k][:, 0:nb[s] * P], ACT.Exp, bias=nmax[:, k:k + 1],
                               accum_out=rsum[:, s % 4:s % 4 + 1]).then_inc(p_ready, 1)

            def copies(i, s):
                act.wait_ge(o_ready, i * NS + s + 1)
                for g in range(ng[s]):
                    m = gbase[s] + g
                    if m % 2 == 0:
                        lo, hi = g * 4, min(nb[s], g * 4 + 4)
                        act.wait_ge(t_ready, i * (A + DC) + m + 1 + TC)
                        act.copy(pT[:, s % 2, lo:hi, :].rearrange("p b q -> p (b q)"), T[0][:, 0:(hi - lo) * P]).then_inc(a_copied, 1)

            def ahead(part, i, s, more):
                if s < NS:
                    part(i, s)
                elif more:
                    part(i + 1, s - NS)

            def body(i, more):
                for s in range(NS):
                    ahead(exps, i, s + 2, more)
                    ahead(copies, i, s + 1, more)
            exps(0, 0)
            exps(0, 1)
            copies(0, 0)
            with act.Fori(0, units // 2 - 1) as i:
                body(i, True)
            body(units // 2 - 1, False)

        @block.vector
        def _(dve):
            dve.sem_inc(o_used, 2)
            dve.sem_inc(d_copied, 1)

            def maxima(i, s):
                n, k = i * NS + s, s % 2
                dve.wait_ge(s_ready, n + 1)
                dve.tensor_reduce(nmax[:, k:k + 1], SC[k][:, 0:nb[s] * P], AX, ALU.max, negate=True).then_inc(m_ready, 1)

            def copies(i, s):
                dve.wait_ge(o_ready, i * NS + s + 1)
                for g in range(ng[s]):
                    m = gbase[s] + g
                    if m % 2 == 1:
                        lo, hi = g * 4, min(nb[s], g * 4 + 4)
                        dve.wait_ge(t_ready, i * (A + DC) + m + 1 + TC)
                        dve.tensor_copy(pT[:, s % 2, lo:hi, :].rearrange("p b q -> p (b q)"), T[1][:, 0:(hi - lo) * P]).then_inc(d_copied, 1)

            def normalise(i, s):
                n, k = i * NS + s, s % 2
                dve.wait_ge(o_ready, n + 1 + 2)
                dve.reciprocal(rinv[:, k:k + 1], rsum[:, s % 4:s % 4 + 1]).then_inc(dve_self, 1)
                dve.wait_ge(dve_self, n + 1)
                dve.wait_ge(stored[k], i * (16 * (NS // 2)) + s // 2 * 16)
                dve.tensor_scalar(ot[:, k], O[k][:], rinv[:, k:k + 1], None, ALU.mult).then_inc(o_used, 1)

            def ahead(part, i, s, more):
                if s < NS:
                    part(i, s)
                elif more:
                    part(i + 1, s - NS)

            def body(i, more):
                for s in range(NS):
                    ahead(maxima, i, s + 2, more)
                    ahead(copies, i, s + 1, more)
                    normalise(i, s)
            maxima(0, 0)
            maxima(0, 1)
            copies(0, 0)
            with dve.Fori(0, units // 2 - 1) as i:
                body(i, True)
            body(units // 2 - 1, False)


PART_PAIRS = [(0, 0), (0, 1), (0, 2), (1, 0), (1, 1), (2, 0)]
HG, DH = 4, 16
KR = len(PART_PAIRS) * DH
NR = 3
PIECES_AT = [8, 8, 8, 8, 8, 8, 0, 0]


def narrow_attention_stage(nc, name, consts, q_parts, k_parts, v, out, m_rows, units):
    st = Stage(nc, name)
    with st.ctx:
        NU = 4
        qs = st.sb("qs", [P, NU, HG, S], BF16)
        ks = st.sb("ks", [P, NU, HG, S], BF16)
        vin = st.sb("vin", [P, 2, QB, HG * DH])
        vp = st.sb("vp", [P, 2, QB, HG, 32])
        pT = st.sb("pT", [P, 2, HG, S])
        ident = st.sb("ident", [P, P])
        identb = st.sb("identb", [P, P], BF16)
        mask = st.sb("mask", [P, P], BF16)
        maskT = st.sb("maskT", [P, P], BF16)
        pm = st.sb("pm", [P, HG, QB, 2])
        nm = st.sb("nm", [P, HG, QB])
        nr = st.sb("nr", [P, HG, QB])
        nb3 = st.sb("nb3", [P, HG, 3, QB], BF16)
        mt = st.sb("mt", [HG * 3 * QB, P], BF16)
        osb = st.sb("osb", [P, 2, 512])
        rinv = st.sb("rinv", [P, 4, HG, 1])
        on = st.sb("on", [P, 2, 4, HG, DH])
        SC = [st.ps(f"SC{k}") for k in range(3)]
        ST = [st.ps(f"ST{k}") for k in range(3)]
        OT = st.ps("OT", (P, S))
        consts_in = st.sem("consts_in")
        qk_loaded = [st.sem(f"qk_loaded{u}") for u in range(NU)]
        v_loaded = [st.sem(f"v_loaded{u}") for u in range(2)]
        m_stored = st.sem("m_stored")
        m_loaded = [st.sem(f"m_loaded{u}") for u in range(2)]
        unit_free = st.sem("unit_free")
        ones_set = st.sem("ones_set")
        vp_ready = st.sem("vp_ready")
        v_seen = st.sem("v_seen")
        sc_ready = st.sem("sc_ready")
        sc_used = st.sem("sc_used")
        parts_ready = st.sem("parts_ready")
        mt_ready = st.sem("mt_ready")
        st_ready = st.sem("st_ready")
        e_ready = st.sem("e_ready")
        av_ready = st.sem("av_ready")
        ot_copied = st.sem("ot_copied")
        on_ready = st.sem("on_ready")
        stored = [st.sem(f"stored{k}") for k in range(2)]
        dve_self = st.sem("dve_self")
        pieces = [(qb, lo, j) for qb in range(QB) for lo in range(0, (qb + 1) * P, 512) for j in range(HG)]
        NP = len(pieces)
        PU = NP + 3
        steps = [(kb, j, lo, min(S - kb * P, lo + 512)) for kb in range(QB) for j in range(HG) for lo in range(0, S - kb * P, 512)]
        NT = len(steps)
        done = [sum(1 for t in steps if t[0] < kb) for kb in range(QB + 1)]
        assert sum(PIECES_AT) == NP and NT % len(ST) == 0 and PU % len(SC) == 0

        def seq(i, u):
            return SeqNumber(i * (NU * PU) + (NP + 1 + u * PU), NP + 1 + u * PU, len(SC))

        def bank_of(q):
            return SC[q.rest] if isinstance(q, SeqNumber) else SC[q % len(SC)]
        block = st.ctx.enter_context(nc.Block())

        @block.sync
        def _(sp):
            for t, key in ((ident, "ident"), (identb, "identb"), (mask, "mask"), (maskT, "maskT")):
                sp.dma_start(t[:], consts[key]).then_inc(consts_in, 16)

            def load_qk(i, u):
                n = i * NU + u
                sp.wait_ge(unit_free, n + 1)
                for r, (a, b) in enumerate(PART_PAIRS):
                    for dst, src, part in ((qs, q_parts, a), (ks, k_parts, b)):
                        sp.dma_start(dst[r * DH:(r + 1) * DH, u], src[part, bass.ds(n * (HG * DH), HG * DH), :].rearrange("(j r) t -> r j t", r=DH))\
                          .then_inc(qk_loaded[u], 16)

            def load_v(i, u):
                n = i * NU + u
                sp.wait_ge(vp_ready, n + 1)
                sp.dma_start(vin[:, u % 2], one(v, i)[:, :, u * HG * DH:(u + 1) * HG * DH].rearrange("a (b p) n -> p (a b) n", p=P)).then_inc(v_loaded[u % 2], 16)

            def store(i, u, h):
                n2 = (i * NU + u) * 2 + h
                sp.wait_ge(on_ready, n2 + 1)
                sp.dma_start(one(out, i)[:, h * 512:(h + 1) * 512, u * HG * DH:(u + 1) * HG * DH].rearrange("a (b p) n -> p (a b) n", p=P),
                             on[:, h].rearrange("p b j e -> p b (j e)")).then_inc(stored[h], 16)

            def maxima_rows(i, u):
                n = i * NU + u
                sp.wait_ge(mt_ready, n + 1)
                sp.dma_start(one(m_rows, n).rearrange("a j r (b t) -> (a j r b) t", t=P), mt[:]).then_inc(m_stored, 16)
                sp.wait_ge(m_stored, (n + 1) * 16)
                sp.dma_start(qs[KR:KR + NR, u], one(m_rows, n).rearrange("a j r t -> r (a j) t")).then_inc(m_loaded[u % 2], 16)

            def body(i, more):
                for u in range(NU):
                    if u + 1 < NU:
                        maxima_rows(i, u + 1)
                    elif more:
                        maxima_rows(i + 1, 0)
                    for h in range(2):
                        store(i, u, h)
                    if more:
                        load_qk(i + 1, u)
                    if u + 2 < NU:
                        load_v(i, u + 2)
                    elif more:
                        load_v(i + 1, u + 2 - NU)
            for u in range(2):
                load_qk(0, u)
                load_v(0, u)
            for u in range(2, NU):
                load_qk(0, u)
            maxima_rows(0, 0)
            with sp.Fori(0, units // NU - 1) as i:
                body(i, True)
            body(units // NU - 1, False)
            for h in range(2):
                sp.wait_ge(stored[h], 16 * units)

        @block.gpsimd
        def _(pool):
            pool.memset(ks[KR:P], 1.0).then_inc(ones_set, 1)
            pool.wait_ge(ones_set, 1)
            pool.memset(vp[:, :, :, :, DH + 1:32], 0.0).then_inc(ones_set, 1)
            pool.wait_ge(ones_set, 2)
            pool.memset(vp[:, :, :, :, DH:DH + 1], 1.0).then_inc(ones_set, 1)
            pool.wait_ge(ones_set, 3)
            pool.sem_inc(vp_ready, 2)
            pool.sem_inc(unit_free, NU)
            with pool.Fori(0, units // 2) as i:
                for u in range(2):
                    n = i * 2 + u
                    pool.wait_ge(v_loaded[u], (i + 1) * 16)
                    pool.wait_ge(unit_free, n - 2 + 1 + NU)
                    pool.sem_inc(v_seen, 1)
                    pool.tensor_copy(vp[:, u, :, :, 0:DH], vin[:, u].rearrange("p b (j e) -> p b j e", j=HG)).then_inc(vp_ready, 1)

        @block.tensor
        def _(pe):
            pe.sem_inc(av_ready, 2)
            pe.wait_ge(consts_in, 64)
            pe.wait_ge(ones_set, 3)

            def piece(i, u, p, q):
                qb, lo, j = pieces[p]
                if p == 0:
                    pe.wait_ge(qk_loaded[u], (i + 1) * (16 * 2 * len(PART_PAIRS)))
                pe.wait_ge(sc_used, count(q + 1))
                bank = bank_of(q)
                hi = min((qb + 1) * P, lo + 512)
                diag = hi == (qb + 1) * P
                last = pe.matmul(bank[:, 0:hi - lo], qs[0:KR, u, j, qb * P:(qb + 1) * P], ks[0:KR, u, j, lo:hi],
                                 start=True, stop=not diag)
                if diag:
                    last = pe.matmul(bank[:, hi - lo - P:hi - lo], identb[:], mask[:], start=False, stop=True)
                last.then_inc(sc_ready, 1)

            def maxima_transpose(unit, q):
                pe.wait_ge(parts_ready, unit + 1)
                pe.wait_ge(sc_used, count(q + 1))
                bank = bank_of(q)[0:HG * NR * QB, 0:P // 2].bitcast(BF16)
                pe.transpose(bank, nb3[:].rearrange("p j r b -> p (j r b)"), identb[:]).then_inc(sc_ready, 1)

            def out_transpose(n, h, q):
                pe.wait_ge(ot_copied, n * 2 + h + 1)
                pe.wait_ge(sc_used, count(q + 1))
                for b in range(4):
                    last = pe.transpose(bank_of(q)[:, b * P:(b + 1) * P], osb[:, h, b * P:(b + 1) * P], ident[:])
                last.then_inc(sc_ready, 1)

            def step(n, u, t):
                kb, j, lo, hi = steps[t]
                pe.wait_ge(e_ready, n * NT + t + 1)
                bank = ST[t % len(ST)]
                last = pe.matmul(bank[:, 0:hi - lo], ks[0:KR + NR, u, j, kb * P:(kb + 1) * P],
                                 qs[0:KR + NR, u, j, kb * P + lo:kb * P + hi], start=True, stop=lo > 0)
                if lo == 0:
                    last = pe.matmul(bank[:, 0:P], identb[:], maskT[:], start=False, stop=True)
                last.then_inc(st_ready, 1)

            def values(i, u, kb):
                n = i * NU + u
                pe.wait_ge(e_ready, n * NT + done[kb + 1] + len(ST))
                if kb == 0:
                    pe.wait_ge(vp_ready, n + 1 + 2)
                    pe.wait_ge(ot_copied, n * 2)
                for h in range(2):
                    lo, hi = max(kb * P, h * 512), (h + 1) * 512
                    if lo < hi:
                        for j in range(HG):
                            last = pe.matmul(OT[32 * j:32 * j + 32, lo:hi], vp[:, u % 2, kb, j, :],
                                             pT[:, kb % 2, j, lo - kb * P:hi - kb * P],
                                             start=(kb == 0), stop=(kb == 4 * h + 3))
                last.then_inc(av_ready, 1)

            def unit(i, u, ahead):
                n = i * NU + u
                q, p = seq(i, u), 0
                for kb in range(QB):
                    for t in range(done[kb], done[kb + 1]):
                        while ahead and p < sum(PIECES_AT[:kb]) + PIECES_AT[kb] * (t + 1 - done[kb]) // (done[kb + 1] - done[kb]):
                            piece(*ahead, p, q)
                            p, q = p + 1, q + 1
                        if t == 0:
                            pe.wait_ge(m_loaded[u % 2], (i * (NU // 2) + u // 2 + 1) * 16)
                        step(n, u, t)
                    if kb == 6 and ahead:
                        maxima_transpose(n + 1, q)
                        q = q + 1
                    if kb == 7:
                        out_transpose(n, 0, q)
                        q = q + 1
                    if kb:
                        values(i, u, kb - 1)
                values(i, u, QB - 1)
                out_transpose(n, 1, q)
                pe.wait_ge(av_ready, (n + 1) * QB + 2)
                pe.sem_inc(unit_free, 1)

            for p in range(NP):
                piece(0, 0, p, p)
            maxima_transpose(0, NP)

            def body(i, more):
                for u in range(NU):
                    unit(i, u, (i, u + 1) if u + 1 < NU else (i + 1, 0) if more else None)
            with pe.Fori(0, units // NU - 1) as i:
                body(i, True)
            body(units // NU - 1, False)

        @block.scalar
        def _(act):
            act.sem_inc(e_ready, len(ST))

            def unit(i, u):
                n = i * NU + u
                for kb in range(QB):
                    act.wait_ge(av_ready, n * QB + kb + 1)
                    for t in range(done[kb], done[kb + 1]):
                        _, j, lo, hi = steps[t]
                        act.wait_ge(st_ready, n * NT + t + 1)
                        act.activation(pT[:, kb % 2, j, lo:hi], ST[t % len(ST)][:, 0:hi - lo], ACT.Exp).then_inc(e_ready, 1)
                    if kb == 5:
                        copy(n, 0)
                copy(n, 1)

            def copy(n, h):
                act.wait_ge(av_ready, n * QB + 4 * (h + 1) + 2)
                act.wait_ge(sc_ready, n * PU + NP + h)
                act.copy(osb[:, h], OT[:, h * 512:(h + 1) * 512]).then_inc(ot_copied, 1)

            with act.Fori(0, units // NU) as i:
                for u in range(NU):
                    unit(i, u)

        @block.vector
        def _(dve):
            dve.memset(pm[:], NEG).then_inc(dve_self, 1)
            dve.wait_ge(dve_self, 1)
            dve.sem_inc(sc_used, len(SC))

            def piece_max(p, q):
                qb, lo, j = pieces[p]
                hi = min((qb + 1) * P, lo + 512)
                dve.wait_ge(sc_ready, count(q + 1))
                dve.tensor_reduce(pm[:, j, qb, lo // 512:lo // 512 + 1], bank_of(q)[:, 0:hi - lo], AX, ALU.max).then_inc(sc_used, 1)

            def maxima(unit, q, link):
                dve.wait_ge(sc_used, count(q + 1) + len(SC))
                link(dve.tensor_reduce(nm[:], pm[:], AX, ALU.max, negate=True))
                link(dve.tensor_copy(nb3[:, :, 0, :], nm[:]))
                link(dve.tensor_tensor(nr[:], nm[:], nb3[:, :, 0, :], ALU.subtract))
                link(dve.tensor_copy(nb3[:, :, 1, :], nr[:]))
                dve.tensor_tensor(nb3[:, :, 2, :], nr[:], nb3[:, :, 1, :], ALU.subtract).then_inc(parts_ready, 1)

            def maxima_copy(unit, q):
                dve.wait_ge(sc_ready, count(q + 1))
                dve.wait_ge(m_stored, unit * 16)
                dve.tensor_copy(mt[:], bank_of(q)[0:HG * NR * QB, 0:P // 2].bitcast(BF16)).then_inc(mt_ready, 1)
                dve.wait_ge(mt_ready, unit + 1)
                dve.sem_inc(sc_used, 1)

            def normalise(n, h, q, link):
                dve.wait_ge(sc_ready, count(q + 1))
                o = bank_of(q)[:].rearrange("p (b j e) -> p b j e", b=4, j=HG)
                link(dve.reciprocal(rinv[:], o[:, :, :, DH:DH + 1]))
                dve.wait_ge(stored[h], n * 16)
                dve.tensor_tensor(on[:, h], o[:, :, :, 0:DH], rinv[:].broadcast_to([P, 4, HG, DH]), ALU.mult).then_inc(on_ready, 1)
                dve.wait_ge(on_ready, n * 2 + h + 1)
                dve.sem_inc(sc_used, 1)

            link = Chain(dve, dve_self, 1)
            for p in range(NP):
                piece_max(p, p)
            maxima(0, NP - 1, link)
            maxima_copy(0, NP)

            def body(i, more):
                for u in range(NU):
                    n = i * NU + u
                    q = seq(i, u)
                    link = Chain(dve, dve_self, n * 6 + 5)
                    if u + 1 < NU or more:
                        for p in range(NP):
                            piece_max(p, q + p)
                        maxima(n + 1, q + (NP - 1), link)
                        maxima_copy(n + 1, q + NP)
                        q = q + NP + 1
                    for h in range(2):
                        normalise(n, h, q + h, link)
            with dve.Fori(0, units // NU - 1) as i:
                body(i, True)
            body(units // NU - 1, False)


HID = 768
DEQUANT = float(np.float32(1.0 / 127.0))


def swiglu_stage(nc, name, xnT, w_gate, w_up, w_down, g_out):
    st = Stage(nc, name)
    with st.ctx:
        M = HID // P
        xT = st.sb("xT", [P, 2, KC, CH])
        wgi = st.sb("wgi", [P, KC, HID], I32)
        wui = st.sb("wui", [P, KC, HID], I32)
        wdi = st.sb("wdi", [P, M, D], I32)
        wg = st.sb("wg", [P, KC, HID])
        wu = st.sb("wu", [P, KC, HID])
        wd = st.sb("wd", [P, M, D])
        sg = st.sb("sg", [P, 2, CH])
        hT = st.sb("hT", [P, 2, M, CH])
        go = st.sb("go", [P, 2, TT, D])
        G = [st.ps(f"G{k}") for k in range(2)]
        U = [st.ps(f"U{k}") for k in range(2)]
        DN = [st.ps(f"D{k}") for k in range(2)]
        w_in = st.sem("w_in")
        w_ready = st.sem("w_ready")
        x_in = [st.sem(f"x_in{u}") for u in range(2)]
        x_free = st.sem("x_free")
        gu_ready = st.sem("gu_ready")
        sg_ready = st.sem("sg_ready")
        h_ready = st.sem("h_ready")
        dn_ready = st.sem("dn_ready")
        go_ready = st.sem("go_ready")
        stored = [st.sem(f"stored{u}") for u in range(2)]
        block = st.ctx.enter_context(nc.Block())

        @block.sync
        def _(sp):
            for dst, src in ((wgi, w_gate), (wui, w_up), (wdi, w_down)):
                sp.dma_start(dst[:], src.rearrange("(c p) n -> p c n", p=P)).then_inc(w_in, 16)
            for u in range(2):
                sp.dma_start(xT[:, u], xnT[:, :, u * CH:(u + 1) * CH]).then_inc(x_in[u], 16)

            def body(i, more):
                for u in range(2):
                    if more:
                        sp.wait_ge(x_free, i * 2 + u + 1)
                        sp.dma_start(xT[:, u], xnT[:, :, bass.ds(((i + 1) * 2 + u) * CH, CH)]).then_inc(x_in[u], 16)
                for u in range(2):
                    sp.wait_ge(go_ready, (i * 2 + u + 1) * 2 + 2)
                    sp.dma_start(one(g_out, i * 2 + u).rearrange("c p t d -> p (c t) d"), go[:, u]).then_inc(stored[u], 16)
            with sp.Fori(0, B - 1) as i:
                body(i, True)
            body(B - 1, False)
            for u in range(2):
                sp.wait_ge(stored[u], 16 * B)

        @block.tensor
        def _(pe):
            pe.wait_ge(w_ready, 3)
            with pe.Fori(0, B) as i:
                for u in range(2):
                    n = i * 2 + u
                    pe.wait_ge(x_in[u], (i + 1) * 16)
                    for m in range(M):
                        pe.wait_ge(h_ready, n * M + m + 1)
                        for bank, w in ((G, wg), (U, wu)):
                            for c in range(KC):
                                last = pe.matmul(bank[m % 2][:], w[:, c, m * P:(m + 1) * P], xT[:, u, c, :],
                                                 start=(c == 0), stop=(c == KC - 1))
                        last.then_inc(gu_ready, 1)
                    pe.wait_ge(gu_ready, (n + 1) * M)
                    pe.sem_inc(x_free, 1)
                for u in range(2):
                    n = i * 2 + u
                    pe.wait_ge(h_ready, (n + 1) * M + 2)
                    for k in range(2):
                        pe.wait_ge(go_ready, n * 2 + k + 1)
                        for t in (2 * k, 2 * k + 1):
                            for m in range(M):
                                last = pe.matmul(DN[k][:, t % 2 * D:(t % 2 + 1) * D], hT[:, u, m, t * P:(t + 1) * P], wd[:, m, :],
                                                 start=(m == 0), stop=(m == M - 1))
                        last.then_inc(dn_ready, 1)

        @block.scalar
        def _(act):
            act.sem_inc(go_ready, 2)
            with act.Fori(0, B) as i:
                for u in range(2):
                    n = i * 2 + u
                    for m in range(M):
                        act.wait_ge(gu_ready, n * M + m + 1)
                        act.wait_ge(h_ready, n * M + m + 1)
                        act.activation(sg[:, m % 2], G[m % 2][:], ACT.Silu).then_inc(sg_ready, 1)
                for u in range(2):
                    n = i * 2 + u
                    act.wait_ge(stored[u], i * 16)
                    for k in range(2):
                        act.wait_ge(dn_ready, n * 2 + k + 1)
                        act.activation(go[:, u, 2 * k:2 * k + 2, :].rearrange("p t d -> p (t d)"), DN[k][:], ACT.Silu).then_inc(go_ready, 1)

        @block.vector
        def _(dve):
            dve.wait_ge(w_in, 48)
            for dst, src in ((wg, wgi), (wu, wui), (wd, wdi)):
                dve.tensor_scalar(dst[:], src[:], DEQUANT, None, ALU.mult).then_inc(w_ready, 1)
            dve.sem_inc(h_ready, 2)
            with dve.Fori(0, B) as i:
                for u in range(2):
                    n = i * 2 + u
                    dve.wait_ge(dn_ready, i * 4)
                    for m in range(M):
                        dve.wait_ge(sg_ready, n * M + m + 1)
                        dve.tensor_tensor(hT[:, u, m, :], U[m % 2][:], sg[:, m % 2], ALU.mult).then_inc(h_ready, 1)


SE, SS, SH = 16, 16, 64
ES = SE * SS
EC = ES // P


def soft_slots_stage(nc, name, consts, xn, gamma, beta, mu, scale, slots, combT, comb_rinv):
    st = Stage(nc, name)
    with st.ctx:
        ident = st.sb("ident", [P, P])
        ones = st.sb("ones", [P, P])
        gm = st.sb("gamma", [P, 1, D])
        bt = st.sb("beta", [P, 1, D])
        sc = st.sb("scale", [P, 1])
        mur = st.sb("mu", [P, KC, ES])
        musq = st.sb("musq", [P, KC, ES])
        mun = st.sb("mun", [P, 1, ES])
        x = st.sb("x", [P, 2, QB, D])
        x2 = st.sb("x2", [P, QB, D])
        sq = st.sb("sq", [P, QB, D])
        stats = st.sb("stats", [P, QB, 6])
        mv = st.sb("mv", [P, QB, 2])
        vep = st.sb("vep", [P, QB])
        std = st.sb("std", [P, QB])
        rstd = st.sb("rstd", [P, QB])
        ssq = st.sb("ssq", [P, QB])
        norm = st.sb("norm", [P, QB])
        rnorm = st.sb("rnorm", [P, QB])
        x2T = st.sb("x2T", [P, KC, S])
        L = st.sb("L", [P, QB, ES])
        C = st.sb("C", [P, QB, ES])
        LT = st.sb("LT", [P, EC, S])
        DW = st.sb("DW", [P, QB, ES])
        CT = st.sb("CT", [P, EC, S])
        cmax = st.sb("cmax", [P, QB])
        csum = st.sb("csum", [P, QB])
        crin = st.sb("crin", [P, QB])
        dmax = st.sb("dmax", [P, EC])
        dsum = st.sb("dsum", [P, EC])
        drin = st.sb("drin", [P, EC])
        slot = st.sb("slot", [P, EC, D])
        W = [st.ps(f"W{k}") for k in range(4)]
        stats_seen = st.sem("stats_seen")
        c_in = st.sem("c_in")
        x_in = [st.sem(f"x_in{u}") for u in range(2)]
        x_used = st.sem("x_used")
        bank_ready = st.sem("bank_ready")
        bank_read = st.sem("bank_read")
        musq_ready = st.sem("musq_ready")
        mun_ready = st.sem("mun_ready")
        munit_ready = st.sem("munit_ready")
        var_ready = st.sem("var_ready")
        std_ready = st.sem("std_ready")
        x2_ready = st.sem("x2_ready")
        ssq_ready = st.sem("ssq_ready")
        norm_ready = st.sem("norm_ready")
        logits_ready = st.sem("logits_ready")
        comb_ready = st.sem("comb_ready")
        lt_ready = st.sem("lt_ready")
        disp_ready = st.sem("disp_ready")
        ct_ready = st.sem("ct_ready")
        slot_ready = st.sem("slot_ready")
        stored = st.sem("stored")
        dve_self = st.sem("dve_self")
        NB = 22
        block = st.ctx.enter_context(nc.Block())

        @block.sync
        def _(sp):
            for dst, src in ((ident[:], consts["ident"]), (ones[:], consts["ones"]), (gm[:, 0], gamma), (bt[:, 0], beta),
                             (sc[:], scale), (mur[:], mu.rearrange("(c p) n -> p c n", p=P))):
                sp.dma_start(dst, src).then_inc(c_in, 16)

            def load(i, u):
                for h in range(2):
                    sp.dma_start(x[:, u, h * TT:(h + 1) * TT, :], one(xn, (i * 2 + u) * 2 + h).rearrange("c p t d -> p (c t) d"))\
                      .then_inc(x_in[u], 16)

            def body(i, more):
                for u in range(2):
                    b = i * 2 + u
                    if more:
                        sp.wait_ge(x_used, b + 1)
                        load(i + 1, u)
                    sp.wait_ge(ct_ready, b + 1)
                    sp.dma_start(one(combT, b).rearrange("b p e t -> p (b e) t"), CT[:]).then_inc(stored, 16)
                    sp.dma_start(one(comb_rinv, b).rearrange("b p t -> (b p) t"), crin[:]).then_inc(stored, 16)
                    sp.wait_ge(slot_ready, (b + 1) * EC)
                    sp.dma_start(one(slots, b).rearrange("b (e p) d -> p (b e) d", p=P), slot[:]).then_inc(stored, 16)
            load(0, 0)
            load(0, 1)
            with sp.Fori(0, B // 2 - 1) as i:
                body(i, True)
            body(B // 2 - 1, False)
            sp.wait_ge(stored, 48 * B)

        @block.tensor
        def _(pe):
            pe.wait_ge(c_in, 96)
            pe.wait_ge(musq_ready, 1)
            for c in range(KC):
                last = pe.matmul(W[0][:, 0:ES], ones[:], musq[:, c, :], start=(c == 0), stop=(c == KC - 1))
            last.then_inc(bank_ready, 1)
            pe.wait_ge(munit_ready, 1)

            def batch(i, u):
                b = i * 2 + u
                k = [0]

                def bank():
                    k[0] += 1
                    pe.wait_ge(bank_read, b * NB + k[0] + 1)
                    return W[(u * NB + k[0]) % 4]

                def transposed(src, e):
                    for h in range(2):
                        w = bank()
                        for t in range(4):
                            last = pe.transpose(w[:, t * P:(t + 1) * P], src[:, h * 4 + t, e * P:(e + 1) * P], ident[:])
                        last.then_inc(bank_ready, 1)
                pe.wait_ge(x2_ready, b + 1)
                for c in range(KC):
                    transposed(x2, c)
                pe.wait_ge(bank_read, b * NB + 1 + 4 + 4)
                for t in range(0, QB, 2):
                    w = bank()
                    for h in range(2):
                        for c in range(KC):
                            last = pe.matmul(w[:, h * ES:(h + 1) * ES], x2T[:, c, (t + h) * P:(t + h + 1) * P], mur[:, c, :],
                                             start=(c == 0), stop=(c == KC - 1))
                    last.then_inc(bank_ready, 1)
                pe.wait_ge(bank_read, b * NB + 1 + 4 + 8)
                for e in range(EC):
                    transposed(L, e)
                pe.wait_ge(comb_ready, b + 1)
                for e in range(EC):
                    transposed(C, e)
                pe.wait_ge(disp_ready, b + 1)
                for t in range(0, QB, 2):
                    w = bank()
                    for h in range(2):
                        for e in range(EC):
                            last = pe.transpose(w[:, h * ES + e * P:h * ES + (e + 1) * P], LT[:, e, (t + h) * P:(t + h + 1) * P], ident[:])
                    last.then_inc(bank_ready, 1)
                pe.wait_ge(bank_read, b * NB + 1 + 4 + 20)
                for e in range(EC):
                    w = bank()
                    for t in range(QB):
                        last = pe.matmul(w[:, 0:D], DW[:, t, e * P:(e + 1) * P], x2[:, t, :], start=(t == 0), stop=(t == QB - 1))
                    last.then_inc(bank_ready, 1)
                assert k[0] == NB
            with pe.Fori(0, B // 2) as i:
                for u in range(2):
                    batch(i, u)

        @block.scalar
        def _(act):
            act.wait_ge(bank_ready, 1)
            act.activation(mun[:, 0], W[0][:, 0:ES], ACT.Sqrt).then_inc(mun_ready, 1)
            with act.Fori(0, B) as b:
                act.wait_ge(var_ready, b + 1)
                act.activation(std[:], vep[:], ACT.Sqrt).then_inc(std_ready, 1)
                act.wait_ge(x2_ready, b + 1)
                for t in range(QB):
                    last = act.activation(sq[:, t, :], x2[:, t, :], ACT.Square, accum_out=ssq[:, t:t + 1])
                last.then_inc(ssq_ready, 1)
                act.wait_ge(ssq_ready, b + 1)
                act.activation(norm[:], ssq[:], ACT.Sqrt).then_inc(norm_ready, 1)
                act.wait_ge(logits_ready, b + 1)
                for t in range(QB):
                    last = act.activation(C[:, t, :], L[:, t, :], ACT.Exp, bias=cmax[:, t:t + 1], accum_out=csum[:, t:t + 1])
                last.then_inc(comb_ready, 1)
                act.wait_ge(lt_ready, b + 1)
                for e in range(EC):
                    last = act.activation(LT[:, e, :], LT[:, e, :], ACT.Exp, bias=dmax[:, e:e + 1], accum_out=dsum[:, e:e + 1])
                last.then_inc(disp_ready, 1)

        @block.vector
        def _(dve):
            dve.wait_ge(c_in, 96)
            dve.tensor_tensor(musq[:], mur[:], mur[:], ALU.mult).then_inc(musq_ready, 1)
            dve.wait_ge(mun_ready, 1)
            link = Chain(dve, dve_self)
            link(dve.tensor_scalar(mun[:], mun[:], 1e-12, None, ALU.max))
            link(dve.reciprocal(mun[:], mun[:]))
            dve.tensor_tensor(mur[:], mur[:], mun[:].broadcast_to([P, KC, ES]), ALU.mult).then_inc(munit_ready, 1)
            dve.sem_inc(bank_read, 1 + 4)
            LINKS = 9

            def batch(i, u):
                b = i * 2 + u
                link = Chain(dve, dve_self, b * LINKS + 2)
                k = [0]

                def bank():
                    k[0] += 1
                    dve.wait_ge(bank_ready, b * NB + 1 + k[0])
                    return W[(u * NB + k[0]) % 4]
                dve.wait_ge(x_in[u], (i + 1) * 32)
                for t in range(QB):
                    last = dve.bn_stats(stats[:, t, :], x[:, u, t, :])
                link(last)
                dve.sem_inc(stats_seen, 1)
                for t in range(QB):
                    last = dve.bn_aggr(mv[:, t, :], stats[:, t, :])
                link(last)
                dve.tensor_scalar(vep[:], mv[:, :, 1], 1e-5, None, ALU.add).then_inc(var_ready, 1)
                dve.wait_ge(std_ready, b + 1)
                link(dve.reciprocal(rstd[:], std[:]))
                for t in range(QB):
                    last = dve.tensor_scalar(x2[:, t, :], x[:, u, t, :], mv[:, t, 0:1], rstd[:, t:t + 1], ALU.subtract, ALU.mult)
                last.then_inc(x_used, 1)
                dve.wait_ge(x_used, b + 1)
                link(dve.tensor_tensor(x2[:], x2[:], gm[:].broadcast_to([P, QB, D]), ALU.mult))
                dve.tensor_tensor(x2[:], x2[:], bt[:].broadcast_to([P, QB, D]), ALU.add).then_inc(x2_ready, 1)
                for c in range(KC):
                    for h in range(2):
                        dve.tensor_copy(x2T[:, c, h * CH:(h + 1) * CH], bank()[:]).then_inc(bank_read, 1)
                dve.wait_ge(norm_ready, b + 1)
                link(dve.tensor_scalar(norm[:], norm[:], 1e-12, None, ALU.max))
                link(dve.reciprocal(rnorm[:], norm[:]))
                link(dve.tensor_scalar(rnorm[:], rnorm[:], sc[:], None, ALU.mult))
                for t in range(0, QB, 2):
                    w = bank()
                    for h in range(2):
                        last = dve.tensor_scalar(L[:, t + h, :], w[:, h * ES:(h + 1) * ES], rnorm[:, t + h:t + h + 1], None, ALU.mult)
                    last.then_inc(bank_read, 1)
                dve.wait_ge(bank_read, b * NB + 1 + 4 + 8)
                dve.tensor_reduce(cmax[:], L[:], AX, ALU.max, negate=True).then_inc(logits_ready, 1)
                for e in range(EC):
                    for h in range(2):
                        dve.tensor_copy(LT[:, e, h * CH:(h + 1) * CH], bank()[:]).then_inc(bank_read, 1)
                dve.wait_ge(bank_read, b * NB + 1 + 4 + 12)
                dve.tensor_reduce(dmax[:], LT[:], AX, ALU.max, negate=True).then_inc(lt_ready, 1)
                dve.wait_ge(stored, b * 48)
                for e in range(EC):
                    for h in range(2):
                        dve.tensor_copy(CT[:, e, h * CH:(h + 1) * CH], bank()[:]).then_inc(bank_read, 1)
                link(dve.reciprocal(crin[:], csum[:]))
                dve.sem_inc(ct_ready, 1)
                for t in range(0, QB, 2):
                    dve.tensor_copy(DW[:, t:t + 2, :].rearrange("p t e -> p (t e)"), bank()[:]).then_inc(bank_read, 1)
                link(dve.reciprocal(drin[:], dsum[:]))
                for e in range(EC):
                    w = bank()
                    dve.tensor_scalar(slot[:, e, :], w[:, 0:D], drin[:, e:e + 1], None, ALU.mult).then_inc(slot_ready, 1)
                    dve.wait_ge(slot_ready, b * EC + e + 1)
                    dve.sem_inc(bank_read, 1)
                assert link.n == LINKS
            with dve.Fori(0, B // 2) as i:
                for u in range(2):
                    batch(i, u)


def soft_experts_stage(nc, name, consts, slots, w1, b1, w2, b2, slot_out):
    st = Stage(nc, name)
    with st.ctx:
        R = B * SS
        GR = 4
        ident = st.sb("ident", [P, P])
        sl = st.sb("sl", [R, SE, D])
        w1t = st.sb("w1", [P, KC, SE, SH])
        b1t = st.sb("b1", [SH, SE])
        w2t = st.sb("w2", [SH, SE, D])
        b2t = st.sb("b2", [R, SE, D])
        slT = st.sb("slT", [P, GR * KC, R])
        hT = st.sb("hT", [SH, GR, R])
        so = st.sb("so", [R, SE, D])
        TP = st.ps("TP")
        HP = st.ps("HP")
        OP = [st.ps(f"OP{k}") for k in range(2)]
        loaded = st.sem("loaded")
        slT_ps = st.sem("slT_ps")
        slT_ready = st.sem("slT_ready")
        h_ps = st.sem("h_ps")
        h_ready = st.sem("h_ready")
        o_ps = st.sem("o_ps")
        o_ready = st.sem("o_ready")
        stored = st.sem("stored")
        block = st.ctx.enter_context(nc.Block())

        @block.sync
        def _(sp):
            sp.dma_start(ident[:], consts["ident"]).then_inc(loaded, 16)
            for b in range(B):
                sp.dma_start(sl[b * SS:(b + 1) * SS], slots[b].rearrange("(e s) d -> s e d", s=SS)).then_inc(loaded, 16)
            for c in range(KC):
                sp.dma_start(w1t[:, c], w1[:, c * P:(c + 1) * P, :].rearrange("e p h -> p e h")).then_inc(loaded, 16)
            sp.dma_start(b1t[:], b1).then_inc(loaded, 16)
            sp.dma_start(w2t[:], w2.rearrange("e h d -> h e d")).then_inc(loaded, 16)
            sp.dma_start(b2t[:], b2).then_inc(loaded, 16)
            sp.wait_ge(o_ready, SE // 2)
            for b in range(B):
                sp.dma_start(slot_out[b].rearrange("(e s) d -> s e d", s=SS), so[b * SS:(b + 1) * SS]).then_inc(stored, 16)
            sp.wait_ge(stored, 16 * B)

        @block.tensor
        def _(pe):
            pe.wait_ge(loaded, 160)
            for g in range(SE // GR):
                if g:
                    pe.wait_ge(slT_ready, g)
                for e in range(GR):
                    for c in range(KC):
                        m = e * KC + c
                        last = pe.transpose(TP[:, m * R:(m + 1) * R], sl[:, g * GR + e, c * P:(c + 1) * P], ident[0:R, 0:R])
                last.then_inc(slT_ps, 1)
                pe.wait_ge(slT_ready, g + 1)
                if g:
                    pe.wait_ge(h_ready, g * GR)
                for e in range(GR):
                    for c in range(KC):
                        last = pe.matmul(HP[0:SH, e * R:(e + 1) * R], w1t[:, c, g * GR + e, :], slT[:, e * KC + c, :],
                                         start=(c == 0), stop=(c == KC - 1))
                last.then_inc(h_ps, 1)
                pe.wait_ge(h_ready, (g + 1) * GR)
                for k in range(GR // 2):
                    if g:
                        pe.wait_ge(o_ready, (g - 1) * 2 + k + 1)
                    for h in range(2):
                        e = k * 2 + h
                        last = pe.matmul(OP[k][0:R, h * D:(h + 1) * D], hT[:, e, :], w2t[:, g * GR + e, :], start=True, stop=True)
                    last.then_inc(o_ps, 1)

        @block.scalar
        def _(act):
            act.wait_ge(loaded, 160)
            for g in range(SE // GR):
                act.wait_ge(h_ps, g + 1)
                if g:
                    act.wait_ge(o_ps, g * 2)
                for e in range(GR):
                    act.activation(hT[:, e, :], HP[0:SH, e * R:(e + 1) * R], ACT.Gelu, bias=b1t[:, g * GR + e:g * GR + e + 1]).then_inc(h_ready, 1)

        @block.vector
        def _(dve):
            dve.wait_ge(loaded, 160)
            for g in range(SE // GR):
                dve.wait_ge(slT_ps, g + 1)
                if g:
                    dve.wait_ge(h_ps, g)
                dve.tensor_copy(slT[:].rearrange("p m r -> p (m r)"), TP[:]).then_inc(slT_ready, 1)
                for k in range(GR // 2):
                    dve.wait_ge(o_ps, g * 2 + k + 1)
                    e = g * GR + k * 2
                    dve.tensor_tensor(so[:, e:e + 2, :].rearrange("r e d -> r (e d)"), OP[k][0:R, :],
                                      b2t[:, e:e + 2, :].rearrange("r e d -> r (e d)"), ALU.add).then_inc(o_ready, 1)


def soft_combine_stage(nc, name, combT, comb_rinv, slot_out, g_out):
    st = Stage(nc, name)
    with st.ctx:
        CT = st.sb("CT", [P, 2, EC, S])
        so = st.sb("so", [P, 2, EC, D])
        crin = st.sb("crin", [P, 2, QB])
        go = st.sb("go", [P, 2, QB, D])
        W = [st.ps(f"W{k}") for k in range(4)]
        loaded = [st.sem(f"loaded{u}") for u in range(2)]
        w_ready = st.sem("w_ready")
        w_read = st.sem("w_read")
        stored = [st.sem(f"stored{u}") for u in range(2)]
        NBK = QB // 2
        block = st.ctx.enter_context(nc.Block())

        @block.sync
        def _(sp):
            def load(b, u):
                sp.dma_start(CT[:, u], combT[b]).then_inc(loaded[u], 16)
                sp.dma_start(so[:, u], slot_out[b].rearrange("(e p) d -> p e d", p=P)).then_inc(loaded[u], 16)
                sp.dma_start(crin[:, u], comb_rinv[b]).then_inc(loaded[u], 16)
            load(0, 0)
            load(1, 1)
            for b in range(B):
                u = b % 2
                sp.wait_ge(w_read, (b + 1) * NBK + 4)
                for h in range(2):
                    sp.dma_start(g_out[b * 2 + h], go[:, u, h * TT:(h + 1) * TT, :]).then_inc(stored[u], 16)
                if b + 2 < B:
                    load(b + 2, u)
            for u in range(2):
                sp.wait_ge(stored[u], 16 * B)

        @block.tensor
        def _(pe):
            with pe.Fori(0, B // 2) as i:
                for u in range(2):
                    b = i * 2 + u
                    pe.wait_ge(loaded[u], (i + 1) * 48)
                    for k in range(NBK):
                        pe.wait_ge(w_read, b * NBK + k + 1)
                        for h in range(2):
                            t = 2 * k + h
                            for e in range(EC):
                                last = pe.matmul(W[k][:, h * D:(h + 1) * D], CT[:, u, e, t * P:(t + 1) * P], so[:, u, e, :],
                                                 start=(e == 0), stop=(e == EC - 1))
                        last.then_inc(w_ready, 1)

        @block.scalar
        def _(act):
            act.sem_inc(w_read, 4)
            with act.Fori(0, B // 2) as i:
                for u in range(2):
                    b = i * 2 + u
                    act.wait_ge(stored[u], i * 32)
                    for k in range(NBK):
                        act.wait_ge(w_ready, b * NBK + k + 1)
                        for h in range(2):
                            t = 2 * k + h
                            last = act.activation(go[:, u, t, :], W[k][:, h * D:(h + 1) * D], ACT.Silu, scale=crin[:, u, t:t + 1])
                        last.then_inc(w_read, 1)


NE, FF = 8, 1024
CAP = TOK // NE
NT_ = TOK // P
SKIP = 4 * NE * CAP
GELU_C = float(np.float32(np.sqrt(2.0) / 1.41421))


def route_stage(nc, name, consts, xnT, xn, w_sw, b_sw, rows, g_index, g_keep):
    st = Stage(nc, name)
    with st.ctx:
        xT = st.sb("xT", [P, 2, KC, CH])
        xa = st.sb("xa", [P, NT_, D])
        wsw = st.sb("wsw", [P, KC, NE])
        bsw = st.sb("bsw", [P, 1, NE])
        iota = st.sb("iota", [P, 1, NE])
        tri = st.sb("tri", [P, P])
        ones = st.sb("ones", [P, P])
        zero = st.sb("zero", [P, NE * CAP * D // P])
        LG = st.sb("LG", [P, NT_, NE])
        mx = st.sb("mx", [P, NT_, 1])
        eq = st.sb("eq", [P, NT_, NE])
        cand = st.sb("cand", [P, NT_, NE])
        first = st.sb("first", [P, NT_, 1])
        oh = st.sb("oh", [P, NT_, NE])
        tot = st.sb("tot", [P, NT_, NE])
        sa = st.sb("sa", [P, NT_, NE])
        sb_ = st.sb("sb", [P, NT_, NE])
        pos = st.sb("pos", [P, NT_, NE])
        ptok = st.sb("ptok", [P, NT_])
        keep = st.sb("keep", [P, NT_])
        base = st.sb("base", [P, NT_])
        gidx = st.sb("gidx", [P, NT_])
        sidx = st.sb("sidx", [P, NT_])
        gu = st.sb("gu", [P, NT_], U32)
        su = st.sb("su", [P, NT_], U32)
        LP = [st.ps(f"L{k}", (P, TT, NE)) for k in range(2)]
        W0 = st.ps("W0", (P, NT_, NE))
        W1 = st.ps("W1", (P, NT_, NE))
        c_in = st.sem("c_in")
        xa_in = st.sem("xa_in")
        x_in = [st.sem(f"x_in{u}") for u in range(2)]
        zeroed = st.sem("zeroed")
        zero_set = st.sem("zero_set")
        l_ready = st.sem("l_ready")
        l_read = st.sem("l_read")
        oh_ready = st.sem("oh_ready")
        count_ready = st.sem("count_ready")
        index_ready = st.sem("index_ready")
        scattered = st.sem("scattered")
        stored = st.sem("stored")
        dve_self = st.sem("dve_self")
        block = st.ctx.enter_context(nc.Block())

        @block.sync
        def _(sp):
            for dst, src in ((wsw[:], w_sw.rearrange("(c p) e -> p c e", p=P)), (bsw[:, 0], b_sw), (iota[:, 0], consts["iota"]),
                             (tri[:], consts["tri"]), (ones[:], consts["ones"])):
                sp.dma_start(dst, src).then_inc(c_in, 16)
            with sp.Fori(0, B) as i:
                for u in range(2):
                    sp.wait_ge(l_read, i * 2 + u + 1)
                    sp.dma_start(xT[:, u], xnT[:, :, bass.ds((i * 2 + u) * CH, CH)]).then_inc(x_in[u], 16)
            sp.wait_ge(zero_set, 1)
            sp.dma_start(rows.rearrange("(p r) d -> p (r d)", p=P), zero[:]).then_inc(zeroed, 16)
            for c in range(2 * B):
                sp.dma_start(xa[:, c * TT:(c + 1) * TT, :], xn[c]).then_inc(xa_in, 16)
            sp.wait_ge(index_ready, 1)
            sp.dma_start(g_index, gu[:]).then_inc(stored, 16)
            sp.dma_start(g_keep, keep[:]).then_inc(stored, 16)
            sp.wait_ge(stored, 32)

        @block.tensor
        def _(pe):
            pe.wait_ge(c_in, 80)
            with pe.Fori(0, B) as i:
                for u in range(2):
                    n = i * 2 + u
                    pe.wait_ge(x_in[u], (i + 1) * 16)
                    pe.wait_ge(l_read, n + 1)
                    for t in range(TT):
                        for c in range(KC):
                            last = pe.matmul(LP[u][:, t, :], xT[:, u, c, t * P:(t + 1) * P], wsw[:, c, :], start=(c == 0), stop=(c == KC - 1))
                    last.then_inc(l_ready, 1)
            pe.wait_ge(oh_ready, 1)
            oh2 = oh[:].rearrange("p t e -> p (t e)")
            pe.matmul(W0[:].rearrange("p t e -> p (t e)"), tri[:], oh2, start=True, stop=True)
            pe.matmul(W1[:].rearrange("p t e -> p (t e)"), ones[:], oh2, start=True, stop=True).then_inc(count_ready, 1)

        @block.gpsimd
        def _(pool):
            pool.memset(zero[:], 0.0).then_inc(zero_set, 1)
            pool.wait_ge(zeroed, 16)
            pool.wait_ge(xa_in, 16 * 2 * B)
            pool.wait_ge(index_ready, 1)
            for t in range(NT_):
                pool.indirect_dma_start(out=rows, out_offset=bass.IndirectOffsetOnAxis(ap=su[:, t:t + 1], axis=0),
                                        in_=xa[:, t, :], in_offset=None, bounds_check=NE * CAP - 1, oob_is_err=False)\
                    .then_inc(scattered, 16)
            pool.wait_ge(scattered, 16 * NT_)

        @block.vector
        def _(dve):
            dve.sem_inc(l_read, 2)
            dve.wait_ge(c_in, 80)
            with dve.Fori(0, B) as i:
                for u in range(2):
                    n = i * 2 + u
                    dve.wait_ge(l_ready, n + 1)
                    dve.tensor_tensor(LG[:, bass.ds(n * TT, TT), :], LP[u][:], bsw[:].broadcast_to([P, TT, NE]), ALU.add).then_inc(l_read, 1)
            dve.wait_ge(l_read, 2 * B + 2)
            link = Chain(dve, dve_self)
            full = [P, NT_, NE]
            link(dve.tensor_reduce(mx[:], LG[:], AX, ALU.max))
            link(dve.tensor_tensor(eq[:], LG[:], mx[:].broadcast_to(full), ALU.is_ge))
            link(dve.scalar_tensor_tensor(out=cand[:], in0=eq[:], scalar=-float(NE), in1=iota[:].broadcast_to(full), op0=ALU.mult, op1=ALU.add))
            link(dve.tensor_reduce(first[:], cand[:], AX, ALU.min))
            dve.tensor_tensor(oh[:], cand[:], first[:].broadcast_to(full), ALU.is_equal).then_inc(oh_ready, 1)
            link(dve.tensor_scalar(base[:], first[:, :, 0], float(CAP), float(NE * CAP), ALU.mult, ALU.add))
            dve.wait_ge(count_ready, 1)
            link(dve.tensor_copy(tot[:], W1[:]))
            src, dst, step = tot, sa, 1
            while step < NT_:
                dve.tensor_copy(dst[:, 0:step, :], src[:, 0:step, :])
                link(dve.tensor_tensor(dst[:, step:, :], src[:, step:, :], src[:, 0:NT_ - step, :], ALU.add))
                src, dst, step = dst, (sb_ if dst is sa else sa), step * 2
            link(dve.tensor_tensor(pos[:], src[:], tot[:], ALU.subtract))
            link(dve.scalar_tensor_tensor(out=cand[:], in0=W0[:], scalar=-1.0, in1=pos[:], op0=ALU.add, op1=ALU.add))
            link(dve.tensor_tensor(pos[:], cand[:], oh[:], ALU.mult))
            link(dve.tensor_reduce(ptok[:], pos[:], AX, ALU.add))
            link(dve.tensor_scalar(keep[:], ptok[:], float(CAP), None, ALU.is_lt))
            link(dve.tensor_scalar(gidx[:], ptok[:], float(CAP - 1), None, ALU.min))
            link(dve.tensor_tensor(gidx[:], gidx[:], base[:], ALU.add))
            link(dve.tensor_scalar(sidx[:], keep[:], -float(SKIP), float(SKIP), ALU.mult, ALU.add))
            link(dve.tensor_tensor(sidx[:], sidx[:], gidx[:], ALU.add))
            dve.tensor_copy(gu[:], gidx[:])
            dve.tensor_copy(su[:], sidx[:]).then_inc(index_ready, 1)


def routed_experts_stage(nc, name, consts, rows, w1, b1, w2, b2, out_rows):
    st = Stage(nc, name)
    with st.ctx:
        M = FF // P
        ident = st.sb("ident", [P, P])
        x = st.sb("x", [P, 2, TT, D])
        xT = st.sb("xT", [P, 2, KC, CAP])
        w1t = st.sb("w1", [P, 2, KC, FF])
        w2t = st.sb("w2", [P, 2, M, D])
        b1t = st.sb("b1", [P, 2, M])
        b1c = st.sb("b1c", [P, 2, M])
        b2t = st.sb("b2", [P, 2, D])
        hT = st.sb("hT", [P, 2, M, CAP])
        o = st.sb("o", [P, 2, TT, D])
        T = [st.ps(f"T{k}") for k in range(2)]
        H = [st.ps(f"H{k}") for k in range(2)]
        O = [st.ps(f"O{k}", (P, 2, D)) for k in range(2)]
        ident_in = st.sem("ident_in")
        loaded = [st.sem(f"loaded{u}") for u in range(2)]
        in_free = st.sem("in_free")
        t_ready = st.sem("t_ready")
        xT_ready = st.sem("xT_ready")
        b1_ready = st.sem("b1_ready")
        h_ps = st.sem("h_ps")
        h_ready = st.sem("h_ready")
        o_ps = st.sem("o_ps")
        o_ready = st.sem("o_ready")
        stored = [st.sem(f"stored{u}") for u in range(2)]
        dve_self = st.sem("dve_self")
        block = st.ctx.enter_context(nc.Block())

        @block.sync
        def _(sp):
            sp.dma_start(ident[:], consts["ident"]).then_inc(ident_in, 16)

            def load(i, u):
                e = i * 2 + u
                for dst, src in ((x[:, u], rows.rearrange("(e t p) d -> e p t d", e=NE, p=P)),
                                 (w1t[:, u], w1.rearrange("e (c p) f -> e p c f", p=P)),
                                 (w2t[:, u], w2.rearrange("e (m p) d -> e p m d", p=P))):
                    sp.dma_start(dst, one(src, e).rearrange("e p a b -> p (e a) b")).then_inc(loaded[u], 16)
                for dst, src in ((b1t[:, u], b1), (b2t[:, u], b2)):
                    sp.dma_start(dst, one(src, e).rearrange("e p a -> (e p) a")).then_inc(loaded[u], 16)

            def body(i, more):
                for u in range(2):
                    e = i * 2 + u
                    sp.wait_ge(o_ready, (e + 1) * 2 + 2)
                    sp.dma_start(one(out_rows.rearrange("(e t p) d -> e p t d", e=NE, p=P), e).rearrange("e p a b -> p (e a) b"), o[:, u])\
                      .then_inc(stored[u], 16)
                    if more:
                        sp.wait_ge(in_free, e + 1)
                        load(i + 1, u)
            load(0, 0)
            load(0, 1)
            with sp.Fori(0, NE // 2 - 1) as i:
                body(i, True)
            body(NE // 2 - 1, False)
            for u in range(2):
                sp.wait_ge(stored[u], 16 * NE // 2)

        @block.tensor
        def _(pe):
            pe.wait_ge(ident_in, 16)
            with pe.Fori(0, NE // 2) as i:
                for u in range(2):
                    e = i * 2 + u
                    pe.wait_ge(loaded[u], (i + 1) * 80)
                    for c in range(KC):
                        pe.wait_ge(xT_ready, e * KC + c + 1)
                        for t in range(TT):
                            last = pe.transpose(T[c][:, t * P:(t + 1) * P], x[:, u, t, c * P:(c + 1) * P], ident[:])
                        last.then_inc(t_ready, 1)
                for u in range(2):
                    e = i * 2 + u
                    pe.wait_ge(xT_ready, (e + 1) * KC + 2)
                    for m in range(M):
                        pe.wait_ge(h_ready, e * M + m + 1)
                        for c in range(KC):
                            last = pe.matmul(H[m % 2][:], w1t[:, u, c, m * P:(m + 1) * P], xT[:, u, c, :], start=(c == 0), stop=(c == KC - 1))
                        last.then_inc(h_ps, 1)
                for u in range(2):
                    e = i * 2 + u
                    pe.wait_ge(h_ready, (e + 1) * M + 2)
                    for k in range(2):
                        pe.wait_ge(o_ready, e * 2 + k + 1)
                        for h in range(2):
                            for m in range(M):
                                last = pe.matmul(O[k][:, h, :], hT[:, u, m, (2 * k + h) * P:(2 * k + h + 1) * P], w2t[:, u, m, :],
                                                 start=(m == 0), stop=(m == M - 1))
                        last.then_inc(o_ps, 1)

        @block.scalar
        def _(act):
            act.sem_inc(h_ready, 2)
            with act.Fori(0, NE // 2) as i:
                for u in range(2):
                    e = i * 2 + u
                    act.wait_ge(b1_ready, e + 1)
                    act.wait_ge(o_ps, i * 4)
                    for m in range(M):
                        act.wait_ge(h_ps, e * M + m + 1)
                        act.activation(hT[:, u, m, :], H[m % 2][:], ACT.Gelu, bias=b1c[:, u, m:m + 1], scale=GELU_C).then_inc(h_ready, 1)

        @block.vector
        def _(dve):
            dve.sem_inc(xT_ready, 2)
            dve.sem_inc(o_ready, 2)
            with dve.Fori(0, NE // 2) as i:
                for u in range(2):
                    e = i * 2 + u
                    dve.wait_ge(loaded[u], (i + 1) * 80)
                    for c in range(KC):
                        dve.wait_ge(t_ready, e * KC + c + 1)
                        dve.tensor_copy(xT[:, u, c, :], T[c][:]).then_inc(xT_ready, 1)
                    dve.tensor_scalar(b1c[:, u], b1t[:, u], GELU_C, None, ALU.mult).then_inc(b1_ready, 1)
                for u in range(2):
                    e = i * 2 + u
                    dve.wait_ge(stored[u], i * 16)
                    for k in range(2):
                        dve.wait_ge(o_ps, e * 2 + k + 1)
                        dve.scalar_tensor_tensor(out=o[:, u, 2 * k:2 * k + 2, :], in0=O[k][:], scalar=1.0 / GELU_C,
                                                 in1=b2t[:, u:u + 1, :].broadcast_to([P, 2, D]), op0=ALU.mult, op1=ALU.add).then_inc(o_ready, 1)
                    dve.wait_ge(o_ready, (e + 1) * 2 + 2)
                    dve.sem_inc(in_free, 1)


def gather_stage(nc, name, xn, out_rows, g_index, g_keep, g_out):
    st = Stage(nc, name)
    with st.ctx:
        gu = st.sb("gu", [P, NT_], U32)
        keep = st.sb("keep", [P, NT_])
        drop = st.sb("drop", [P, NT_])
        x = st.sb("x", [P, 2 * B, TT, D])
        y = st.sb("y", [P, 2 * B, TT, D])
        index_in = st.sem("index_in")
        x_in = st.sem("x_in")
        gathered = [st.sem(f"gathered{c}") for c in range(2 * B)]
        drop_ready = st.sem("drop_ready")
        kept = st.sem("kept")
        mixed = st.sem("mixed")
        out_ready = st.sem("out_ready")
        stored = st.sem("stored")
        block = st.ctx.enter_context(nc.Block())

        @block.sync
        def _(sp):
            sp.dma_start(gu[:], g_index).then_inc(index_in, 16)
            sp.dma_start(keep[:], g_keep).then_inc(index_in, 16)
            for c in range(2 * B):
                sp.dma_start(x[:, c], xn[c]).then_inc(x_in, 16)
            for c in range(2 * B):
                sp.wait_ge(out_ready, c + 1)
                sp.dma_start(g_out[c], y[:, c]).then_inc(stored, 16)
            sp.wait_ge(stored, 16 * 2 * B)

        @block.gpsimd
        def _(pool):
            pool.wait_ge(index_in, 32)
            for c in range(2 * B):
                for t in range(TT):
                    k = c * TT + t
                    pool.indirect_dma_start(out=y[:, c, t, :], out_offset=None, in_=out_rows,
                                            in_offset=bass.IndirectOffsetOnAxis(ap=gu[:, k:k + 1], axis=0)).then_inc(gathered[c], 16)

        @block.vector
        def _(dve):
            dve.wait_ge(index_in, 32)
            dve.tensor_scalar(drop[:], keep[:], -1.0, 1.0, ALU.mult, ALU.add).then_inc(drop_ready, 1)
            dve.wait_ge(drop_ready, 1)
            dve.wait_ge(x_in, 16 * 2 * B)
            for c in range(2 * B):
                dve.wait_ge(gathered[c], 16 * TT)
                for t in range(TT):
                    k = c * TT + t
                    last = dve.tensor_scalar(y[:, c, t, :], y[:, c, t, :], keep[:, k:k + 1], None, ALU.mult)
                last.then_inc(kept, 1)
                dve.wait_ge(kept, c + 1)
                for t in range(TT):
                    k = c * TT + t
                    last = dve.scalar_tensor_tensor(out=y[:, c, t, :], in0=x[:, c, t, :], scalar=drop[:, k:k + 1], in1=y[:, c, t, :],
                                                    op0=ALU.mult, op1=ALU.add)
                last.then_inc(mixed, 1)

        @block.scalar
        def _(act):
            for c in range(2 * B):
                act.wait_ge(mixed, c + 1)
                act.activation(y[:, c], y[:, c], ACT.Silu).then_inc(out_ready, 1)


def build_layers(nc, a, out):
    def scratch(name, shape, dt=F32):
        return nc.dram_tensor(name, shape, dt).ap()

    def tiles(ap):
        return ap.rearrange("(c t p) d -> c p t d", t=TT, p=P)

    def token_major(ap):
        return lambda i, u: [(0, TT, one(ap, i)[:, u * CH:(u + 1) * CH, :].rearrange("b (t p) (c n) -> p (b t) c n", p=P, n=P))]

    def head_major(ap):
        return lambda i, u: [(t, t + 1, one(ap, i)[:, :, u * CH + t * P:u * CH + (t + 1) * P, :].rearrange("b c p n -> p b c n"))
                             for t in range(TT)]

    x0 = a["x"].rearrange("b s d -> (b s) d")
    x1, x2, x3 = (scratch(f"x{k}", (TOK, D)) for k in (1, 2, 3))
    xn = scratch("xn", (TOK, D))
    xnT_rows = scratch("xnT", (D, TOK))
    xnT = xnT_rows.rearrange("(c p) t -> p c t", p=P)
    g = scratch("g", (TOK, D))

    q0, k0 = scratch("q0", (B, D, S)), scratch("k0", (B, D, S))
    v0, s0 = scratch("v0", (B, S, D)), scratch("s0", (B, S, D))
    update_stage(nc, "n0", a, tiles(x0), xnT=xnT)

    def qk0(i, u, j):
        dst = q0 if j < KC else k0
        return one(dst, i)[:, j % KC * P:(j % KC + 1) * P, u * CH:(u + 1) * CH].rearrange("b p t -> (b p) t")
    project_stage(nc, "p0", a, xnT, a["w0"], KC, KC, D, 1.0 / 16.0, qk0, token_major(v0))
    attention_stage(nc, "a0", a, q0.rearrange("b (h f) s -> b h f s", h=1), k0, v0, s0.rearrange("b (h s) d -> b h s d", h=1),
                    B, 1, KC, D, False)
    swiglu_stage(nc, "f0", xnT, a["wg0"], a["wu0"], a["wd0"], tiles(g))

    q_parts, k_parts = scratch("q_parts", (3, B * D, S), BF16), scratch("k_parts", (3, B * D, S), BF16)
    vn, on = scratch("vn", (B, S, D)), scratch("on", (B, S, D))
    m_rows = scratch("m_rows", (B * 4, HG, NR, S), BF16)

    def qk_parts(i, u, j):
        dst = q_parts if j < KC else k_parts
        return dst[:, bass.ds(i * D + j % KC * P, P), u * CH:(u + 1) * CH].rearrange("s p t -> p s t")
    update_stage(nc, "n1", a, tiles(x0), x_out=tiles(x1), xnT=xnT, xn=tiles(xn), s_in=tiles(s0.rearrange("b s d -> (b s) d")),
                 g_in=tiles(g))
    project_stage(nc, "p1", a, xnT, a["w1"], KC, KC, D, 0.25, qk_parts, token_major(vn),
                  rope=(a["perm16"], a["cos16"], a["sin16"]), parts=True)
    narrow_attention_stage(nc, "a1", a, q_parts, k_parts, vn, on, m_rows, B * 4)
    slots, slot_out = scratch("slots", (B, ES, D)), scratch("slot_out", (B, ES, D))
    combT, comb_rinv = scratch("combT", (B, P, EC, S)), scratch("comb_rinv", (B, P, QB))
    soft_slots_stage(nc, "e1", a, tiles(xn), a["gamma"], a["beta"], a["mu"], a["scale"], slots, combT, comb_rinv)
    soft_experts_stage(nc, "e2", a, slots, a["se_w1"], a["se_b1"], a["se_w2"], a["se_b2"], slot_out)
    soft_combine_stage(nc, "e3", combT, comb_rinv, slot_out, tiles(g))

    update_stage(nc, "n2", a, tiles(x1), x_out=tiles(x2), xnT=xnT, xn=tiles(xn), o_in=token_major(on), w_o=a["wo1"],
                 o_chunks=KC, g_in=tiles(g))
    project_stage(nc, "p2", a, xnT, a["w2"], KC, KC, D, 0.25, qk_parts, token_major(vn), parts=True)
    narrow_attention_stage(nc, "a2", a, q_parts, k_parts, vn, on, m_rows, B * 4)
    rows, out_rows = scratch("rows", (TOK, D)), scratch("out_rows", (TOK, D))
    g_index, g_keep = scratch("g_index", (P, TOK // P), U32), scratch("g_keep", (P, TOK // P))
    route_stage(nc, "r1", a, xnT, tiles(xn), a["w_sw"], a["b_sw"], rows, g_index, g_keep)
    routed_experts_stage(nc, "r2", a, rows, a["re_w1"], a["re_b1"], a["re_w2"], a["re_b2"], out_rows)
    gather_stage(nc, "r3", tiles(xn), out_rows, g_index, g_keep, tiles(g))

    NQ, NK = 8, 4
    q3, k3 = scratch("q3", (B * NQ, P, S)), scratch("k3", (B * NK, P, S))
    v3, o3 = scratch("v3", (B, NK, S, P)), scratch("o3", (B, NQ, S, P))
    update_stage(nc, "n3", a, tiles(x2), x_out=tiles(x3), xnT=xnT, o_in=token_major(on), w_o=a["wo2"], o_chunks=KC, g_in=tiles(g))

    def qk3(i, u, j):
        dst = one(q3, i * NQ + j) if j < NQ else one(k3, i * NK + (j - NQ))
        return dst[:, :, u * CH:(u + 1) * CH].rearrange("b p t -> (b p) t")
    project_stage(nc, "p3", a, xnT, a["w3"], NQ, NK, NK * P, float(np.float32(1.0 / np.sqrt(128.0))), qk3, head_major(v3),
                  rope=(a["perm128"], a["cos128"], a["sin128"]))
    attention_stage(nc, "a3", a, q3.rearrange("(u h) p s -> u h p s", h=NQ // NK), k3, v3.rearrange("b k s n -> (b k) s n"),
                    o3.rearrange("b (k h) s n -> (b k) h s n", h=NQ // NK), B * NK, NQ // NK, 1, P, True)
    swiglu_stage(nc, "f3", xnT, a["wg3"], a["wu3"], a["wd3"], tiles(g))
    update_stage(nc, "n4", a, tiles(x3), x_out=tiles(out.rearrange("b s d -> (b s) d")), o_in=head_major(o3), w_o=a["wo3"],
                 o_chunks=NQ, g_in=tiles(g))


def shape_constants():
    bf = mybir.dt.np(BF16)
    eye, ones = np.eye(P, dtype=np.float32), np.ones((P, P), np.float32)
    c = {"ident": eye, "identb": eye.astype(bf), "ones": ones, "tri": np.triu(ones),
         "mask": (np.triu(ones, 1) * NEG).astype(bf), "maskT": (np.tril(ones, -1) * NEG).astype(bf),
         "iota": np.tile(np.arange(8, dtype=np.float32), (P, 1))}
    for dh in (16, 128):
        half = dh // 2
        inv = (np.float32(1.0) / np.float32(10000.0) ** (np.arange(0, dh, 2, dtype=np.float32) / np.float32(dh))).astype(np.float32)
        angle = np.arange(S, dtype=np.float32)[:, None] * inv[None, :]
        feature = np.arange(P) % dh
        perm = np.zeros((P, P), np.float32)
        for p in range(P):
            if feature[p] < half:
                perm[p + half, p] = -1.0
            else:
                perm[p - half, p] = 1.0
        c[f"perm{dh}"] = perm
        c[f"cos{dh}"] = np.ascontiguousarray(np.cos(angle)[:, feature % half].T)
        c[f"sin{dh}"] = np.ascontiguousarray(np.sin(angle)[:, feature % half].T)
    return c


def kernel(**inputs):
    import concourse.bacc as bacc
    from concourse.bass_utils import run_bass_kernel_spmd

    t = {name: np.asarray(v) for name, v in inputs.items()}

    def repeated(v, shape):
        return np.broadcast_to(v, shape)
    arrays = {
        "x": t["L0_attn_x"],
        "w0": t["L0_attn_W_qkv"].T,
        "wg0": t["L0_ffn_w_gate"].T, "wu0": t["L0_ffn_w_up"].T, "wd0": t["L0_ffn_w_down"].T,
        "w1": t["L1_attn_w_qkv"], "wo1": t["L1_attn_w_out"],
        "gamma": repeated(t["L1_ffn_ln_gamma"], (P, D)), "beta": repeated(t["L1_ffn_ln_beta"], (P, D)),
        "mu": t["L1_ffn_mu"].reshape(D, ES), "scale": repeated(t["L1_ffn_scale"], (P, 1)),
        "se_w1": t["L1_ffn_w1"], "se_b1": t["L1_ffn_b1"].T,
        "se_w2": t["L1_ffn_w2"], "se_b2": repeated(t["L1_ffn_b2"], (SH, SE, D)),
        "w2": np.concatenate([t[f"L2_attn_W{c}"].reshape(D, D) for c in "qkv"], axis=1),
        "wo2": t["L2_attn_Wout"].reshape(D, D),
        "w_sw": t["L2_ffn_W_sw"], "b_sw": repeated(t["L2_ffn_b_sw"], (P, 8)),
        "re_w1": t["L2_ffn_W1"], "re_b1": t["L2_ffn_b1"].reshape(8, 8, P).transpose(0, 2, 1),
        "re_w2": t["L2_ffn_W2"], "re_b2": repeated(t["L2_ffn_b2"][:, None, :], (8, P, D)),
        "w3": np.concatenate([t[f"L3_attn_W{c}"] for c in "qkv"], axis=1), "wo3": t["L3_attn_Wo"],
        "wg3": t["L3_ffn_w_gate"].T, "wu3": t["L3_ffn_w_up"].T, "wd3": t["L3_ffn_w_down"].T,
    }
    arrays.update(shape_constants())
    arrays = {name: np.ascontiguousarray(v) for name, v in arrays.items()}
    nc = bacc.Bacc("TRN2", target_bir_lowering=False, num_devices=1)
    a = {name: nc.dram_tensor(f"in_{name}", v.shape, mybir.dt.from_np(v.dtype), kind="ExternalInput").ap()
         for name, v in arrays.items()}
    out = nc.dram_tensor("out_x", (B, S, D), F32, kind="ExternalOutput").ap()
    build_layers(nc, a, out)
    r = run_bass_kernel_spmd(nc, [{f"in_{name}": v for name, v in arrays.items()}], core_ids=[0])
    return r.results[0]["out_x"]
```

```python
import numpy as np
import concourse.bass as bass
from concourse import mybir
from contextlib import ExitStack

F32 = mybir.dt.float32
BF16 = mybir.dt.bfloat16
F32R = mybir.dt.float32r
I32 = mybir.dt.int32
U32 = mybir.dt.uint32
ALU = mybir.AluOpType
ACT = mybir.ActivationFunctionType
AX = mybir.AxisListType.X

P = 128
B, S, D = 4, 1024, 256
TOK = B * S
CH = 512
KC = D // P
TT = CH // P
QB = S // P
NEG = -1.0e30
PAIRS = [(0, 0), (0, 1), (1, 0)]


class Chain:

    def __init__(self, eng, sem, base=0):
        self.eng, self.sem, self.base, self.n = eng, sem, base, 0

    def __call__(self, ins):
        self.n += 1
        ins.then_inc(self.sem, 1)
        self.eng.wait_ge(self.sem, self.base + self.n)


class SeqNumber:

    def __init__(self, value, rest, banks):
        self.value, self.rest, self.banks = value, rest % banks, banks

    def __add__(self, k):
        return SeqNumber(self.value + k, self.rest + k, self.banks)


def count(q):
    return q.value if isinstance(q, SeqNumber) else q


class Stage:

    def __init__(self, nc, name):
        self.nc, self.name, self.ctx, self.sems = nc, name, ExitStack(), []
        self.ctx.callback(self.clear)

    def clear(self):
        self.nc.clear_and_free_semaphores(self.sems)
        self.nc.all_engine_barrier()

    def sb(self, name, shape, dt=F32):
        return self.ctx.enter_context(self.nc.sbuf_tensor(f"{self.name}_{name}", shape, dt))

    def ps(self, name, shape=(P, 512), dt=F32):
        return self.ctx.enter_context(self.nc.psum_tensor(f"{self.name}_{name}", list(shape), dt))

    def sem(self, name):
        self.sems.append(self.nc.alloc_semaphore(name=f"{self.name}_{name}"))
        return self.sems[-1]


def one(ap, i):
    return ap[bass.ds(i, 1)]


def update_stage(nc, name, consts, x_in, x_out=None, xnT=None, xn=None, s_in=None, o_in=None, w_o=None,
                 o_chunks=0, g_in=None):
    st = Stage(nc, name)
    with st.ctx:
        upd, norm, proj = g_in is not None, xnT is not None, o_in is not None
        ident = st.sb("ident", [P, P])
        xt = st.sb("x", [P, 2, TT, D])
        if upd:
            gt = st.sb("g", [P, 2, TT, D])
            tmp = st.sb("tmp", [P, TT, D])
            xnew = st.sb("xnew", [P, 2, TT, D])
            if not proj:
                sin = st.sb("s", [P, 2, TT, D])
        if proj:
            NG = TT * o_chunks // 4
            ot = st.sb("o", [P, 2, TT, o_chunks * P])
            oT = st.sb("oT", [P, TT * o_chunks, P])
            wo = st.sb("wo", [P, o_chunks, D])
            T = [st.ps(f"T{k}") for k in range(2)]
            SP_ = [st.ps(f"S{k}", (P, 2, D)) for k in range(2)]
        if norm:
            stats = st.sb("stats", [P, TT, 6])
            mv = st.sb("mv", [P, TT, 2])
            vep = st.sb("vep", [P, TT])
            std = st.sb("std", [P, TT])
            rstd = st.sb("rstd", [P, TT])
            xnt = st.sb("xn", [P, 2, TT, D])
            xnTt = st.sb("xnT", [P, 2, KC, CH])
            X = [st.ps(f"X{k}") for k in range(2)]
        loaded = [st.sem(f"loaded{u}") for u in range(2)]
        consts_in = st.sem("consts_in")
        x_stored = [st.sem(f"x_stored{u}") for u in range(2)]
        stored = [st.sem(f"stored{u}") for u in range(2)]
        stats_seen = st.sem("stats_seen")
        inputs_free = st.sem("inputs_free")
        oT_ready = st.sem("oT_ready")
        oT_copied = st.sem("oT_copied")
        s_ready = st.sem("s_ready")
        s_used = st.sem("s_used")
        x_ready = st.sem("x_ready")
        var_ready = st.sem("var_ready")
        std_ready = st.sem("std_ready")
        xn_ready = st.sem("xn_ready")
        xT_ready = st.sem("xT_ready")
        xT_copied = st.sem("xT_copied")
        dve_self = st.sem("dve_self")
        loads = 1 + (1 if upd else 0) + (1 if upd and not proj else 0) + (len(o_in(0, 0)) if proj else 0)
        stores = (1 if norm else 0) + (1 if xn is not None else 0)

        def in_turn(eng, project, turn):
            def body(i, more):
                for u in range(2):
                    if proj and (u == 0 or more):
                        project(*((i, 1) if u == 0 else (i + 1, 0)))
                    if norm:
                        turn(i, u)
            if proj:
                project(0, 0)
            with eng.Fori(0, B - 1) as i:
                body(i, True)
            body(B - 1, False)
        block = st.ctx.enter_context(nc.Block())

        @block.sync
        def _(sp):
            sp.dma_start(ident[:], consts["ident"]).then_inc(consts_in, 16)
            if proj:
                sp.dma_start(wo[:], w_o.rearrange("(c p) n -> p c n", p=P)).then_inc(consts_in, 16)

            def load(i, u):
                n = i * 2 + u
                sp.dma_start(xt[:, u], one(x_in, n).rearrange("c p t d -> p (c t) d")).then_inc(loaded[u], 16)
                if upd:
                    sp.dma_start(gt[:, u], one(g_in, n).rearrange("c p t d -> p (c t) d")).then_inc(loaded[u], 16)
                    if not proj:
                        sp.dma_start(sin[:, u], one(s_in, n).rearrange("c p t d -> p (c t) d")).then_inc(loaded[u], 16)
                if proj:
                    for lo, hi, src in o_in(i, u):
                        sp.dma_start(ot[:, u, lo:hi, :].rearrange("p t (c n) -> p t c n", n=P), src).then_inc(loaded[u], 16)

            def body(i, more):
                for u in range(2):
                    n = i * 2 + u
                    if x_out is not None:
                        sp.wait_ge(x_ready, n + 1)
                        sp.dma_start(one(x_out, n).rearrange("c p t d -> p (c t) d"), xnew[:, u]).then_inc(x_stored[u], 16)
                    if more:
                        sp.wait_ge(inputs_free, n + 1)
                        load(i + 1, u)
                    if xn is not None:
                        sp.wait_ge(xn_ready, n + 1)
                        sp.dma_start(one(xn, n).rearrange("c p t d -> p (c t) d"), xnt[:, u]).then_inc(stored[u], 16)
                    if norm:
                        sp.wait_ge(xT_copied, n * KC + 2 * KC)
                        sp.dma_start(xnT[:, :, bass.ds(n * CH, CH)], xnTt[:, u]).then_inc(stored[u], 16)
            load(0, 0)
            load(0, 1)
            with sp.Fori(0, B - 1) as i:
                body(i, True)
            body(B - 1, False)
            for u in range(2):
                if x_out is not None:
                    sp.wait_ge(x_stored[u], 16 * B)
                if stores:
                    sp.wait_ge(stored[u], 16 * stores * B)

        @block.tensor
        def _(pe):
            pe.wait_ge(consts_in, 32 if proj else 16)

            def project(i, u):
                n = i * 2 + u
                pe.wait_ge(loaded[u], (i + 1) * (16 * loads))
                for g in range(NG):
                    pe.wait_ge(oT_copied, n * NG + g + 1)
                    for k in range(4):
                        t, c = divmod(g * 4 + k, o_chunks)
                        last = pe.transpose(T[g % 2][:, k * P:(k + 1) * P], ot[:, u, t, c * P:(c + 1) * P], ident[:])
                    last.then_inc(oT_ready, 1)
                pe.wait_ge(oT_copied, n * NG + NG + 2)
                for t in range(TT):
                    if t % 2 == 0:
                        pe.wait_ge(s_used, n * 2 + t // 2 + 1)
                    for c in range(o_chunks):
                        last = pe.matmul(SP_[t // 2][:, t % 2, :], oT[:, t * o_chunks + c, :], wo[:, c, :],
                                         start=(c == 0), stop=(c == o_chunks - 1))
                    if t % 2 == 1:
                        last.then_inc(s_ready, 1)

            def turn(i, u):
                n = i * 2 + u
                pe.wait_ge(xn_ready, n + 1)
                for c in range(KC):
                    pe.wait_ge(xT_copied, n * KC + c + 1)
                    for t in range(TT):
                        last = pe.transpose(X[c][:, t * P:(t + 1) * P], xnt[:, u, t, c * P:(c + 1) * P], ident[:])
                    last.then_inc(xT_ready, 1)
            in_turn(pe, project, turn)

        @block.scalar
        def _(act):
            act.sem_inc(oT_copied, 2)
            act.sem_inc(xT_copied, KC)

            def project(i, u):
                n = i * 2 + u
                act.wait_ge(s_ready, n * 2)
                for g in range(NG):
                    act.wait_ge(oT_ready, n * NG + g + 1)
                    act.copy(oT[:, g * 4:g * 4 + 4, :].rearrange("p a b -> p (a b)"), T[g % 2][:]).then_inc(oT_copied, 1)

            def turn(i, u):
                n = i * 2 + u
                act.wait_ge(var_ready, n + 1)
                act.activation(std[:], vep[:], ACT.Sqrt).then_inc(std_ready, 1)
                act.wait_ge(stored[u], i * (16 * stores))
                for c in range(KC):
                    act.wait_ge(xT_ready, n * KC + c + 1)
                    act.copy(xnTt[:, u, c, :], X[c][:]).then_inc(xT_copied, 1)
            in_turn(act, project, turn)

        @block.vector
        def _(dve):
            dve.sem_inc(s_used, 2)
            PER = 2 * ((1 if proj else 2 if upd else 0) + (3 if norm else 0))
            with dve.Fori(0, B) as i:
                link = Chain(dve, dve_self, i * PER)
                for u in range(2):
                    n = i * 2 + u
                    dve.wait_ge(loaded[u], (i + 1) * (16 * loads))
                    if upd and proj:
                        for h in range(2):
                            dve.wait_ge(s_ready, n * 2 + h + 1)
                            dve.tensor_tensor(tmp[:, 2 * h:2 * h + 2, :], SP_[h][:], gt[:, u, 2 * h:2 * h + 2, :],
                                              ALU.mult).then_inc(s_used, 1)
                        dve.wait_ge(s_used, n * 2 + 4)
                    elif upd:
                        link(dve.tensor_tensor(tmp[:], sin[:, u], gt[:, u], ALU.mult))
                    if upd:
                        dve.wait_ge(x_stored[u], i * 16)
                        link(dve.tensor_tensor(xnew[:, u], xt[:, u], tmp[:], ALU.add))
                        dve.sem_inc(x_ready, 1)
                        dve.sem_inc(inputs_free, 1)
                    if not norm:
                        continue
                    xc = xnew if upd else xt
                    for t in range(TT):
                        last = dve.bn_stats(stats[:, t, :], xc[:, u, t, :])
                    link(last)
                    dve.sem_inc(stats_seen, 1)
                    for t in range(TT):
                        last = dve.bn_aggr(mv[:, t, :], stats[:, t, :])
                    link(last)
                    dve.tensor_scalar(vep[:], mv[:, :, 1], 1e-5, None, ALU.add).then_inc(var_ready, 1)
                    dve.wait_ge(std_ready, n + 1)
                    link(dve.reciprocal(rstd[:], std[:]))
                    dve.wait_ge(stored[u], i * (16 * stores))
                    for t in range(TT):
                        last = dve.tensor_scalar(xnt[:, u, t, :], xc[:, u, t, :], mv[:, t, 0:1], rstd[:, t:t + 1],
                                                 ALU.subtract, ALU.mult)
                    last.then_inc(xn_ready, 1)
                    if not upd:
                        dve.wait_ge(xn_ready, n + 1)
                        dve.sem_inc(inputs_free, 1)


def project_stage(nc, name, consts, xnT, w, q_tiles, k_tiles, v_cols, q_scale, qk_out, v_out, rope=None, parts=False):
    st = Stage(nc, name)
    with st.ctx:
        J = q_tiles + k_tiles
        NW = J * P + v_cols
        VB = v_cols // 256
        VS = TT * VB // 2
        VD = len(v_out(0, 0))
        xT = st.sb("xT", [P, 2, KC, CH])
        xs = [st.sb(f"x{k}", [P, 2, KC, CH], F32R) for k in range(2)]
        wf = st.sb("wf", [P, KC, NW])
        wt = [st.sb(f"w{k}", [P, KC, NW], F32R) for k in range(2)]
        FS = J if parts else 2
        QS = J if parts and not rope else 2
        qs = st.sb("qs", [P, QS, CH])
        if rope:
            perm = st.sb("perm", [P, P])
            cos = st.sb("cos", [P, S])
            sin = st.sb("sin", [P, S])
            tc = st.sb("tc", [P, 2, CH])
            ts = st.sb("ts", [P, 2, CH])
            RP = [st.ps(f"R{k}") for k in range(2)]
        if parts:
            part = st.sb("part", [P, FS, 3, CH], BF16)
            rest = st.sb("rest", [P, FS, CH])
        if rope or not parts:
            fin = st.sb("fin", [P, FS, CH])
        else:
            fin = qs
        vs = st.sb("v", [P, 2, TT, v_cols])
        QP = [st.ps(f"Q{k}") for k in range(2)]
        VP = [st.ps(f"V{k}") for k in range(2)]
        consts_in = st.sem("consts_in")
        x_in = [st.sem(f"x_in{u}") for u in range(2)]
        wh_ready = st.sem("wh_ready")
        w_ready = st.sem("w_ready")
        x_free = st.sem("x_free")
        xh_ready = st.sem("xh_ready")
        x_ready = st.sem("x_ready")
        q_ready = st.sem("q_ready")
        q_copied = st.sem("q_copied")
        r_ready = st.sem("r_ready")
        cos_ready = st.sem("cos_ready")
        f_ready = st.sem("f_ready")
        hi_ready = st.sem("hi_ready")
        r1_ready = st.sem("r1_ready")
        mid_ready = st.sem("mid_ready")
        tile_ready = st.sem("tile_ready")
        tile_stored = [st.sem(f"tile_stored{k}") for k in range(2)]
        v_ready = st.sem("v_ready")
        v_copied = st.sem("v_copied")
        v_stored = [st.sem(f"v_stored{u}") for u in range(2)]
        dve_self = st.sem("dve_self")
        assert J % 2 == 0
        terms = [(c, a, b) for c in range(KC) for a, b in PAIRS]
        block = st.ctx.enter_context(nc.Block())

        @block.sync
        def _(sp):
            sp.dma_start(wf[:], w.rearrange("(c p) n -> p c n", p=P)).then_inc(consts_in, 16)
            if rope:
                for t, src in zip((perm, cos, sin), rope):
                    sp.dma_start(t[:], src).then_inc(consts_in, 16)

            def load(i, u):
                sp.dma_start(xT[:, u], xnT[:, :, bass.ds((i * 2 + u) * CH, CH)]).then_inc(x_in[u], 16)
            ready, credits = (tile_ready, 2) if parts else (f_ready, 2) if rope else (q_copied, 2)

            def body(i, more):
                for u in range(2):
                    n = i * 2 + u
                    if more:
                        sp.wait_ge(x_ready, n + 1)
                        load(i + 1, u)
                    for j in range(J):
                        sp.wait_ge(ready, n * J + (j + 1 + credits))
                        sp.dma_start(qk_out(i, u, j), part[:, j] if parts else fin[:, j % 2]).then_inc(tile_stored[j % 2], 16)
                    sp.wait_ge(v_copied, (n + 1) * VS + 2)
                    for lo, hi, dst in v_out(i, u):
                        sp.dma_start(dst, vs[:, u, lo:hi, :].rearrange("p t (c n) -> p t c n", n=P)).then_inc(v_stored[u], 16)
            load(0, 0)
            load(0, 1)
            with sp.Fori(0, B - 1) as i:
                body(i, True)
            body(B - 1, False)
            for k in range(2):
                sp.wait_ge(tile_stored[k], 16 * B * J)
                sp.wait_ge(v_stored[k], 16 * VD * B)

        @block.tensor
        def _(pe):
            pe.sem_inc(x_free, 2)
            pe.wait_ge(consts_in, 64 if rope else 16)
            pe.wait_ge(w_ready, 1)

            def rotate(n, j):
                m = n * J + j
                pe.wait_ge(q_copied, m + 3)
                pe.wait_ge(f_ready, m + 1)
                pe.matmul(RP[j % 2][:], perm[:], qs[:, j % 2], start=True, stop=True).then_inc(r_ready, 1)

            with pe.Fori(0, B) as i:
                for u in range(2):
                    n = i * 2 + u
                    pe.wait_ge(x_ready, n + 1)
                    for j in range(J):
                        pe.wait_ge(q_copied, n * J + j + 1)
                        for term in terms:
                            c, a, b = term
                            last = pe.matmul(QP[j % 2][:], wt[a][:, c, j * P:(j + 1) * P], xs[b][:, u, c, :],
                                             start=term == terms[0], stop=term == terms[-1])
                        last.then_inc(q_ready, 1)
                        if rope and j:
                            rotate(n, j - 1)
                    for k in range(VS):
                        pe.wait_ge(v_copied, n * VS + k + 1)
                        for h in range(2):
                            t, b = divmod(k * 2 + h, VB)
                            for term in terms:
                                c, x, y = term
                                last = pe.matmul(VP[k % 2][:, h * 256:(h + 1) * 256], xs[x][:, u, c, t * P:(t + 1) * P],
                                                 wt[y][:, c, J * P + b * 256:J * P + (b + 1) * 256],
                                                 start=term == terms[0], stop=term == terms[-1])
                        last.then_inc(v_ready, 1)
                        if rope and k == 0:
                            rotate(n, J - 1)
                    pe.wait_ge(v_ready, (n + 1) * VS)
                    pe.sem_inc(x_free, 1)

        @block.scalar
        def _(act):
            act.sem_inc(q_copied, 2)

            def split(i, u):
                act.wait_ge(x_in[u], (i + 1) * 16)
                act.wait_ge(x_free, i * 2 + u + 1)
                act.copy(xs[0][:, u], xT[:, u]).then_inc(xh_ready, 1)

            def body(i, more):
                for u in range(2):
                    n = i * 2 + u
                    if u == 0 or more:
                        split(*((i, 1) if u == 0 else (i + 1, 0)))

                    def high(j):
                        m = n * J + j
                        if rope:
                            act.wait_ge(f_ready, m + 3)
                        else:
                            act.wait_ge(q_copied, m + 3)
                        act.wait_ge(tile_stored[j % 2], n * (16 * J // 2))
                        act.copy(part[:, j, 0, :], fin[:, j]).then_inc(hi_ready, 1)

                    def mid(j):
                        act.wait_ge(r1_ready, n * J + j + 1)
                        act.copy(part[:, j, 1, :], rest[:, j]).then_inc(mid_ready, 1)

                    for j in range(J + (2 if parts else 0)):
                        if j < J:
                            m = n * J + j
                            act.wait_ge(q_ready, m + 1)
                            if rope:
                                act.wait_ge(f_ready, m + 1)
                                act.wait_ge(cos_ready, m + 1)
                            elif not parts:
                                act.wait_ge(tile_stored[j % 2], (n * (J // 2) + j // 2) * 16)
                            dst = qs if (rope or parts) else fin
                            ins = act.activation(dst[:, j % QS], QP[j % 2][:], ACT.Copy, scale=q_scale if j < q_tiles else 1.0)
                            ins.then_inc(q_copied, 1)
                        if parts and 1 <= j <= J:
                            high(j - 1)
                        if parts and j >= 2:
                            mid(j - 2)
                    act.wait_ge(v_stored[u], i * (16 * VD))
                    for k in range(VS):
                        act.wait_ge(v_ready, n * VS + k + 1)
                        act.copy(vs[:, u].rearrange("p t n -> p (t n)")[:, k * 512:(k + 1) * 512], VP[k % 2][:]).then_inc(v_copied, 1)
            split(0, 0)
            act.wait_ge(consts_in, 64 if rope else 16)
            act.copy(wt[0][:], wf[:]).then_inc(wh_ready, 1)
            with act.Fori(0, B - 1) as i:
                body(i, True)
            body(B - 1, False)

        @block.vector
        def _(dve):
            dve.sem_inc(f_ready, 2)
            dve.sem_inc(tile_ready, 2)
            per = 1 if rope else 0

            def split(i, u):
                dve.wait_ge(xh_ready, i * 2 + u + 1)
                dve.tensor_tensor(xs[1][:, u], xT[:, u], xs[0][:, u], ALU.subtract).then_inc(x_ready, 1)

            def body(i, more):
                link = Chain(dve, dve_self, i * (2 * J * per))
                for u in range(2):
                    n = i * 2 + u
                    if u == 0 or more:
                        split(*((i, 1) if u == 0 else (i + 1, 0)))
                    for j in range(J + (2 if parts else 0)):
                        m, k = n * J + j, j % 2
                        if rope and j < J:
                            dve.wait_ge(r_ready, m + 1)
                            half = sin[:, u * CH:(u + 1) * CH]
                            link(dve.tensor_tensor(ts[:, k], RP[k][:], half, ALU.mult))
                            dve.wait_ge(cos_ready, m + 3)
                            if not parts:
                                dve.wait_ge(tile_stored[k], (n * (J // 2) + j // 2) * 16)
                            dve.tensor_tensor(fin[:, j % FS], tc[:, k], ts[:, k], ALU.add).then_inc(f_ready, 1)
                        if parts and 1 <= j <= J:
                            dve.wait_ge(hi_ready, m - 1 + 1)
                            dve.tensor_tensor(rest[:, j - 1], fin[:, j - 1], part[:, j - 1, 0, :], ALU.subtract).then_inc(r1_ready, 1)
                        if parts and j >= 2:
                            dve.wait_ge(mid_ready, m - 2 + 1)
                            dve.tensor_tensor(part[:, j - 2, 2, :], rest[:, j - 2], part[:, j - 2, 1, :], ALU.subtract).then_inc(tile_ready, 1)

            split(0, 0)
            dve.wait_ge(wh_ready, 1)
            dve.tensor_tensor(wt[1][:], wf[:], wt[0][:], ALU.subtract).then_inc(w_ready, 1)
            with dve.Fori(0, B - 1) as i:
                body(i, True)
            body(B - 1, False)

        @block.gpsimd
        def _(pool):
            pool.sem_inc(cos_ready, 2)
            pool.sem_inc(v_copied, 2)
            if not rope:
                return
            with pool.Fori(0, B) as i:
                for u in range(2):
                    for j in range(J):
                        m, k = (i * 2 + u) * J + j, j % 2
                        pool.wait_ge(q_copied, m + 3)
                        pool.wait_ge(f_ready, m + 1)
                        pool.tensor_tensor(tc[:, k], qs[:, k], cos[:, u * CH:(u + 1) * CH], ALU.mult).then_inc(cos_ready, 1)


def attention_stage(nc, name, consts, qT, kT, v, out, units, heads, kc, dv, causal):
    st = Stage(nc, name)
    with st.ctx:
        qt = st.sb("q", [P, 2, heads, kc, S])
        kt = st.sb("k", [P, 2, kc, S])
        qp = [st.sb(f"qp{x}", [P, 2, heads, kc, S], F32R) for x in range(2)]
        kp = [st.sb(f"kp{x}", [P, 2, kc, S], F32R) for x in range(2)]
        vt = st.sb("v", [P, 2, QB, dv])
        ident = st.sb("ident", [P, P])
        if causal:
            identb = st.sb("identb", [P, P], BF16)
            mask = st.sb("mask", [P, P], BF16)
        prob = st.sb("prob", [P, 2, S])
        pT = st.sb("pT", [P, 2, QB, P])
        nmax = st.sb("nmax", [P, 2])
        rsum = st.sb("rsum", [P, 4])
        rinv = st.sb("rinv", [P, 2])
        ot = st.sb("o", [P, 2, dv])
        SC = [st.ps(f"SC{k}", (P, S)) for k in range(2)]
        T = [st.ps(f"T{k}") for k in range(2)]
        O = [st.ps(f"O{k}", (P, dv)) for k in range(2)]
        consts_in = st.sem("consts_in")
        loaded = [st.sem(f"loaded{u}") for u in range(2)]
        unit_free = st.sem("unit_free")
        hi_ready = st.sem("hi_ready")
        lo_ready = st.sem("lo_ready")
        s_ready = st.sem("s_ready")
        m_ready = st.sem("m_ready")
        p_ready = st.sem("p_ready")
        t_ready = st.sem("t_ready")
        a_copied = st.sem("a_copied")
        d_copied = st.sem("d_copied")
        o_ready = st.sem("o_ready")
        o_used = st.sem("o_used")
        stored = [st.sem(f"stored{k}") for k in range(2)]
        dve_self = st.sem("dve_self")
        order = [0, 7, 1, 6, 2, 5, 3, 4] if causal else list(range(QB))
        blocks = [(qb + 1 if causal else QB) for qb in order]
        NS = 2 * heads * QB
        nb = [blocks[s % QB] for s in range(NS)]
        ng = [(b + 3) // 4 for b in nb]
        gbase = [sum(ng[:s]) for s in range(NS + 1)]
        acount = [sum(1 for g in range(gbase[s]) if g % 2 == 0) for s in range(NS + 1)]
        dcount = [sum(1 for g in range(gbase[s]) if g % 2 == 1) for s in range(NS + 1)]
        assert gbase[NS] % 2 == 0
        A, DC = acount[NS], dcount[NS]
        TC = ng[NS - 1]
        SU = heads * QB
        R = heads + 1
        SPLIT_AT = SU * 3 // 8

        def to_cut(u, r):
            if r < heads:
                return qt[:, u, r], qp[0][:, u, r], qp[1][:, u, r]
            return kt[:, u], kp[0][:, u], kp[1][:, u]
        block = st.ctx.enter_context(nc.Block())

        @block.sync
        def _(sp):
            sp.dma_start(ident[:], consts["ident"]).then_inc(consts_in, 16)
            if causal:
                sp.dma_start(identb[:], consts["identb"]).then_inc(consts_in, 16)
                sp.dma_start(mask[:], consts["mask"]).then_inc(consts_in, 16)
            def load(i, u):
                n = i * 2 + u
                sp.wait_ge(unit_free, n + 1)
                for h in range(heads):
                    sp.dma_start(qt[:, u, h], one(qT, n)[:, h].rearrange("a (c p) t -> p (a c) t", p=P)).then_inc(loaded[u], 16)
                sp.dma_start(kt[:, u], one(kT, n).rearrange("a (c p) t -> p (a c) t", p=P)).then_inc(loaded[u], 16)
                sp.dma_start(vt[:, u], one(v, n).rearrange("a (b p) n -> p (a b) n", p=P)).then_inc(loaded[u], 16)
            for u in range(2):
                load(0, u)

            def body(i, more):
                for s in range(NS):
                    u, h, qb = s // (heads * QB), s // QB % heads, order[s % QB]
                    k = s % 2
                    sp.wait_ge(o_used, i * NS + s + 1 + 2)
                    sp.dma_start(one(out, i * 2 + u)[:, h, qb * P:(qb + 1) * P, :].rearrange("a p n -> (a p) n"),
                                 ot[:, k]).then_inc(stored[k], 16)
                    if more and (s + 1) % (heads * QB) == 0:
                        load(i + 1, u)
            with sp.Fori(0, units // 2 - 1) as i:
                body(i, True)
            body(units // 2 - 1, False)
            for k in range(2):
                sp.wait_ge(stored[k], 16 * (units // 2) * (NS // 2))

        @block.tensor
        def _(pe):
            pe.sem_inc(unit_free, 2)
            pe.wait_ge(consts_in, 48 if causal else 16)

            def scores(i, s):
                n, k = i * NS + s, s % 2
                u, h, qb = s // (heads * QB), s // QB % heads, order[s % QB]
                if s % (heads * QB) == 0:
                    pe.wait_ge(loaded[u], (i + 1) * (16 * (heads + 2)))
                    pe.wait_ge(lo_ready, (i * 2 + u + 1) * R)
                pe.wait_ge(p_ready, n + 1)
                w = nb[s] * P
                for lo in range(0, w, 512):
                    hi = min(w, lo + 512)
                    last_part = causal and hi == w
                    cut = hi - lo > P
                    terms = [(c, x, y) for c in range(kc) for x, y in (PAIRS if cut else [(0, 0)])]
                    for term in terms:
                        c, x, y = term
                        q, key = (qp[x], kp[y]) if cut else (qt, kt)
                        last = pe.matmul(SC[k][:, lo:hi], q[:, u, h, c, qb * P:(qb + 1) * P], key[:, u, c, lo:hi],
                                         start=term == terms[0], stop=term == terms[-1] and not last_part)
                    if last_part:
                        last = pe.matmul(SC[k][:, w - P:w], identb[:], mask[:], start=False, stop=True)
                last.then_inc(s_ready, 1)

            def transposes(i, s):
                n, k = i * NS + s, s % 2
                pe.wait_ge(p_ready, n + 1 + 2)
                for g in range(ng[s]):
                    m = gbase[s] + g
                    if m % 2 == 0:
                        pe.wait_ge(a_copied, i * A + m // 2 + 1)
                    else:
                        pe.wait_ge(d_copied, i * DC + m // 2 + 1)
                    for b in range(g * 4, min(nb[s], g * 4 + 4)):
                        last = pe.transpose(T[m % 2][:, b % 4 * P:(b % 4 + 1) * P], prob[:, k, b * P:(b + 1) * P], ident[:])
                    last.then_inc(t_ready, 1)

            def values(i, s):
                n, k = i * NS + s, s % 2
                u = s // (heads * QB)
                pe.wait_ge(a_copied, i * A + acount[s + 1] + 1)
                pe.wait_ge(d_copied, i * DC + dcount[s + 1] + 1)
                pe.wait_ge(o_used, n + 1)
                for b in range(nb[s]):
                    last = pe.matmul(O[k][:], pT[:, k, b, :], vt[:, u, b, :], start=(b == 0), stop=(b == nb[s] - 1))
                last.then_inc(o_ready, 1)
                if (s + 1) % (heads * QB) == 0:
                    pe.wait_ge(o_ready, n + 1 + 2)
                    pe.sem_inc(unit_free, 1)

            def ahead(part, i, s, more):
                if s < NS:
                    part(i, s)
                elif more:
                    part(i + 1, s - NS)

            def body(i, more):
                for s in range(NS):
                    ahead(scores, i, s + 2, more)
                    ahead(transposes, i, s + 1, more)
                    values(i, s)
            pe.sem_inc(o_ready, 2)
            pe.sem_inc(t_ready, TC)
            scores(0, 0)
            scores(0, 1)
            transposes(0, 0)
            with pe.Fori(0, units // 2 - 1) as i:
                body(i, True)
            body(units // 2 - 1, False)

        @block.scalar
        def _(act):
            act.sem_inc(p_ready, 2)
            act.sem_inc(a_copied, 1)

            def cut(i, u, r):
                if r == 0:
                    act.wait_ge(loaded[u], (i + 1) * (16 * (heads + 2)))
                    act.wait_ge(unit_free, i * 2 + u + 1)
                whole, high, _ = to_cut(u, r)
                act.copy(high, whole).then_inc(hi_ready, 1)

            def exps(i, s):
                n, k = i * NS + s, s % 2
                act.wait_ge(m_ready, n + 1)
                act.wait_ge(t_ready, i * (A + DC) + (gbase[s - 1] + TC if s else 0))
                act.activation(prob[:, k, 0:nb[s] * P], SC[k][:, 0:nb[s] * P], ACT.Exp, bias=nmax[:, k:k + 1],
                               accum_out=rsum[:, s % 4:s % 4 + 1]).then_inc(p_ready, 1)

            def copies(i, s):
                act.wait_ge(o_ready, i * NS + s + 1)
                for g in range(ng[s]):
                    m = gbase[s] + g
                    if m % 2 == 0:
                        lo, hi = g * 4, min(nb[s], g * 4 + 4)
                        act.wait_ge(t_ready, i * (A + DC) + m + 1 + TC)
                        act.copy(pT[:, s % 2, lo:hi, :].rearrange("p b q -> p (b q)"), T[0][:, 0:(hi - lo) * P]).then_inc(a_copied, 1)

            def ahead(part, i, s, more):
                if s < NS:
                    part(i, s)
                elif more:
                    part(i + 1, s - NS)

            def body(i, more):
                for s in range(NS):
                    ahead(exps, i, s + 2, more)
                    ahead(copies, i, s + 1, more)
                    r = s % SU - SPLIT_AT
                    if 0 <= r < R and (s < SU or more):
                        cut(*((i, 1) if s < SU else (i + 1, 0)), r)
            for r in range(R):
                cut(0, 0, r)
            exps(0, 0)
            exps(0, 1)
            copies(0, 0)
            with act.Fori(0, units // 2 - 1) as i:
                body(i, True)
            body(units // 2 - 1, False)

        @block.vector
        def _(dve):
            dve.sem_inc(o_used, 2)
            dve.sem_inc(d_copied, 1)

            def maxima(i, s):
                n, k = i * NS + s, s % 2
                dve.wait_ge(s_ready, n + 1)
                dve.tensor_reduce(nmax[:, k:k + 1], SC[k][:, 0:nb[s] * P], AX, ALU.max, negate=True).then_inc(m_ready, 1)

            def copies(i, s):
                dve.wait_ge(o_ready, i * NS + s + 1)
                for g in range(ng[s]):
                    m = gbase[s] + g
                    if m % 2 == 1:
                        lo, hi = g * 4, min(nb[s], g * 4 + 4)
                        dve.wait_ge(t_ready, i * (A + DC) + m + 1 + TC)
                        dve.tensor_copy(pT[:, s % 2, lo:hi, :].rearrange("p b q -> p (b q)"), T[1][:, 0:(hi - lo) * P]).then_inc(d_copied, 1)

            def normalise(i, s):
                n, k = i * NS + s, s % 2
                dve.wait_ge(o_ready, n + 1 + 2)
                dve.reciprocal(rinv[:, k:k + 1], rsum[:, s % 4:s % 4 + 1]).then_inc(dve_self, 1)
                dve.wait_ge(dve_self, n + 1)
                dve.wait_ge(stored[k], i * (16 * (NS // 2)) + s // 2 * 16)
                dve.tensor_scalar(ot[:, k], O[k][:], rinv[:, k:k + 1], None, ALU.mult).then_inc(o_used, 1)

            def ahead(part, i, s, more):
                if s < NS:
                    part(i, s)
                elif more:
                    part(i + 1, s - NS)

            def body(i, more):
                for s in range(NS):
                    ahead(maxima, i, s + 2, more)
                    ahead(copies, i, s + 1, more)
                    normalise(i, s)
            for r in range(R):
                dve.wait_ge(hi_ready, r + 1)
                whole, high, low = to_cut(0, r)
                dve.tensor_tensor(low, whole, high, ALU.subtract).then_inc(lo_ready, 1)
            maxima(0, 0)
            maxima(0, 1)
            copies(0, 0)
            with dve.Fori(0, units // 2 - 1) as i:
                body(i, True)
            body(units // 2 - 1, False)

        @block.gpsimd
        def _(pool):
            def cut(i, u):
                for r in range(R):
                    pool.wait_ge(hi_ready, (i * 2 + u) * R + (r + 1))
                    whole, high, low = to_cut(u, r)
                    pool.tensor_tensor(low, whole, high, ALU.subtract).then_inc(lo_ready, 1)
            cut(0, 1)
            with pool.Fori(1, units // 2) as i:
                for u in range(2):
                    cut(i, u)


PART_PAIRS = [(0, 0), (0, 1), (0, 2), (1, 0), (1, 1), (2, 0)]
HG, DH = 4, 16
KR = len(PART_PAIRS) * DH
NR = 3
PIECES_AT = [3, 7, 6, 6, 4, 4, 4, 4]
LEAD = 14
VALUES_AT = 0.6
EARLY = 2


def narrow_attention_stage(nc, name, consts, q_parts, k_parts, v, out, m_rows, units):
    st = Stage(nc, name)
    with st.ctx:
        NU = 4
        qs = st.sb("qs", [P, NU, HG, S], BF16)
        ks = st.sb("ks", [P, NU, HG, S], BF16)
        vin = st.sb("vin", [P, 2, QB, HG * DH])
        vp = st.sb("vp", [P, 2, QB, HG, 32])
        pT = st.sb("pT", [P, 2, HG, S])
        ident = st.sb("ident", [P, P])
        identb = st.sb("identb", [P, P], BF16)
        mask = st.sb("mask", [P, P], BF16)
        maskT = st.sb("maskT", [P, P], BF16)
        pm = st.sb("pm", [P, HG, QB, 2])
        nm = st.sb("nm", [P, HG, QB])
        nr = st.sb("nr", [P, HG, QB])
        nb3 = st.sb("nb3", [P, HG, 3, QB], BF16)
        mt = st.sb("mt", [HG * 3 * QB, P], BF16)
        osb = st.sb("osb", [P, 2, 512])
        rinv = st.sb("rinv", [P, 4, HG, 1])
        on = st.sb("on", [P, 2, 4, HG, DH])
        SC = [st.ps(f"SC{k}") for k in range(2)]
        ST = [st.ps(f"ST{k}", (P, S)) for k in range(2)]
        OT = st.ps("OT", (P, S))
        consts_in = st.sem("consts_in")
        qk_loaded = [st.sem(f"qk_loaded{u}") for u in range(NU)]
        v_loaded = [st.sem(f"v_loaded{u}") for u in range(2)]
        m_stored = st.sem("m_stored")
        m_loaded = [st.sem(f"m_loaded{u}") for u in range(2)]
        unit_free = st.sem("unit_free")
        ones_set = st.sem("ones_set")
        vp_ready = st.sem("vp_ready")
        v_seen = st.sem("v_seen")
        sc_ready = st.sem("sc_ready")
        sc_used = st.sem("sc_used")
        parts_ready = st.sem("parts_ready")
        mt_ready = st.sem("mt_ready")
        st_ready = st.sem("st_ready")
        e_ready = st.sem("e_ready")
        av_ready = st.sem("av_ready")
        ot_copied = st.sem("ot_copied")
        on_ready = st.sem("on_ready")
        stored = [st.sem(f"stored{k}") for k in range(2)]
        dve_self = st.sem("dve_self")
        pieces = []
        for qb in range(QB):
            for lo in range(0, (qb + 1) * P, 512):
                hi = min((qb + 1) * P, lo + 512)
                nh = min(HG, 512 // (hi - lo))
                pieces += [(qb, lo, hi, j, nh) for j in range(0, HG, nh)]
        NP = len(pieces)
        PU = NP + 3
        steps = []
        for kb in range(QB):
            nh = min(HG, S // (S - kb * P)) if S - kb * P <= 256 else 2 if S - kb * P <= 512 else 1
            steps += [(kb, j, nh) for j in range(0, HG, nh)]
        NT = len(steps)
        done = [sum(1 for t in steps if t[0] < kb) for kb in range(QB + 1)]
        assert NT % len(ST) == 0 and (NU * PU) % len(SC) == 0

        shared, k = [], 0
        for kb in range(QB):
            shared.append([])
            for _ in range(PIECES_AT[kb]):
                shared[kb].append(("piece", 1, LEAD + k) if k < NP - LEAD else ("piece", 2, k - (NP - LEAD)))
                k += 1
                if k == NP - LEAD + 4:
                    shared[kb].append(("maxima", 1, 0))
        assert k == NP
        shared[QB - 1].append(("out", 0, 0))

        def events(kb, n_ahead):
            return [e for e in shared[kb] if e[1] <= n_ahead]

        def ahead_of(i, u, k):
            return (i, u + k) if u + k < NU else (i + 1, u + k - NU)

        def followers(u, more):
            return 2 if more else min(2, NU - 1 - u)

        START = NP + 1 + LEAD

        def skipped(u, more):
            return 0 if more or u < NU - 1 else LEAD

        def seq(i, u, more):
            start = START + u * PU - skipped(u, more)
            return SeqNumber(i * (NU * PU) + start, start, len(SC))

        def width(kb):
            return S - kb * P

        def st_view(t):
            kb, j, nh = steps[t]
            tile, w = ST[t % len(ST)], width(kb)
            if nh == 2:
                src = tile[:].rearrange("p (h w) -> p h w", h=2)[:, :, 0:w]
            else:
                src = tile[:, 0:nh * w].rearrange("p (h w) -> p h w", h=nh)
            return src, pT[:, kb % 2, j:j + nh, 0:w]

        def bank_of(q):
            return SC[q.rest] if isinstance(q, SeqNumber) else SC[q % len(SC)]
        block = st.ctx.enter_context(nc.Block())

        @block.sync
        def _(sp):
            def load_qk(i, u):
                n = i * NU + u
                sp.wait_ge(unit_free, n + 1)
                for r, (a, b) in enumerate(PART_PAIRS):
                    for dst, src, part in ((qs, q_parts, a), (ks, k_parts, b)):
                        sp.dma_start(dst[r * DH:(r + 1) * DH, u], src[part, bass.ds(n * (HG * DH), HG * DH), :].rearrange("(j r) t -> r j t", r=DH))\
                          .then_inc(qk_loaded[u], 16)

            def load_v(i, u):
                n = i * NU + u
                sp.wait_ge(vp_ready, n + 1)
                sp.dma_start(vin[:, u % 2], one(v, i)[:, :, u * HG * DH:(u + 1) * HG * DH].rearrange("a (b p) n -> p (a b) n", p=P)).then_inc(v_loaded[u % 2], 16)

            def store(i, u, h):
                n2 = (i * NU + u) * 2 + h
                sp.wait_ge(on_ready, n2 + 1)
                sp.dma_start(one(out, i)[:, h * 512:(h + 1) * 512, u * HG * DH:(u + 1) * HG * DH].rearrange("a (b p) n -> p (a b) n", p=P),
                             on[:, h].rearrange("p b j e -> p b (j e)")).then_inc(stored[h], 16)

            def maxima_rows(i, u):
                n = i * NU + u
                sp.wait_ge(mt_ready, n + 1)
                sp.dma_start(one(m_rows, n).rearrange("a j r (b t) -> (a j r b) t", t=P), mt[:]).then_inc(m_stored, 16)
                sp.wait_ge(m_stored, (n + 1) * 16)
                sp.dma_start(qs[KR:KR + NR, u], one(m_rows, n).rearrange("a j r t -> r (a j) t")).then_inc(m_loaded[u % 2], 16)

            def body(i, more):
                for u in range(NU):
                    if u + 1 < NU:
                        maxima_rows(i, u + 1)
                    elif more:
                        maxima_rows(i + 1, 0)
                    for h in range(2):
                        store(i, u, h)
                    if more:
                        load_qk(i + 1, u)
                    if u + 2 < NU:
                        load_v(i, u + 2)
                    elif more:
                        load_v(i + 1, u + 2 - NU)
            load_qk(0, 0)
            for t, key in ((ident, "ident"), (identb, "identb"), (mask, "mask"), (maskT, "maskT")):
                sp.dma_start(t[:], consts[key]).then_inc(consts_in, 16)
            load_qk(0, 1)
            load_v(0, 0)
            load_v(0, 1)
            for u in range(2, NU):
                load_qk(0, u)
            maxima_rows(0, 0)
            with sp.Fori(0, units // NU - 1) as i:
                body(i, True)
            body(units // NU - 1, False)
            for h in range(2):
                sp.wait_ge(stored[h], 16 * units)

        @block.gpsimd
        def _(pool):
            pool.sem_inc(vp_ready, 2)
            pool.sem_inc(unit_free, NU)
            pool.memset(ks[KR:P], 1.0).then_inc(ones_set, 1)
            pool.wait_ge(ones_set, 1)
            pool.memset(vp[:, :, :, :, DH + 1:32], 0.0).then_inc(ones_set, 1)
            pool.wait_ge(ones_set, 2)
            pool.memset(vp[:, :, :, :, DH:DH + 1], 1.0).then_inc(ones_set, 1)
            pool.wait_ge(ones_set, 3)
            with pool.Fori(0, units // 2) as i:
                for u in range(2):
                    n = i * 2 + u
                    pool.wait_ge(v_loaded[u], (i + 1) * 16)
                    pool.wait_ge(unit_free, n - 2 + 1 + NU)
                    pool.sem_inc(v_seen, 1)
                    pool.tensor_copy(vp[:, u, :, :, 0:DH], vin[:, u].rearrange("p b (j e) -> p b j e", j=HG)).then_inc(vp_ready, 1)

        @block.tensor
        def _(pe):
            pe.sem_inc(av_ready, 2)
            pe.wait_ge(consts_in, 64)

            def piece(i, u, p, q):
                qb, lo, hi, j0, nh = pieces[p]
                if p == 0:
                    pe.wait_ge(qk_loaded[u], (i + 1) * (16 * 2 * len(PART_PAIRS)))
                pe.wait_ge(sc_used, count(q + 1))
                w, diag = hi - lo, hi == (qb + 1) * P
                for j in range(j0, j0 + nh):
                    bank = bank_of(q)[:, (j - j0) * w:(j - j0 + 1) * w]
                    last = pe.matmul(bank, qs[0:KR, u, j, qb * P:(qb + 1) * P], ks[0:KR, u, j, lo:hi], start=True, stop=not diag)
                    if diag:
                        last = pe.matmul(bank[:, w - P:w], identb[:], mask[:], start=False, stop=True)
                last.then_inc(sc_ready, 1)

            def maxima_transpose(unit, q):
                pe.wait_ge(parts_ready, unit + 1)
                pe.wait_ge(sc_used, count(q + 1))
                bank = bank_of(q)[0:HG * NR * QB, 0:P // 2].bitcast(BF16)
                pe.transpose(bank, nb3[:].rearrange("p j r b -> p (j r b)"), identb[:]).then_inc(sc_ready, 1)

            def out_transpose(n, h, q):
                pe.wait_ge(ot_copied, n * 2 + h + 1)
                pe.wait_ge(sc_used, count(q + 1))
                for b in range(4):
                    last = pe.transpose(bank_of(q)[:, b * P:(b + 1) * P], osb[:, h, b * P:(b + 1) * P], ident[:])
                last.then_inc(sc_ready, 1)

            def step(n, u, t):
                kb, j0, nh = steps[t]
                pe.wait_ge(e_ready, n * NT + t + 1)
                src = st_view(t)[0]
                for j in range(j0, j0 + nh):
                    for lo in range(0, width(kb), 512):
                        hi = min(width(kb), lo + 512)
                        last = pe.matmul(src[:, j - j0, lo:hi], ks[0:KR + NR, u, j, kb * P:(kb + 1) * P],
                                         qs[0:KR + NR, u, j, kb * P + lo:kb * P + hi], start=True, stop=lo > 0)
                        if lo == 0:
                            last = pe.matmul(src[:, j - j0, 0:P], identb[:], maskT[:], start=False, stop=True)
                last.then_inc(st_ready, 1)

            def values(n, u, kb, h):
                if h == first_half(kb):
                    pe.wait_ge(e_ready, n * NT + done[kb + 1] + len(ST))
                    if kb == 0:
                        pe.wait_ge(vp_ready, n + 1 + 2)
                        pe.wait_ge(ot_copied, n * 2)
                lo, hi = max(kb * P, h * 512), (h + 1) * 512
                for j in range(HG):
                    last = pe.matmul(OT[32 * j:32 * j + 32, lo:hi], vp[:, u % 2, kb, j, :],
                                     pT[:, kb % 2, j, lo - kb * P:hi - kb * P],
                                     start=(kb == 0), stop=(kb == 4 * h + 3))
                if h == 1:
                    last.then_inc(av_ready, 1)

            def first_half(kb):
                return 0 if kb < 4 else 1

            def early_steps(i, u):
                pe.wait_ge(m_loaded[u % 2], (i * (NU // 2) + u // 2 + 1) * 16)
                for t in range(EARLY):
                    step(i * NU + u, u, t)

            def unit(i, u, more):
                n, n_ahead = i * NU + u, followers(u, more)
                q = seq(i, u, more)
                for kb in range(QB):
                    own = done[kb + 1] - done[kb]
                    work = [(k / own, "step", done[kb] + k) for k in range(own)]
                    if kb:
                        halves = range(first_half(kb - 1), 2)
                        work += [((k + VALUES_AT) / len(halves), "values", h) for k, h in enumerate(halves)]
                    work = [w[1:] for w in sorted(work)]
                    mine = events(kb, n_ahead)
                    for k, (kind, x) in enumerate(work):
                        if kind == "values":
                            values(n, u, kb - 1, x)
                        elif x >= EARLY:
                            step(n, u, x)
                        for what, a, p in mine[len(mine) * k // len(work):len(mine) * (k + 1) // len(work)]:
                            if what == "piece":
                                piece(*ahead_of(i, u, a), p, q)
                            elif what == "maxima":
                                maxima_transpose(n + 1, q)
                            else:
                                out_transpose(n, 0, q)
                            q = q + 1
                values(n, u, QB - 1, 1)
                if n_ahead:
                    early_steps(*ahead_of(i, u, 1))
                out_transpose(n, 1, q)
                pe.wait_ge(av_ready, (n + 1) * QB + 2)
                pe.sem_inc(unit_free, 1)

            for p in range(NP):
                piece(0, 0, p, p)
            for p in range(LEAD):
                if p == LEAD // 2:
                    maxima_transpose(0, NP + p)
                piece(0, 1, p, NP + p + (p >= LEAD // 2))
            pe.wait_ge(ones_set, 3)
            early_steps(0, 0)

            def body(i, more):
                for u in range(NU):
                    unit(i, u, more)
            with pe.Fori(0, units // NU - 1) as i:
                body(i, True)
            body(units // NU - 1, False)

        @block.scalar
        def _(act):
            act.sem_inc(e_ready, len(ST))

            def unit(i, u, more):
                n = i * NU + u
                seen = START + n * PU - skipped(u, more)
                for kb in range(QB):
                    act.wait_ge(av_ready, n * QB + kb + 1)
                    for t in range(done[kb], done[kb + 1]):
                        src, dst = st_view(t)
                        act.wait_ge(st_ready, n * NT + t + 1)
                        act.activation(dst, src, ACT.Exp).then_inc(e_ready, 1)
                    if kb == 5:
                        copy(n, 0, seen)
                copy(n, 1, seen)

            def copy(n, h, seen):
                act.wait_ge(av_ready, n * QB + 4 * (h + 1) + 2)
                act.wait_ge(sc_ready, seen - 1 + h)
                act.copy(osb[:, h], OT[:, h * 512:(h + 1) * 512]).then_inc(ot_copied, 1)

            def body(i, more):
                for u in range(NU):
                    unit(i, u, more)
            with act.Fori(0, units // NU - 1) as i:
                body(i, True)
            body(units // NU - 1, False)

        @block.vector
        def _(dve):
            dve.memset(pm[:], NEG).then_inc(dve_self, 1)
            dve.wait_ge(dve_self, 1)
            dve.sem_inc(sc_used, len(SC))

            def piece_max(p, q):
                qb, lo, hi, j, nh = pieces[p]
                dve.wait_ge(sc_ready, count(q + 1))
                src = bank_of(q)[:, 0:nh * (hi - lo)].rearrange("p (h w) -> p h w", h=nh)
                dve.tensor_reduce(pm[:, j:j + nh, qb, lo // 512:lo // 512 + 1], src, AX, ALU.max).then_inc(sc_used, 1)

            def maxima(unit, q, link):
                dve.wait_ge(sc_used, count(q + 1) + len(SC))
                link(dve.tensor_reduce(nm[:], pm[:], AX, ALU.max, negate=True))
                link(dve.tensor_copy(nb3[:, :, 0, :], nm[:]))
                link(dve.tensor_tensor(nr[:], nm[:], nb3[:, :, 0, :], ALU.subtract))
                link(dve.tensor_copy(nb3[:, :, 1, :], nr[:]))
                dve.tensor_tensor(nb3[:, :, 2, :], nr[:], nb3[:, :, 1, :], ALU.subtract).then_inc(parts_ready, 1)

            def maxima_copy(unit, q):
                dve.wait_ge(sc_ready, count(q + 1))
                dve.wait_ge(m_stored, unit * 16)
                dve.tensor_copy(mt[:], bank_of(q)[0:HG * NR * QB, 0:P // 2].bitcast(BF16)).then_inc(mt_ready, 1)
                dve.wait_ge(mt_ready, unit + 1)
                dve.sem_inc(sc_used, 1)

            def normalise(n, h, q, link):
                dve.wait_ge(sc_ready, count(q + 1))
                o = bank_of(q)[:].rearrange("p (b j e) -> p b j e", b=4, j=HG)
                link(dve.reciprocal(rinv[:], o[:, :, :, DH:DH + 1]))
                dve.wait_ge(stored[h], n * 16)
                dve.tensor_tensor(on[:, h], o[:, :, :, 0:DH], rinv[:].broadcast_to([P, 4, HG, DH]), ALU.mult).then_inc(on_ready, 1)
                dve.wait_ge(on_ready, n * 2 + h + 1)
                dve.sem_inc(sc_used, 1)

            link = Chain(dve, dve_self, 1)
            for p in range(NP):
                piece_max(p, p)
            maxima(0, NP - 1, link)
            for p in range(LEAD):
                if p == LEAD // 2:
                    maxima_copy(0, NP + p)
                piece_max(p, NP + p + (p >= LEAD // 2))

            def body(i, more):
                for u in range(NU):
                    n = i * NU + u
                    q = seq(i, u, more)
                    link = Chain(dve, dve_self, n * 6 + 5)
                    for kb in range(QB):
                        for what, a, p in events(kb, followers(u, more)):
                            if what == "piece":
                                piece_max(p, q)
                                if p == NP - 1:
                                    maxima(n + 1, q, link)
                            elif what == "maxima":
                                maxima_copy(n + 1, q)
                            else:
                                normalise(n, 0, q, link)
                            q = q + 1
                    normalise(n, 1, q, link)
            with dve.Fori(0, units // NU - 1) as i:
                body(i, True)
            body(units // NU - 1, False)


HID = 768
DEQUANT = float(np.float32(1.0 / 127.0))


def swiglu_stage(nc, name, xnT, w_gate, w_up, w_down, g_out):
    st = Stage(nc, name)
    with st.ctx:
        M = HID // P
        xT = st.sb("xT", [P, 2, KC, CH])
        xs = [st.sb(f"x{k}", [P, 2, KC, CH], F32R) for k in range(2)]
        wgi = st.sb("wgi", [P, KC, HID], I32)
        wui = st.sb("wui", [P, KC, HID], I32)
        wdi = st.sb("wdi", [P, M, D], I32)
        wf = [st.sb(f"wf{k}", [P, KC * HID]) for k in range(3)]
        wg = [st.sb(f"wg{k}", [P, KC, HID], F32R) for k in range(2)]
        wu = [st.sb(f"wu{k}", [P, KC, HID], F32R) for k in range(2)]
        wd = [st.sb(f"wd{k}", [P, M, D], F32R) for k in range(2)]
        sg = st.sb("sg", [P, 2, CH])
        h = st.sb("h", [P, 2, CH])
        hs = [st.sb(f"h{k}", [P, 2, M, CH], F32R) for k in range(2)]
        go = st.sb("go", [P, 2, TT, D])
        G = [st.ps(f"G{k}") for k in range(2)]
        U = [st.ps(f"U{k}") for k in range(2)]
        DN = [st.ps(f"D{k}") for k in range(2)]
        w_in = [st.sem(f"w_in{k}") for k in range(3)]
        wf_ready = st.sem("wf_ready")
        wh_ready = st.sem("wh_ready")
        w_ready = st.sem("w_ready")
        x_in = [st.sem(f"x_in{u}") for u in range(2)]
        x_free = st.sem("x_free")
        xh_ready = st.sem("xh_ready")
        x_ready = st.sem("x_ready")
        gu_ready = st.sem("gu_ready")
        sg_ready = st.sem("sg_ready")
        h_ready = st.sem("h_ready")
        hh_ready = st.sem("hh_ready")
        hl_ready = st.sem("hl_ready")
        dn_ready = st.sem("dn_ready")
        go_ready = st.sem("go_ready")
        stored = [st.sem(f"stored{u}") for u in range(2)]
        block = st.ctx.enter_context(nc.Block())

        @block.sync
        def _(sp):
            sp.dma_start(xT[:, 0], xnT[:, :, 0:CH]).then_inc(x_in[0], 16)
            for k, (dst, src) in enumerate(((wgi, w_gate), (wui, w_up), (wdi, w_down))):
                sp.dma_start(dst[:], src.rearrange("(c p) n -> p c n", p=P)).then_inc(w_in[k], 16)
            sp.dma_start(xT[:, 1], xnT[:, :, CH:2 * CH]).then_inc(x_in[1], 16)

            def body(i, more):
                for u in range(2):
                    if more:
                        sp.wait_ge(x_ready, i * 2 + u + 1)
                        sp.dma_start(xT[:, u], xnT[:, :, bass.ds(((i + 1) * 2 + u) * CH, CH)]).then_inc(x_in[u], 16)
                for u in range(2):
                    sp.wait_ge(go_ready, (i * 2 + u + 1) * 2 + 2)
                    sp.dma_start(one(g_out, i * 2 + u).rearrange("c p t d -> p (c t) d"), go[:, u]).then_inc(stored[u], 16)
            with sp.Fori(0, B - 1) as i:
                body(i, True)
            body(B - 1, False)
            for u in range(2):
                sp.wait_ge(stored[u], 16 * B)

        @block.tensor
        def _(pe):
            pe.sem_inc(x_free, 2)
            pe.wait_ge(w_ready, 2)
            with pe.Fori(0, B) as i:
                for u in range(2):
                    n = i * 2 + u
                    pe.wait_ge(x_ready, n + 1)
                    for m in range(M):
                        pe.wait_ge(h_ready, n * M + m + 1)
                        for bank, w in ((G, wg), (U, wu)):
                            terms = [(c, a, b) for c in range(KC) for a, b in PAIRS]
                            for c, a, b in terms:
                                last = pe.matmul(bank[m % 2][:], w[a][:, c, m * P:(m + 1) * P], xs[b][:, u, c, :],
                                                 start=(c, a, b) == terms[0], stop=(c, a, b) == terms[-1])
                        last.then_inc(gu_ready, 1)
                    pe.wait_ge(gu_ready, (n + 1) * M)
                    pe.sem_inc(x_free, 1)
                for u in range(2):
                    n = i * 2 + u
                    pe.wait_ge(w_ready, 3)
                    pe.wait_ge(hl_ready, (n + 1) * M + 2)
                    for k in range(2):
                        pe.wait_ge(go_ready, n * 2 + k + 1)
                        for t in (2 * k, 2 * k + 1):
                            terms = [(m, a, b) for m in range(M) for a, b in PAIRS]
                            for m, a, b in terms:
                                last = pe.matmul(DN[k][:, t % 2 * D:(t % 2 + 1) * D], hs[a][:, u, m, t * P:(t + 1) * P], wd[b][:, m, :],
                                                 start=(m, a, b) == terms[0], stop=(m, a, b) == terms[-1])
                        last.then_inc(dn_ready, 1)

        @block.scalar
        def _(act):
            act.sem_inc(go_ready, 2)

            def split(i, u):
                act.wait_ge(x_in[u], (i + 1) * 16)
                act.wait_ge(x_free, i * 2 + u + 1)
                act.copy(xs[0][:, u].rearrange("p c t -> p (c t)"), xT[:, u].rearrange("p c t -> p (c t)")).then_inc(xh_ready, 1)

            def high(n, u, m):
                if m == 0:
                    act.wait_ge(dn_ready, n * 2 - u * 2)
                act.wait_ge(h_ready, n * M + m + 1 + 2)
                act.copy(hs[0][:, u, m, :], h[:, m % 2]).then_inc(hh_ready, 1)

            def body(i, more):
                for u in range(2):
                    n = i * 2 + u
                    for m in range(M):
                        act.wait_ge(gu_ready, n * M + m + 1)
                        act.wait_ge(h_ready, n * M + m + 1)
                        act.activation(sg[:, m % 2], G[m % 2][:], ACT.Silu).then_inc(sg_ready, 1)
                        if m:
                            high(n, u, m - 1)
                    high(n, u, M - 1)
                    if more:
                        split(i + 1, u)
                for u in range(2):
                    n = i * 2 + u
                    act.wait_ge(stored[u], i * 16)
                    for k in range(2):
                        act.wait_ge(dn_ready, n * 2 + k + 1)
                        act.activation(go[:, u, 2 * k:2 * k + 2, :].rearrange("p t d -> p (t d)"), DN[k][:], ACT.Silu).then_inc(go_ready, 1)
            split(0, 0)
            for k, w in enumerate((wg, wu, wd)):
                act.wait_ge(wf_ready, k + 1)
                act.copy(w[0][:].rearrange("p a b -> p (a b)"), wf[k][:]).then_inc(wh_ready, 1)
            split(0, 1)
            with act.Fori(0, B - 1) as i:
                body(i, True)
            body(B - 1, False)

        @block.vector
        def _(dve):
            def split(i, u):
                dve.wait_ge(xh_ready, i * 2 + u + 1)
                dve.tensor_tensor(xs[1][:, u], xT[:, u], xs[0][:, u], ALU.subtract).then_inc(x_ready, 1)

            def body(i, more):
                for u in range(2):
                    n = i * 2 + u
                    for m in range(M):
                        dve.wait_ge(sg_ready, n * M + m + 1)
                        dve.wait_ge(hl_ready, n * M + m + 1)
                        dve.tensor_tensor(h[:, m % 2], U[m % 2][:], sg[:, m % 2], ALU.mult).then_inc(h_ready, 1)
                    if more:
                        split(i + 1, u)
            def scale(k):
                dve.wait_ge(w_in[k], 16)
                dve.tensor_scalar(wf[k][:], (wgi, wui, wdi)[k][:].rearrange("p a b -> p (a b)"), DEQUANT, None, ALU.mult)\
                   .then_inc(wf_ready, 1)

            def low(k):
                w = (wg, wu, wd)[k]
                dve.wait_ge(wh_ready, k + 1)
                dve.tensor_tensor(w[1][:].rearrange("p a b -> p (a b)"), wf[k][:], w[0][:].rearrange("p a b -> p (a b)"),
                                  ALU.subtract).then_inc(w_ready, 1)
            scale(0)
            split(0, 0)
            scale(1)
            low(0)
            low(1)
            scale(2)
            low(2)
            split(0, 1)
            dve.sem_inc(h_ready, 2)
            with dve.Fori(0, B - 1) as i:
                body(i, True)
            body(B - 1, False)

        @block.gpsimd
        def _(pool):
            pool.sem_inc(hl_ready, 2)
            with pool.Fori(0, B) as i:
                for u in range(2):
                    n = i * 2 + u
                    for m in range(M):
                        pool.wait_ge(hh_ready, n * M + m + 1)
                        pool.tensor_tensor(hs[1][:, u, m, :], h[:, m % 2], hs[0][:, u, m, :], ALU.subtract).then_inc(hl_ready, 1)


SE, SS, SH = 16, 16, 64
ES = SE * SS
EC = ES // P


def soft_slots_stage(nc, name, consts, xn, gamma, beta, mu, scale, slots, combT, comb_rinv):
    st = Stage(nc, name)
    with st.ctx:
        ident = st.sb("ident", [P, P])
        ones = st.sb("ones", [P, P])
        gm = st.sb("gamma", [P, 1, D])
        bt = st.sb("beta", [P, 1, D])
        sc = st.sb("scale", [P, 1])
        mur = st.sb("mu", [P, KC, ES])
        musq = st.sb("musq", [P, KC, ES])
        mun = st.sb("mun", [P, 1, ES])
        x = st.sb("x", [P, 2, QB, D])
        x2 = st.sb("x2", [P, QB, D])
        sq = st.sb("sq", [P, QB, D])
        stats = st.sb("stats", [P, QB, 6])
        mv = st.sb("mv", [P, QB, 2])
        vep = st.sb("vep", [P, QB])
        std = st.sb("std", [P, QB])
        rstd = st.sb("rstd", [P, QB])
        ssq = st.sb("ssq", [P, QB])
        norm = st.sb("norm", [P, QB])
        rnorm = st.sb("rnorm", [P, QB])
        x2T = st.sb("x2T", [P, KC, S])
        L = st.sb("L", [P, QB, ES])
        C = st.sb("C", [P, QB, ES])
        LT = st.sb("LT", [P, EC, S])
        DW = st.sb("DW", [P, QB, ES])
        CT = st.sb("CT", [P, EC, S])
        cmax = st.sb("cmax", [P, QB])
        csum = st.sb("csum", [P, QB])
        crin = st.sb("crin", [P, QB])
        dmax = st.sb("dmax", [P, EC])
        dsum = st.sb("dsum", [P, EC])
        drin = st.sb("drin", [P, EC])
        slot = st.sb("slot", [P, EC, D])
        W = [st.ps(f"W{k}") for k in range(4)]
        stats_seen = st.sem("stats_seen")
        c_in = st.sem("c_in")
        x_in = [st.sem(f"x_in{u}") for u in range(2)]
        x_used = st.sem("x_used")
        bank_ready = st.sem("bank_ready")
        bank_read = st.sem("bank_read")
        musq_ready = st.sem("musq_ready")
        mun_ready = st.sem("mun_ready")
        munit_ready = st.sem("munit_ready")
        var_ready = st.sem("var_ready")
        std_ready = st.sem("std_ready")
        x2_ready = st.sem("x2_ready")
        ssq_ready = st.sem("ssq_ready")
        norm_ready = st.sem("norm_ready")
        logits_ready = st.sem("logits_ready")
        comb_ready = st.sem("comb_ready")
        lt_ready = st.sem("lt_ready")
        disp_ready = st.sem("disp_ready")
        ct_ready = st.sem("ct_ready")
        slot_ready = st.sem("slot_ready")
        stored = st.sem("stored")
        dve_self = st.sem("dve_self")
        NB = 22
        block = st.ctx.enter_context(nc.Block())

        @block.sync
        def _(sp):
            for dst, src in ((ident[:], consts["ident"]), (ones[:], consts["ones"]), (gm[:, 0], gamma), (bt[:, 0], beta),
                             (sc[:], scale), (mur[:], mu.rearrange("(c p) n -> p c n", p=P))):
                sp.dma_start(dst, src).then_inc(c_in, 16)

            def load(i, u):
                for h in range(2):
                    sp.dma_start(x[:, u, h * TT:(h + 1) * TT, :], one(xn, (i * 2 + u) * 2 + h).rearrange("c p t d -> p (c t) d"))\
                      .then_inc(x_in[u], 16)

            def body(i, more):
                for u in range(2):
                    b = i * 2 + u
                    if more:
                        sp.wait_ge(x_used, b + 1)
                        load(i + 1, u)
                    sp.wait_ge(ct_ready, b + 1)
                    sp.dma_start(one(combT, b).rearrange("b p e t -> p (b e) t"), CT[:]).then_inc(stored, 16)
                    sp.dma_start(one(comb_rinv, b).rearrange("b p t -> (b p) t"), crin[:]).then_inc(stored, 16)
                    sp.wait_ge(slot_ready, (b + 1) * EC)
                    sp.dma_start(one(slots, b).rearrange("b (e p) d -> p (b e) d", p=P), slot[:]).then_inc(stored, 16)
            load(0, 0)
            load(0, 1)
            with sp.Fori(0, B // 2 - 1) as i:
                body(i, True)
            body(B // 2 - 1, False)
            sp.wait_ge(stored, 48 * B)

        @block.tensor
        def _(pe):
            pe.wait_ge(c_in, 96)
            pe.wait_ge(musq_ready, 1)
            for c in range(KC):
                last = pe.matmul(W[0][:, 0:ES], ones[:], musq[:, c, :], start=(c == 0), stop=(c == KC - 1))
            last.then_inc(bank_ready, 1)
            pe.wait_ge(munit_ready, 1)

            def batch(i, u):
                b = i * 2 + u
                k = [0]

                def bank():
                    k[0] += 1
                    pe.wait_ge(bank_read, b * NB + k[0] + 1)
                    return W[(u * NB + k[0]) % 4]

                def transposed(src, e):
                    for h in range(2):
                        w = bank()
                        for t in range(4):
                            last = pe.transpose(w[:, t * P:(t + 1) * P], src[:, h * 4 + t, e * P:(e + 1) * P], ident[:])
                        last.then_inc(bank_ready, 1)
                pe.wait_ge(x2_ready, b + 1)
                for c in range(KC):
                    transposed(x2, c)
                pe.wait_ge(bank_read, b * NB + 1 + 4 + 4)
                for t in range(0, QB, 2):
                    w = bank()
                    for h in range(2):
                        for c in range(KC):
                            last = pe.matmul(w[:, h * ES:(h + 1) * ES], x2T[:, c, (t + h) * P:(t + h + 1) * P], mur[:, c, :],
                                             start=(c == 0), stop=(c == KC - 1))
                    last.then_inc(bank_ready, 1)
                pe.wait_ge(bank_read, b * NB + 1 + 4 + 8)
                for e in range(EC):
                    transposed(L, e)
                pe.wait_ge(comb_ready, b + 1)
                for e in range(EC):
                    transposed(C, e)
                pe.wait_ge(disp_ready, b + 1)
                for t in range(0, QB, 2):
                    w = bank()
                    for h in range(2):
                        for e in range(EC):
                            last = pe.transpose(w[:, h * ES + e * P:h * ES + (e + 1) * P], LT[:, e, (t + h) * P:(t + h + 1) * P], ident[:])
                    last.then_inc(bank_ready, 1)
                pe.wait_ge(bank_read, b * NB + 1 + 4 + 20)
                for e in range(EC):
                    w = bank()
                    for t in range(QB):
                        last = pe.matmul(w[:, 0:D], DW[:, t, e * P:(e + 1) * P], x2[:, t, :], start=(t == 0), stop=(t == QB - 1))
                    last.then_inc(bank_ready, 1)
                assert k[0] == NB
            with pe.Fori(0, B // 2) as i:
                for u in range(2):
                    batch(i, u)

        @block.scalar
        def _(act):
            act.wait_ge(bank_ready, 1)
            act.activation(mun[:, 0], W[0][:, 0:ES], ACT.Sqrt).then_inc(mun_ready, 1)
            with act.Fori(0, B) as b:
                act.wait_ge(var_ready, b + 1)
                act.activation(std[:], vep[:], ACT.Sqrt).then_inc(std_ready, 1)
                act.wait_ge(x2_ready, b + 1)
                for t in range(QB):
                    last = act.activation(sq[:, t, :], x2[:, t, :], ACT.Square, accum_out=ssq[:, t:t + 1])
                last.then_inc(ssq_ready, 1)
                act.wait_ge(ssq_ready, b + 1)
                act.activation(norm[:], ssq[:], ACT.Sqrt).then_inc(norm_ready, 1)
                act.wait_ge(logits_ready, b + 1)
                for t in range(QB):
                    last = act.activation(C[:, t, :], L[:, t, :], ACT.Exp, bias=cmax[:, t:t + 1], accum_out=csum[:, t:t + 1])
                last.then_inc(comb_ready, 1)
                act.wait_ge(lt_ready, b + 1)
                for e in range(EC):
                    last = act.activation(LT[:, e, :], LT[:, e, :], ACT.Exp, bias=dmax[:, e:e + 1], accum_out=dsum[:, e:e + 1])
                last.then_inc(disp_ready, 1)

        @block.vector
        def _(dve):
            dve.wait_ge(c_in, 96)
            dve.tensor_tensor(musq[:], mur[:], mur[:], ALU.mult).then_inc(musq_ready, 1)
            dve.wait_ge(mun_ready, 1)
            link = Chain(dve, dve_self)
            link(dve.tensor_scalar(mun[:], mun[:], 1e-12, None, ALU.max))
            link(dve.reciprocal(mun[:], mun[:]))
            dve.tensor_tensor(mur[:], mur[:], mun[:].broadcast_to([P, KC, ES]), ALU.mult).then_inc(munit_ready, 1)
            dve.sem_inc(bank_read, 1 + 4)
            LINKS = 9

            def batch(i, u):
                b = i * 2 + u
                link = Chain(dve, dve_self, b * LINKS + 2)
                k = [0]

                def bank():
                    k[0] += 1
                    dve.wait_ge(bank_ready, b * NB + 1 + k[0])
                    return W[(u * NB + k[0]) % 4]
                dve.wait_ge(x_in[u], (i + 1) * 32)
                for t in range(QB):
                    last = dve.bn_stats(stats[:, t, :], x[:, u, t, :])
                link(last)
                dve.sem_inc(stats_seen, 1)
                for t in range(QB):
                    last = dve.bn_aggr(mv[:, t, :], stats[:, t, :])
                link(last)
                dve.tensor_scalar(vep[:], mv[:, :, 1], 1e-5, None, ALU.add).then_inc(var_ready, 1)
                dve.wait_ge(std_ready, b + 1)
                link(dve.reciprocal(rstd[:], std[:]))
                for t in range(QB):
                    last = dve.tensor_scalar(x2[:, t, :], x[:, u, t, :], mv[:, t, 0:1], rstd[:, t:t + 1], ALU.subtract, ALU.mult)
                last.then_inc(x_used, 1)
                dve.wait_ge(x_used, b + 1)
                link(dve.tensor_tensor(x2[:], x2[:], gm[:].broadcast_to([P, QB, D]), ALU.mult))
                dve.tensor_tensor(x2[:], x2[:], bt[:].broadcast_to([P, QB, D]), ALU.add).then_inc(x2_ready, 1)
                for c in range(KC):
                    for h in range(2):
                        dve.tensor_copy(x2T[:, c, h * CH:(h + 1) * CH], bank()[:]).then_inc(bank_read, 1)
                dve.wait_ge(norm_ready, b + 1)
                link(dve.tensor_scalar(norm[:], norm[:], 1e-12, None, ALU.max))
                link(dve.reciprocal(rnorm[:], norm[:]))
                link(dve.tensor_scalar(rnorm[:], rnorm[:], sc[:], None, ALU.mult))
                for t in range(0, QB, 2):
                    w = bank()
                    for h in range(2):
                        last = dve.tensor_scalar(L[:, t + h, :], w[:, h * ES:(h + 1) * ES], rnorm[:, t + h:t + h + 1], None, ALU.mult)
                    last.then_inc(bank_read, 1)
                dve.wait_ge(bank_read, b * NB + 1 + 4 + 8)
                dve.tensor_reduce(cmax[:], L[:], AX, ALU.max, negate=True).then_inc(logits_ready, 1)
                for e in range(EC):
                    for h in range(2):
                        dve.tensor_copy(LT[:, e, h * CH:(h + 1) * CH], bank()[:]).then_inc(bank_read, 1)
                dve.wait_ge(bank_read, b * NB + 1 + 4 + 12)
                dve.tensor_reduce(dmax[:], LT[:], AX, ALU.max, negate=True).then_inc(lt_ready, 1)
                dve.wait_ge(stored, b * 48)
                for e in range(EC):
                    for h in range(2):
                        dve.tensor_copy(CT[:, e, h * CH:(h + 1) * CH], bank()[:]).then_inc(bank_read, 1)
                link(dve.reciprocal(crin[:], csum[:]))
                dve.sem_inc(ct_ready, 1)
                for t in range(0, QB, 2):
                    dve.tensor_copy(DW[:, t:t + 2, :].rearrange("p t e -> p (t e)"), bank()[:]).then_inc(bank_read, 1)
                link(dve.reciprocal(drin[:], dsum[:]))
                for e in range(EC):
                    w = bank()
                    dve.tensor_scalar(slot[:, e, :], w[:, 0:D], drin[:, e:e + 1], None, ALU.mult).then_inc(slot_ready, 1)
                    dve.wait_ge(slot_ready, b * EC + e + 1)
                    dve.sem_inc(bank_read, 1)
                assert link.n == LINKS
            with dve.Fori(0, B // 2) as i:
                for u in range(2):
                    batch(i, u)


def soft_experts_stage(nc, name, consts, slots, w1, b1, w2, b2, slot_out):
    st = Stage(nc, name)
    with st.ctx:
        R = B * SS
        GR = 4
        ident = st.sb("ident", [P, P])
        sl = st.sb("sl", [R, SE, D])
        w1t = st.sb("w1", [P, KC, SE, SH])
        b1t = st.sb("b1", [SH, SE])
        w2t = st.sb("w2", [SH, SE, D])
        b2t = st.sb("b2", [R, SE, D])
        slT = st.sb("slT", [P, GR * KC, R])
        hT = st.sb("hT", [SH, GR, R])
        so = st.sb("so", [R, SE, D])
        TP = st.ps("TP")
        HP = st.ps("HP")
        OP = [st.ps(f"OP{k}") for k in range(2)]
        loaded = st.sem("loaded")
        slT_ps = st.sem("slT_ps")
        slT_ready = st.sem("slT_ready")
        h_ps = st.sem("h_ps")
        h_ready = st.sem("h_ready")
        o_ps = st.sem("o_ps")
        o_ready = st.sem("o_ready")
        stored = st.sem("stored")
        block = st.ctx.enter_context(nc.Block())

        @block.sync
        def _(sp):
            sp.dma_start(ident[:], consts["ident"]).then_inc(loaded, 16)
            for b in range(B):
                sp.dma_start(sl[b * SS:(b + 1) * SS], slots[b].rearrange("(e s) d -> s e d", s=SS)).then_inc(loaded, 16)
            for c in range(KC):
                sp.dma_start(w1t[:, c], w1[:, c * P:(c + 1) * P, :].rearrange("e p h -> p e h")).then_inc(loaded, 16)
            sp.dma_start(b1t[:], b1).then_inc(loaded, 16)
            sp.dma_start(w2t[:], w2.rearrange("e h d -> h e d")).then_inc(loaded, 16)
            sp.dma_start(b2t[:], b2).then_inc(loaded, 16)
            sp.wait_ge(o_ready, SE // 2)
            for b in range(B):
                sp.dma_start(slot_out[b].rearrange("(e s) d -> s e d", s=SS), so[b * SS:(b + 1) * SS]).then_inc(stored, 16)
            sp.wait_ge(stored, 16 * B)

        @block.tensor
        def _(pe):
            pe.wait_ge(loaded, 160)
            for g in range(SE // GR):
                if g:
                    pe.wait_ge(slT_ready, g)
                for e in range(GR):
                    for c in range(KC):
                        m = e * KC + c
                        last = pe.transpose(TP[:, m * R:(m + 1) * R], sl[:, g * GR + e, c * P:(c + 1) * P], ident[0:R, 0:R])
                last.then_inc(slT_ps, 1)
                pe.wait_ge(slT_ready, g + 1)
                if g:
                    pe.wait_ge(h_ready, g * GR)
                for e in range(GR):
                    for c in range(KC):
                        last = pe.matmul(HP[0:SH, e * R:(e + 1) * R], w1t[:, c, g * GR + e, :], slT[:, e * KC + c, :],
                                         start=(c == 0), stop=(c == KC - 1))
                last.then_inc(h_ps, 1)
                pe.wait_ge(h_ready, (g + 1) * GR)
                for k in range(GR // 2):
                    if g:
                        pe.wait_ge(o_ready, (g - 1) * 2 + k + 1)
                    for h in range(2):
                        e = k * 2 + h
                        last = pe.matmul(OP[k][0:R, h * D:(h + 1) * D], hT[:, e, :], w2t[:, g * GR + e, :], start=True, stop=True)
                    last.then_inc(o_ps, 1)

        @block.scalar
        def _(act):
            act.wait_ge(loaded, 160)
            for g in range(SE // GR):
                act.wait_ge(h_ps, g + 1)
                if g:
                    act.wait_ge(o_ps, g * 2)
                for e in range(GR):
                    act.activation(hT[:, e, :], HP[0:SH, e * R:(e + 1) * R], ACT.Gelu, bias=b1t[:, g * GR + e:g * GR + e + 1]).then_inc(h_ready, 1)

        @block.vector
        def _(dve):
            dve.wait_ge(loaded, 160)
            for g in range(SE // GR):
                dve.wait_ge(slT_ps, g + 1)
                if g:
                    dve.wait_ge(h_ps, g)
                dve.tensor_copy(slT[:].rearrange("p m r -> p (m r)"), TP[:]).then_inc(slT_ready, 1)
                for k in range(GR // 2):
                    dve.wait_ge(o_ps, g * 2 + k + 1)
                    e = g * GR + k * 2
                    dve.tensor_tensor(so[:, e:e + 2, :].rearrange("r e d -> r (e d)"), OP[k][0:R, :],
                                      b2t[:, e:e + 2, :].rearrange("r e d -> r (e d)"), ALU.add).then_inc(o_ready, 1)


def soft_combine_stage(nc, name, combT, comb_rinv, slot_out, g_out):
    st = Stage(nc, name)
    with st.ctx:
        CT = st.sb("CT", [P, 2, EC, S])
        so = st.sb("so", [P, 2, EC, D])
        crin = st.sb("crin", [P, 2, QB])
        go = st.sb("go", [P, 2, QB, D])
        W = [st.ps(f"W{k}") for k in range(4)]
        loaded = [st.sem(f"loaded{u}") for u in range(2)]
        w_ready = st.sem("w_ready")
        w_read = st.sem("w_read")
        stored = [st.sem(f"stored{u}") for u in range(2)]
        NBK = QB // 2
        block = st.ctx.enter_context(nc.Block())

        @block.sync
        def _(sp):
            def load(b, u):
                sp.dma_start(CT[:, u], combT[b]).then_inc(loaded[u], 16)
                sp.dma_start(so[:, u], slot_out[b].rearrange("(e p) d -> p e d", p=P)).then_inc(loaded[u], 16)
                sp.dma_start(crin[:, u], comb_rinv[b]).then_inc(loaded[u], 16)
            load(0, 0)
            load(1, 1)
            for b in range(B):
                u = b % 2
                sp.wait_ge(w_read, (b + 1) * NBK + 4)
                for h in range(2):
                    sp.dma_start(g_out[b * 2 + h], go[:, u, h * TT:(h + 1) * TT, :]).then_inc(stored[u], 16)
                if b + 2 < B:
                    load(b + 2, u)
            for u in range(2):
                sp.wait_ge(stored[u], 16 * B)

        @block.tensor
        def _(pe):
            with pe.Fori(0, B // 2) as i:
                for u in range(2):
                    b = i * 2 + u
                    pe.wait_ge(loaded[u], (i + 1) * 48)
                    for k in range(NBK):
                        pe.wait_ge(w_read, b * NBK + k + 1)
                        for h in range(2):
                            t = 2 * k + h
                            for e in range(EC):
                                last = pe.matmul(W[k][:, h * D:(h + 1) * D], CT[:, u, e, t * P:(t + 1) * P], so[:, u, e, :],
                                                 start=(e == 0), stop=(e == EC - 1))
                        last.then_inc(w_ready, 1)

        @block.scalar
        def _(act):
            act.sem_inc(w_read, 4)
            with act.Fori(0, B // 2) as i:
                for u in range(2):
                    b = i * 2 + u
                    act.wait_ge(stored[u], i * 32)
                    for k in range(NBK):
                        act.wait_ge(w_ready, b * NBK + k + 1)
                        for h in range(2):
                            t = 2 * k + h
                            last = act.activation(go[:, u, t, :], W[k][:, h * D:(h + 1) * D], ACT.Silu, scale=crin[:, u, t:t + 1])
                        last.then_inc(w_read, 1)


NE, FF = 8, 1024
CAP = TOK // NE
NT_ = TOK // P
SKIP = 4 * NE * CAP
GELU_C = float(np.float32(np.sqrt(2.0) / 1.41421))


def route_stage(nc, name, consts, xnT, xn, w_sw, b_sw, rows, g_index, g_keep):
    st = Stage(nc, name)
    with st.ctx:
        xT = st.sb("xT", [P, 2, KC, CH])
        xa = st.sb("xa", [P, NT_, D])
        wsw = st.sb("wsw", [P, KC, NE])
        bsw = st.sb("bsw", [P, 1, NE])
        iota = st.sb("iota", [P, 1, NE])
        tri = st.sb("tri", [P, P])
        ones = st.sb("ones", [P, P])
        zero = st.sb("zero", [P, NE * CAP * D // P])
        LG = st.sb("LG", [P, NT_, NE])
        mx = st.sb("mx", [P, NT_, 1])
        eq = st.sb("eq", [P, NT_, NE])
        cand = st.sb("cand", [P, NT_, NE])
        first = st.sb("first", [P, NT_, 1])
        oh = st.sb("oh", [P, NT_, NE])
        tot = st.sb("tot", [P, NT_, NE])
        sa = st.sb("sa", [P, NT_, NE])
        sb_ = st.sb("sb", [P, NT_, NE])
        pos = st.sb("pos", [P, NT_, NE])
        ptok = st.sb("ptok", [P, NT_])
        keep = st.sb("keep", [P, NT_])
        base = st.sb("base", [P, NT_])
        gidx = st.sb("gidx", [P, NT_])
        sidx = st.sb("sidx", [P, NT_])
        gu = st.sb("gu", [P, NT_], U32)
        su = st.sb("su", [P, NT_], U32)
        LP = [st.ps(f"L{k}", (P, TT, NE)) for k in range(2)]
        W0 = st.ps("W0", (P, NT_, NE))
        W1 = st.ps("W1", (P, NT_, NE))
        c_in = st.sem("c_in")
        xa_in = st.sem("xa_in")
        x_in = [st.sem(f"x_in{u}") for u in range(2)]
        zeroed = st.sem("zeroed")
        zero_set = st.sem("zero_set")
        l_ready = st.sem("l_ready")
        l_read = st.sem("l_read")
        oh_ready = st.sem("oh_ready")
        count_ready = st.sem("count_ready")
        index_ready = st.sem("index_ready")
        scattered = st.sem("scattered")
        stored = st.sem("stored")
        dve_self = st.sem("dve_self")
        block = st.ctx.enter_context(nc.Block())

        @block.sync
        def _(sp):
            for dst, src in ((wsw[:], w_sw.rearrange("(c p) e -> p c e", p=P)), (bsw[:, 0], b_sw), (iota[:, 0], consts["iota"]),
                             (tri[:], consts["tri"]), (ones[:], consts["ones"])):
                sp.dma_start(dst, src).then_inc(c_in, 16)
            with sp.Fori(0, B) as i:
                for u in range(2):
                    sp.wait_ge(l_read, i * 2 + u + 1)
                    sp.dma_start(xT[:, u], xnT[:, :, bass.ds((i * 2 + u) * CH, CH)]).then_inc(x_in[u], 16)
            sp.wait_ge(zero_set, 1)
            sp.dma_start(rows.rearrange("(p r) d -> p (r d)", p=P), zero[:]).then_inc(zeroed, 16)
            for c in range(2 * B):
                sp.dma_start(xa[:, c * TT:(c + 1) * TT, :], xn[c]).then_inc(xa_in, 16)
            sp.wait_ge(index_ready, 1)
            sp.dma_start(g_index, gu[:]).then_inc(stored, 16)
            sp.dma_start(g_keep, keep[:]).then_inc(stored, 16)
            sp.wait_ge(stored, 32)

        @block.tensor
        def _(pe):
            pe.wait_ge(c_in, 80)
            with pe.Fori(0, B) as i:
                for u in range(2):
                    n = i * 2 + u
                    pe.wait_ge(x_in[u], (i + 1) * 16)
                    pe.wait_ge(l_read, n + 1)
                    for t in range(TT):
                        for c in range(KC):
                            last = pe.matmul(LP[u][:, t, :], xT[:, u, c, t * P:(t + 1) * P], wsw[:, c, :], start=(c == 0), stop=(c == KC - 1))
                    last.then_inc(l_ready, 1)
            pe.wait_ge(oh_ready, 1)
            oh2 = oh[:].rearrange("p t e -> p (t e)")
            pe.matmul(W0[:].rearrange("p t e -> p (t e)"), tri[:], oh2, start=True, stop=True)
            pe.matmul(W1[:].rearrange("p t e -> p (t e)"), ones[:], oh2, start=True, stop=True).then_inc(count_ready, 1)

        @block.gpsimd
        def _(pool):
            pool.memset(zero[:], 0.0).then_inc(zero_set, 1)
            pool.wait_ge(zeroed, 16)
            pool.wait_ge(xa_in, 16 * 2 * B)
            pool.wait_ge(index_ready, 1)
            for t in range(NT_):
                pool.indirect_dma_start(out=rows, out_offset=bass.IndirectOffsetOnAxis(ap=su[:, t:t + 1], axis=0),
                                        in_=xa[:, t, :], in_offset=None, bounds_check=NE * CAP - 1, oob_is_err=False)\
                    .then_inc(scattered, 16)
            pool.wait_ge(scattered, 16 * NT_)

        @block.vector
        def _(dve):
            dve.sem_inc(l_read, 2)
            dve.wait_ge(c_in, 80)
            with dve.Fori(0, B) as i:
                for u in range(2):
                    n = i * 2 + u
                    dve.wait_ge(l_ready, n + 1)
                    dve.tensor_tensor(LG[:, bass.ds(n * TT, TT), :], LP[u][:], bsw[:].broadcast_to([P, TT, NE]), ALU.add).then_inc(l_read, 1)
            dve.wait_ge(l_read, 2 * B + 2)
            link = Chain(dve, dve_self)
            full = [P, NT_, NE]
            link(dve.tensor_reduce(mx[:], LG[:], AX, ALU.max))
            link(dve.tensor_tensor(eq[:], LG[:], mx[:].broadcast_to(full), ALU.is_ge))
            link(dve.scalar_tensor_tensor(out=cand[:], in0=eq[:], scalar=-float(NE), in1=iota[:].broadcast_to(full), op0=ALU.mult, op1=ALU.add))
            link(dve.tensor_reduce(first[:], cand[:], AX, ALU.min))
            dve.tensor_tensor(oh[:], cand[:], first[:].broadcast_to(full), ALU.is_equal).then_inc(oh_ready, 1)
            link(dve.tensor_scalar(base[:], first[:, :, 0], float(CAP), float(NE * CAP), ALU.mult, ALU.add))
            dve.wait_ge(count_ready, 1)
            link(dve.tensor_copy(tot[:], W1[:]))
            src, dst, step = tot, sa, 1
            while step < NT_:
                dve.tensor_copy(dst[:, 0:step, :], src[:, 0:step, :])
                link(dve.tensor_tensor(dst[:, step:, :], src[:, step:, :], src[:, 0:NT_ - step, :], ALU.add))
                src, dst, step = dst, (sb_ if dst is sa else sa), step * 2
            link(dve.tensor_tensor(pos[:], src[:], tot[:], ALU.subtract))
            link(dve.scalar_tensor_tensor(out=cand[:], in0=W0[:], scalar=-1.0, in1=pos[:], op0=ALU.add, op1=ALU.add))
            link(dve.tensor_tensor(pos[:], cand[:], oh[:], ALU.mult))
            link(dve.tensor_reduce(ptok[:], pos[:], AX, ALU.add))
            link(dve.tensor_scalar(keep[:], ptok[:], float(CAP), None, ALU.is_lt))
            link(dve.tensor_scalar(gidx[:], ptok[:], float(CAP - 1), None, ALU.min))
            link(dve.tensor_tensor(gidx[:], gidx[:], base[:], ALU.add))
            link(dve.tensor_scalar(sidx[:], keep[:], -float(SKIP), float(SKIP), ALU.mult, ALU.add))
            link(dve.tensor_tensor(sidx[:], sidx[:], gidx[:], ALU.add))
            dve.tensor_copy(gu[:], gidx[:])
            dve.tensor_copy(su[:], sidx[:]).then_inc(index_ready, 1)


def routed_experts_stage(nc, name, consts, rows, w1, b1, w2, b2, out_rows):
    st = Stage(nc, name)
    with st.ctx:
        M = FF // P
        ident = st.sb("ident", [P, P])
        x = st.sb("x", [P, 2, TT, D])
        xT = st.sb("xT", [P, 2, KC, CAP])
        w1t = st.sb("w1", [P, 2, KC, FF])
        w2t = st.sb("w2", [P, 2, M, D])
        b1t = st.sb("b1", [P, 2, M])
        b1c = st.sb("b1c", [P, 2, M])
        b2t = st.sb("b2", [P, 2, D])
        hT = st.sb("hT", [P, 2, M, CAP])
        o = st.sb("o", [P, 2, TT, D])
        T = [st.ps(f"T{k}") for k in range(2)]
        H = [st.ps(f"H{k}") for k in range(2)]
        O = [st.ps(f"O{k}", (P, 2, D)) for k in range(2)]
        ident_in = st.sem("ident_in")
        loaded = [st.sem(f"loaded{u}") for u in range(2)]
        in_free = st.sem("in_free")
        t_ready = st.sem("t_ready")
        xT_ready = st.sem("xT_ready")
        b1_ready = st.sem("b1_ready")
        h_ps = st.sem("h_ps")
        h_ready = st.sem("h_ready")
        o_ps = st.sem("o_ps")
        o_ready = st.sem("o_ready")
        stored = [st.sem(f"stored{u}") for u in range(2)]
        dve_self = st.sem("dve_self")
        block = st.ctx.enter_context(nc.Block())

        @block.sync
        def _(sp):
            sp.dma_start(ident[:], consts["ident"]).then_inc(ident_in, 16)

            def load(i, u):
                e = i * 2 + u
                for dst, src in ((x[:, u], rows.rearrange("(e t p) d -> e p t d", e=NE, p=P)),
                                 (w1t[:, u], w1.rearrange("e (c p) f -> e p c f", p=P)),
                                 (w2t[:, u], w2.rearrange("e (m p) d -> e p m d", p=P))):
                    sp.dma_start(dst, one(src, e).rearrange("e p a b -> p (e a) b")).then_inc(loaded[u], 16)
                for dst, src in ((b1t[:, u], b1), (b2t[:, u], b2)):
                    sp.dma_start(dst, one(src, e).rearrange("e p a -> (e p) a")).then_inc(loaded[u], 16)

            def body(i, more):
                for u in range(2):
                    e = i * 2 + u
                    sp.wait_ge(o_ready, (e + 1) * 2 + 2)
                    sp.dma_start(one(out_rows.rearrange("(e t p) d -> e p t d", e=NE, p=P), e).rearrange("e p a b -> p (e a) b"), o[:, u])\
                      .then_inc(stored[u], 16)
                    if more:
                        sp.wait_ge(in_free, e + 1)
                        load(i + 1, u)
            load(0, 0)
            load(0, 1)
            with sp.Fori(0, NE // 2 - 1) as i:
                body(i, True)
            body(NE // 2 - 1, False)
            for u in range(2):
                sp.wait_ge(stored[u], 16 * NE // 2)

        @block.tensor
        def _(pe):
            pe.wait_ge(ident_in, 16)
            with pe.Fori(0, NE // 2) as i:
                for u in range(2):
                    e = i * 2 + u
                    pe.wait_ge(loaded[u], (i + 1) * 80)
                    for c in range(KC):
                        pe.wait_ge(xT_ready, e * KC + c + 1)
                        for t in range(TT):
                            last = pe.transpose(T[c][:, t * P:(t + 1) * P], x[:, u, t, c * P:(c + 1) * P], ident[:])
                        last.then_inc(t_ready, 1)
                    pe.wait_ge(xT_ready, (e + 1) * KC + 2)
                    for m in range(M):
                        pe.wait_ge(h_ready, e * M + m + 1)
                        for c in range(KC):
                            last = pe.matmul(H[m % 2][:], w1t[:, u, c, m * P:(m + 1) * P], xT[:, u, c, :], start=(c == 0), stop=(c == KC - 1))
                        last.then_inc(h_ps, 1)
                for u in range(2):
                    e = i * 2 + u
                    pe.wait_ge(h_ready, (e + 1) * M + 2)
                    for k in range(2):
                        pe.wait_ge(o_ready, e * 2 + k + 1)
                        for h in range(2):
                            for m in range(M):
                                last = pe.matmul(O[k][:, h, :], hT[:, u, m, (2 * k + h) * P:(2 * k + h + 1) * P], w2t[:, u, m, :],
                                                 start=(m == 0), stop=(m == M - 1))
                        last.then_inc(o_ps, 1)

        @block.scalar
        def _(act):
            act.sem_inc(h_ready, 2)
            with act.Fori(0, NE // 2) as i:
                for u in range(2):
                    e = i * 2 + u
                    act.wait_ge(b1_ready, e + 1)
                    act.wait_ge(o_ps, i * 4)
                    for m in range(M):
                        act.wait_ge(h_ps, e * M + m + 1)
                        act.activation(hT[:, u, m, :], H[m % 2][:], ACT.Gelu, bias=b1c[:, u, m:m + 1], scale=GELU_C).then_inc(h_ready, 1)

        @block.vector
        def _(dve):
            dve.sem_inc(xT_ready, 2)
            dve.sem_inc(o_ready, 2)
            with dve.Fori(0, NE // 2) as i:
                for u in range(2):
                    e = i * 2 + u
                    dve.wait_ge(loaded[u], (i + 1) * 80)
                    for c in range(KC):
                        dve.wait_ge(t_ready, e * KC + c + 1)
                        dve.tensor_copy(xT[:, u, c, :], T[c][:]).then_inc(xT_ready, 1)
                    dve.tensor_scalar(b1c[:, u], b1t[:, u], GELU_C, None, ALU.mult).then_inc(b1_ready, 1)
                for u in range(2):
                    e = i * 2 + u
                    dve.wait_ge(stored[u], i * 16)
                    for k in range(2):
                        dve.wait_ge(o_ps, e * 2 + k + 1)
                        dve.scalar_tensor_tensor(out=o[:, u, 2 * k:2 * k + 2, :], in0=O[k][:], scalar=1.0 / GELU_C,
                                                 in1=b2t[:, u:u + 1, :].broadcast_to([P, 2, D]), op0=ALU.mult, op1=ALU.add).then_inc(o_ready, 1)
                    dve.wait_ge(o_ready, (e + 1) * 2 + 2)
                    dve.sem_inc(in_free, 1)


def gather_stage(nc, name, xn, out_rows, g_index, g_keep, g_out):
    st = Stage(nc, name)
    with st.ctx:
        gu = st.sb("gu", [P, NT_], U32)
        keep = st.sb("keep", [P, NT_])
        drop = st.sb("drop", [P, NT_])
        x = st.sb("x", [P, 2 * B, TT, D])
        y = st.sb("y", [P, 2 * B, TT, D])
        index_in = st.sem("index_in")
        x_in = st.sem("x_in")
        gathered = [st.sem(f"gathered{c}") for c in range(2 * B)]
        drop_ready = st.sem("drop_ready")
        kept = st.sem("kept")
        mixed = st.sem("mixed")
        out_ready = st.sem("out_ready")
        stored = st.sem("stored")
        block = st.ctx.enter_context(nc.Block())

        @block.sync
        def _(sp):
            sp.dma_start(gu[:], g_index).then_inc(index_in, 16)
            sp.dma_start(keep[:], g_keep).then_inc(index_in, 16)
            for c in range(2 * B):
                sp.dma_start(x[:, c], xn[c]).then_inc(x_in, 16)
            for c in range(2 * B):
                sp.wait_ge(out_ready, c + 1)
                sp.dma_start(g_out[c], y[:, c]).then_inc(stored, 16)
            sp.wait_ge(stored, 16 * 2 * B)

        @block.gpsimd
        def _(pool):
            pool.wait_ge(index_in, 32)
            for c in range(2 * B):
                for t in range(TT):
                    k = c * TT + t
                    pool.indirect_dma_start(out=y[:, c, t, :], out_offset=None, in_=out_rows,
                                            in_offset=bass.IndirectOffsetOnAxis(ap=gu[:, k:k + 1], axis=0)).then_inc(gathered[c], 16)

        @block.vector
        def _(dve):
            dve.wait_ge(index_in, 32)
            dve.tensor_scalar(drop[:], keep[:], -1.0, 1.0, ALU.mult, ALU.add).then_inc(drop_ready, 1)
            dve.wait_ge(drop_ready, 1)
            dve.wait_ge(x_in, 16 * 2 * B)
            for c in range(2 * B):
                dve.wait_ge(gathered[c], 16 * TT)
                for t in range(TT):
                    k = c * TT + t
                    last = dve.tensor_scalar(y[:, c, t, :], y[:, c, t, :], keep[:, k:k + 1], None, ALU.mult)
                last.then_inc(kept, 1)
                dve.wait_ge(kept, c + 1)
                for t in range(TT):
                    k = c * TT + t
                    last = dve.scalar_tensor_tensor(out=y[:, c, t, :], in0=x[:, c, t, :], scalar=drop[:, k:k + 1], in1=y[:, c, t, :],
                                                    op0=ALU.mult, op1=ALU.add)
                last.then_inc(mixed, 1)

        @block.scalar
        def _(act):
            for c in range(2 * B):
                act.wait_ge(mixed, c + 1)
                act.activation(y[:, c], y[:, c], ACT.Silu).then_inc(out_ready, 1)


def build_layers(nc, a, out):
    def scratch(name, shape, dt=F32):
        return nc.dram_tensor(name, shape, dt).ap()

    def tiles(ap):
        return ap.rearrange("(c t p) d -> c p t d", t=TT, p=P)

    def token_major(ap):
        return lambda i, u: [(0, TT, one(ap, i)[:, u * CH:(u + 1) * CH, :].rearrange("b (t p) (c n) -> p (b t) c n", p=P, n=P))]

    def head_major(ap):
        return lambda i, u: [(t, t + 1, one(ap, i)[:, :, u * CH + t * P:u * CH + (t + 1) * P, :].rearrange("b c p n -> p b c n"))
                             for t in range(TT)]

    x0 = a["x"].rearrange("b s d -> (b s) d")
    x1, x2, x3 = (scratch(f"x{k}", (TOK, D)) for k in (1, 2, 3))
    xn = scratch("xn", (TOK, D))
    xnT_rows = scratch("xnT", (D, TOK))
    xnT = xnT_rows.rearrange("(c p) t -> p c t", p=P)
    g = scratch("g", (TOK, D))

    q0, k0 = scratch("q0", (B, D, S)), scratch("k0", (B, D, S))
    v0, s0 = scratch("v0", (B, S, D)), scratch("s0", (B, S, D))
    update_stage(nc, "n0", a, tiles(x0), xnT=xnT)

    def qk0(i, u, j):
        dst = q0 if j < KC else k0
        return one(dst, i)[:, j % KC * P:(j % KC + 1) * P, u * CH:(u + 1) * CH].rearrange("b p t -> (b p) t")
    project_stage(nc, "p0", a, xnT, a["w0"], KC, KC, D, 1.0 / 16.0, qk0, token_major(v0))
    attention_stage(nc, "a0", a, q0.rearrange("b (h f) s -> b h f s", h=1), k0, v0, s0.rearrange("b (h s) d -> b h s d", h=1),
                    B, 1, KC, D, False)
    swiglu_stage(nc, "f0", xnT, a["wg0"], a["wu0"], a["wd0"], tiles(g))

    q_parts, k_parts = scratch("q_parts", (3, B * D, S), BF16), scratch("k_parts", (3, B * D, S), BF16)
    vn, on = scratch("vn", (B, S, D)), scratch("on", (B, S, D))
    m_rows = scratch("m_rows", (B * 4, HG, NR, S), BF16)

    def qk_parts(i, u, j):
        dst = q_parts if j < KC else k_parts
        return dst[:, bass.ds(i * D + j % KC * P, P), u * CH:(u + 1) * CH].rearrange("s p t -> p s t")
    update_stage(nc, "n1", a, tiles(x0), x_out=tiles(x1), xnT=xnT, xn=tiles(xn), s_in=tiles(s0.rearrange("b s d -> (b s) d")),
                 g_in=tiles(g))
    project_stage(nc, "p1", a, xnT, a["w1"], KC, KC, D, 0.25, qk_parts, token_major(vn),
                  rope=(a["perm16"], a["cos16"], a["sin16"]), parts=True)
    narrow_attention_stage(nc, "a1", a, q_parts, k_parts, vn, on, m_rows, B * 4)
    slots, slot_out = scratch("slots", (B, ES, D)), scratch("slot_out", (B, ES, D))
    combT, comb_rinv = scratch("combT", (B, P, EC, S)), scratch("comb_rinv", (B, P, QB))
    soft_slots_stage(nc, "e1", a, tiles(xn), a["gamma"], a["beta"], a["mu"], a["scale"], slots, combT, comb_rinv)
    soft_experts_stage(nc, "e2", a, slots, a["se_w1"], a["se_b1"], a["se_w2"], a["se_b2"], slot_out)
    soft_combine_stage(nc, "e3", combT, comb_rinv, slot_out, tiles(g))

    update_stage(nc, "n2", a, tiles(x1), x_out=tiles(x2), xnT=xnT, xn=tiles(xn), o_in=token_major(on), w_o=a["wo1"],
                 o_chunks=KC, g_in=tiles(g))
    project_stage(nc, "p2", a, xnT, a["w2"], KC, KC, D, 0.25, qk_parts, token_major(vn), parts=True)
    narrow_attention_stage(nc, "a2", a, q_parts, k_parts, vn, on, m_rows, B * 4)
    rows, out_rows = scratch("rows", (TOK, D)), scratch("out_rows", (TOK, D))
    g_index, g_keep = scratch("g_index", (P, TOK // P), U32), scratch("g_keep", (P, TOK // P))
    route_stage(nc, "r1", a, xnT, tiles(xn), a["w_sw"], a["b_sw"], rows, g_index, g_keep)
    routed_experts_stage(nc, "r2", a, rows, a["re_w1"], a["re_b1"], a["re_w2"], a["re_b2"], out_rows)
    gather_stage(nc, "r3", tiles(xn), out_rows, g_index, g_keep, tiles(g))

    NQ, NK = 8, 4
    q3, k3 = scratch("q3", (B * NQ, P, S)), scratch("k3", (B * NK, P, S))
    v3, o3 = scratch("v3", (B, NK, S, P)), scratch("o3", (B, NQ, S, P))
    update_stage(nc, "n3", a, tiles(x2), x_out=tiles(x3), xnT=xnT, o_in=token_major(on), w_o=a["wo2"], o_chunks=KC, g_in=tiles(g))

    def qk3(i, u, j):
        dst = one(q3, i * NQ + j) if j < NQ else one(k3, i * NK + (j - NQ))
        return dst[:, :, u * CH:(u + 1) * CH].rearrange("b p t -> (b p) t")
    project_stage(nc, "p3", a, xnT, a["w3"], NQ, NK, NK * P, float(np.float32(1.0 / np.sqrt(128.0))), qk3, head_major(v3),
                  rope=(a["perm128"], a["cos128"], a["sin128"]))
    attention_stage(nc, "a3", a, q3.rearrange("(u h) p s -> u h p s", h=NQ // NK), k3, v3.rearrange("b k s n -> (b k) s n"),
                    o3.rearrange("b (k h) s n -> (b k) h s n", h=NQ // NK), B * NK, NQ // NK, 1, P, True)
    swiglu_stage(nc, "f3", xnT, a["wg3"], a["wu3"], a["wd3"], tiles(g))
    update_stage(nc, "n4", a, tiles(x3), x_out=tiles(out.rearrange("b s d -> (b s) d")), o_in=head_major(o3), w_o=a["wo3"],
                 o_chunks=NQ, g_in=tiles(g))


def shape_constants():
    bf = mybir.dt.np(BF16)
    eye, ones = np.eye(P, dtype=np.float32), np.ones((P, P), np.float32)
    c = {"ident": eye, "identb": eye.astype(bf), "ones": ones, "tri": np.triu(ones),
         "mask": (np.triu(ones, 1) * NEG).astype(bf), "maskT": (np.tril(ones, -1) * NEG).astype(bf),
         "iota": np.tile(np.arange(8, dtype=np.float32), (P, 1))}
    for dh in (16, 128):
        half = dh // 2
        inv = (np.float32(1.0) / np.float32(10000.0) ** (np.arange(0, dh, 2, dtype=np.float32) / np.float32(dh))).astype(np.float32)
        angle = np.arange(S, dtype=np.float32)[:, None] * inv[None, :]
        feature = np.arange(P) % dh
        perm = np.zeros((P, P), np.float32)
        for p in range(P):
            if feature[p] < half:
                perm[p + half, p] = -1.0
            else:
                perm[p - half, p] = 1.0
        c[f"perm{dh}"] = perm
        c[f"cos{dh}"] = np.ascontiguousarray(np.cos(angle)[:, feature % half].T)
        c[f"sin{dh}"] = np.ascontiguousarray(np.sin(angle)[:, feature % half].T)
    return c


def kernel(**inputs):
    import concourse.bacc as bacc
    from concourse.bass_utils import run_bass_kernel_spmd

    t = {name: np.asarray(v) for name, v in inputs.items()}

    def repeated(v, shape):
        return np.broadcast_to(v, shape)
    arrays = {
        "x": t["L0_attn_x"],
        "w0": t["L0_attn_W_qkv"].T,
        "wg0": t["L0_ffn_w_gate"].T, "wu0": t["L0_ffn_w_up"].T, "wd0": t["L0_ffn_w_down"].T,
        "w1": t["L1_attn_w_qkv"], "wo1": t["L1_attn_w_out"],
        "gamma": repeated(t["L1_ffn_ln_gamma"], (P, D)), "beta": repeated(t["L1_ffn_ln_beta"], (P, D)),
        "mu": t["L1_ffn_mu"].reshape(D, ES), "scale": repeated(t["L1_ffn_scale"], (P, 1)),
        "se_w1": t["L1_ffn_w1"], "se_b1": t["L1_ffn_b1"].T,
        "se_w2": t["L1_ffn_w2"], "se_b2": repeated(t["L1_ffn_b2"], (SH, SE, D)),
        "w2": np.concatenate([t[f"L2_attn_W{c}"].reshape(D, D) for c in "qkv"], axis=1),
        "wo2": t["L2_attn_Wout"].reshape(D, D),
        "w_sw": t["L2_ffn_W_sw"], "b_sw": repeated(t["L2_ffn_b_sw"], (P, 8)),
        "re_w1": t["L2_ffn_W1"], "re_b1": t["L2_ffn_b1"].reshape(8, 8, P).transpose(0, 2, 1),
        "re_w2": t["L2_ffn_W2"], "re_b2": repeated(t["L2_ffn_b2"][:, None, :], (8, P, D)),
        "w3": np.concatenate([t[f"L3_attn_W{c}"] for c in "qkv"], axis=1), "wo3": t["L3_attn_Wo"],
        "wg3": t["L3_ffn_w_gate"].T, "wu3": t["L3_ffn_w_up"].T, "wd3": t["L3_ffn_w_down"].T,
    }
    arrays.update(shape_constants())
    arrays = {name: np.ascontiguousarray(v) for name, v in arrays.items()}
    nc = bacc.Bacc("TRN2", target_bir_lowering=False, num_devices=1)
    a = {name: nc.dram_tensor(f"in_{name}", v.shape, mybir.dt.from_np(v.dtype), kind="ExternalInput").ap()
         for name, v in arrays.items()}
    out = nc.dram_tensor("out_x", (B, S, D), F32, kind="ExternalOutput").ap()
    build_layers(nc, a, out)
    r = run_bass_kernel_spmd(nc, [{f"in_{name}": v for name, v in arrays.items()}], core_ids=[0])
    return r.results[0]["out_x"]
```
